# Optimizing a Trainium2 kernel written in Bass

```python
import numpy as np
import jax
import jax.numpy as jnp

def _softmax(x, axis=-1):
    return jax.nn.softmax(x, axis=axis)

def _gelu(x):
    return jax.nn.gelu(x, approximate=True)

def _silu(x):
    return jax.nn.silu(x)

def _sigmoid(x):
    return jax.nn.sigmoid(x)

def _layernorm(x, axis=-1, eps=1e-05):
    m = jnp.mean(x, axis=axis, keepdims=True)
    v = jnp.var(x, axis=axis, keepdims=True)
    return (x - m) / jnp.sqrt(v + eps)

def _scatter_add(tgt, idx, src, axis=0):
    return tgt.at[idx].add(src)

def _segment_sum(src, seg, n):
    return jax.ops.segment_sum(src, seg, n)
kernel_name = 'mk_cond_resid_d4_seqx_r4_e2dbf8'

def setup_inputs(seed: int=0):
    np.random.seed(seed)
    _w = jnp.asarray

    def _rec_inputs():
        import jax
        import jax.numpy as jnp
        _rk = jax.random.key(seed)
        x = -7.109e-05 + 0.9999 * jax.random.normal(jax.random.fold_in(_rk, 1), (64, 64, 512), jnp.float32)
        _lenS = 64 - jax.random.randint(jax.random.fold_in(_rk, 7), (64,), 0, max(1, 64 // 4) + 1, jnp.int32)
        _lenS2 = 64 - jax.random.randint(jax.random.fold_in(_rk, 8), (64,), 0, max(1, 64 // 4) + 1, jnp.int32)
        itok_B_1_198 = jax.random.randint(jax.random.fold_in(_rk, 11), (64,), 1, 199, jnp.int32)
        itok_Bx257_0_4111 = jax.random.randint(jax.random.fold_in(_rk, 12), (64, 257), 0, 1028, jnp.int32)
        itok_B_37_3939 = jax.random.randint(jax.random.fold_in(_rk, 13), (64,), 37, 985, jnp.int32)
        itok_B_0_15 = jax.random.randint(jax.random.fold_in(_rk, 14), (64,), 0, 16, jnp.int32)
        itok_B_0_6 = jax.random.randint(jax.random.fold_in(_rk, 15), (64,), 0, 7, jnp.int32)
        return (x, itok_B_1_198, itok_Bx257_0_4111, itok_B_37_3939, itok_B_0_15, itok_B_0_6)
    x, itok_B_1_198, itok_Bx257_0_4111, itok_B_37_3939, itok_B_0_15, itok_B_0_6 = _rec_inputs()

    def _L0_cond_setup():
        import jax, jax.numpy as jnp
        import numpy as np
        B, C, T = (128, 64, 512)
        S, D = (200, 64)
        key = jax.random.key(seed)
        k1, k2, k3 = jax.random.split(key, 3)
        x = jax.random.normal(k1, (B, C, T), dtype=jnp.float32)
        conditions = jax.random.randint(k2, (B,), 0, S, dtype=jnp.int64)
        weights = jax.random.normal(k3, (S, C, D), dtype=jnp.float32) / jnp.sqrt(jnp.float32(C))
        return {'x': x, 'conditions': conditions, 'weights': weights}
    _L0_cond_all = _L0_cond_setup()
    _L0_cond_in = {k: v for k, v in _L0_cond_all.items() if k in ('weights',)}
    del _L0_cond_all

    def _L1_cond_setup():
        import jax, jax.numpy as jnp
        import numpy as np
        H, G, HD = (8, 4, 64)
        GSZ = H // G
        BLOCK = 16
        WINDOW = 256
        SCALE = 256.0 ** (-0.5)
        EPS = 1e-06
        THETA = 10000.0
        B, T, D = (16, 4, 512)
        NBLK = 257

        def _rms(x, scale):
            var = jnp.mean(x * x, axis=-1, keepdims=True)
            return x * jax.lax.rsqrt(var + EPS) * (1.0 + scale)

        def _rope(x, pos):
            half = HD // 2
            inv = 1.0 / THETA ** (jnp.arange(half, dtype=jnp.float32) / half)
            ang = pos[:, :, None].astype(jnp.float32) * inv
            cos = jnp.cos(ang)[:, None, :, :]
            sin = jnp.sin(ang)[:, None, :, :]
            x1, x2 = (x[..., :half], x[..., half:])
            return jnp.concatenate([x1 * cos - x2 * sin, x2 * cos + x1 * sin], axis=-1)
        key = jax.random.key(seed)
        ks = jax.random.split(key, 10)
        inv_d = 1.0 / np.sqrt(D)
        return {'x': jax.random.normal(ks[0], (B, T, D), jnp.float32), 'Wq': jax.random.normal(ks[1], (H * HD, D), jnp.float32) * inv_d, 'Wk': jax.random.normal(ks[2], (G * HD, D), jnp.float32) * inv_d, 'Wv': jax.random.normal(ks[3], (G * HD, D), jnp.float32) * inv_d, 'Wo': jax.random.normal(ks[4], (D, H * HD), jnp.float32) * inv_d, 'q_norm_scale': jax.random.normal(ks[5], (HD,), jnp.float32) * 0.02, 'k_norm_scale': jax.random.normal(ks[6], (HD,), jnp.float32) * 0.02, 'k_blocks': jax.random.normal(ks[7], (B * NBLK, G, BLOCK, HD), jnp.float32), 'v_blocks': jax.random.normal(ks[8], (B * NBLK, G, BLOCK, HD), jnp.float32), 'block_tables': jnp.arange(B * NBLK, dtype=jnp.int32).reshape(B, NBLK), 'kv_lens': jax.random.randint(ks[9], (B,), 0, 1024, dtype=jnp.int32)}
    _L1_cond_all = _L1_cond_setup()
    _L1_cond_in = {k: v for k, v in _L1_cond_all.items() if k in ('Wq', 'Wk', 'Wv', 'Wo', 'q_norm_scale', 'k_norm_scale', 'k_blocks', 'v_blocks')}
    del _L1_cond_all

    def _L2_cond_setup():
        import jax, jax.numpy as jnp
        import numpy as np
        key = jax.random.key(seed)
        k1, k2, k3, k4 = jax.random.split(key, 4)
        B, S, IN, OUT, E = (64, 64, 512, 512, 16)
        bound = 1.0 / np.sqrt(IN)
        x = jax.random.normal(k1, (B, S, IN), dtype=jnp.float32)
        idx = jax.random.randint(k2, (B,), 0, E, dtype=jnp.int64)
        W = jax.random.uniform(k3, (E, IN, OUT), dtype=jnp.float32, minval=-bound, maxval=bound)
        b = jnp.full((E, OUT), 0.1, dtype=jnp.float32)
        return {'x': x, 'id': idx, 'W': W, 'b': b}
    _L2_cond_all = _L2_cond_setup()
    _L2_cond_in = {k: v for k, v in _L2_cond_all.items() if k in ('W', 'b')}
    del _L2_cond_all

    def _L3_cond_setup():
        import jax, jax.numpy as jnp
        import numpy as np
        B, T, D_IN, D_OUT = (16, 512, 512, 512)
        N_ADAPTERS, RANK = (8, 16)
        key = jax.random.key(seed)
        k_x, k_w, k_a, k_b, k_s, k_idx = jax.random.split(key, 6)
        x = jax.random.normal(k_x, (B, T, D_IN), dtype=jnp.float32)
        W = jax.random.normal(k_w, (D_OUT, D_IN), dtype=jnp.float32) * (1.0 / np.sqrt(D_IN))
        A = jax.random.normal(k_a, (N_ADAPTERS, RANK, D_IN), dtype=jnp.float32) * 0.02
        Bm = jax.random.normal(k_b, (N_ADAPTERS, D_OUT, RANK), dtype=jnp.float32) * 0.02
        scalings = jnp.ones((N_ADAPTERS,), dtype=jnp.float32)
        adapter_idx = jax.random.randint(k_idx, (B,), 0, N_ADAPTERS, dtype=jnp.int32)
        return {'x': x, 'W': W, 'A': A, 'Bm': Bm, 'scalings': scalings, 'adapter_idx': adapter_idx}
    _L3_cond_all = _L3_cond_setup()
    _L3_cond_in = {k: v for k, v in _L3_cond_all.items() if k in ('W', 'A', 'Bm', 'scalings')}
    del _L3_cond_all
    return {'x': x, 'itok_B_1_198': itok_B_1_198, 'itok_Bx257_0_4111': itok_Bx257_0_4111, 'itok_B_37_3939': itok_B_37_3939, 'itok_B_0_15': itok_B_0_15, 'itok_B_0_6': itok_B_0_6, 'L0_cond_weights': _L0_cond_in['weights'], 'L1_cond_Wq': _L1_cond_in['Wq'], 'L1_cond_Wk': _L1_cond_in['Wk'], 'L1_cond_Wv': _L1_cond_in['Wv'], 'L1_cond_Wo': _L1_cond_in['Wo'], 'L1_cond_q_norm_scale': _L1_cond_in['q_norm_scale'], 'L1_cond_k_norm_scale': _L1_cond_in['k_norm_scale'], 'L1_cond_k_blocks': _L1_cond_in['k_blocks'], 'L1_cond_v_blocks': _L1_cond_in['v_blocks'], 'L2_cond_W': _L2_cond_in['W'], 'L2_cond_b': _L2_cond_in['b'], 'L3_cond_W': _L3_cond_in['W'], 'L3_cond_A': _L3_cond_in['A'], 'L3_cond_Bm': _L3_cond_in['Bm'], 'L3_cond_scalings': _L3_cond_in['scalings']}

def reference(x, itok_B_1_198, itok_Bx257_0_4111, itok_B_37_3939, itok_B_0_15, itok_B_0_6, L0_cond_weights, L1_cond_Wq, L1_cond_Wk, L1_cond_Wv, L1_cond_Wo, L1_cond_q_norm_scale, L1_cond_k_norm_scale, L1_cond_k_blocks, L1_cond_v_blocks, L2_cond_W, L2_cond_b, L3_cond_W, L3_cond_A, L3_cond_Bm, L3_cond_scalings):
    import jax
    import jax.numpy as jnp

    def _L0_cond_ref(x, conditions, weights):
        import jax, jax.numpy as jnp
        import numpy as np
        B, C, T = (128, 64, 512)
        S, D = (200, 64)
        w = weights[conditions]
        return jnp.einsum('bct,bcd->bdt', x, w)

    def _L1_cond_ref(x, Wq, Wk, Wv, Wo, q_norm_scale, k_norm_scale, k_blocks, v_blocks, block_tables, kv_lens):
        import jax, jax.numpy as jnp
        import numpy as np
        H, G, HD = (8, 4, 64)
        GSZ = H // G
        BLOCK = 16
        WINDOW = 256
        SCALE = 256.0 ** (-0.5)
        EPS = 1e-06
        THETA = 10000.0
        B, T, D = (16, 4, 512)
        NBLK = 257

        def _rms(x, scale):
            var = jnp.mean(x * x, axis=-1, keepdims=True)
            return x * jax.lax.rsqrt(var + EPS) * (1.0 + scale)

        def _rope(x, pos):
            half = HD // 2
            inv = 1.0 / THETA ** (jnp.arange(half, dtype=jnp.float32) / half)
            ang = pos[:, :, None].astype(jnp.float32) * inv
            cos = jnp.cos(ang)[:, None, :, :]
            sin = jnp.sin(ang)[:, None, :, :]
            x1, x2 = (x[..., :half], x[..., half:])
            return jnp.concatenate([x1 * cos - x2 * sin, x2 * cos + x1 * sin], axis=-1)
        Bx, Tx, _ = x.shape
        q = jnp.einsum('btd,od->bto', x, Wq).reshape(Bx, Tx, H, HD).transpose(0, 2, 1, 3)
        k = jnp.einsum('btd,od->bto', x, Wk).reshape(Bx, Tx, G, HD).transpose(0, 2, 1, 3)
        v = jnp.einsum('btd,od->bto', x, Wv).reshape(Bx, Tx, G, HD).transpose(0, 2, 1, 3)
        q = _rms(q, q_norm_scale)
        k = _rms(k, k_norm_scale)
        pos = kv_lens[:, None] + jnp.arange(Tx, dtype=jnp.int32)
        q = _rope(q, pos)
        k = _rope(k, pos)
        slot = pos // BLOCK
        off = pos % BLOCK
        blk = jnp.take_along_axis(block_tables, slot, axis=1)
        k_blocks = k_blocks.at[blk, :, off, :].set(k.transpose(0, 2, 1, 3))
        v_blocks = v_blocks.at[blk, :, off, :].set(v.transpose(0, 2, 1, 3))
        k_all = k_blocks[block_tables].transpose(0, 2, 1, 3, 4).reshape(Bx, G, -1, HD)
        v_all = v_blocks[block_tables].transpose(0, 2, 1, 3, 4).reshape(Bx, G, -1, HD)
        S = k_all.shape[2]
        qg = q.reshape(Bx, G, GSZ, Tx, HD)
        scores = jnp.einsum('bghtd,bgsd->bghts', qg, k_all) * SCALE
        kpos = jnp.arange(S, dtype=jnp.int32)
        allowed = (kpos[None, None, :] <= pos[:, :, None]) & (kpos[None, None, :] > pos[:, :, None] - WINDOW)
        scores = jnp.where(allowed[:, None, None, :, :], scores, -jnp.inf)
        p = jax.nn.softmax(scores, axis=-1)
        o = jnp.einsum('bghts,bgsd->bghtd', p, v_all).reshape(Bx, H, Tx, HD)
        o = o.transpose(0, 2, 1, 3).reshape(Bx, Tx, H * HD)
        return jnp.einsum('bto,do->btd', o, Wo)

    def _L2_cond_ref(x, id, W, b):
        import jax, jax.numpy as jnp
        import numpy as np
        Wg = W[id]
        bg = b[id]
        out = jnp.einsum('bsi,bio->bso', x, Wg) + bg[:, None, :]
        return out

    def _L3_cond_ref(x, W, A, Bm, scalings, adapter_idx):
        import jax, jax.numpy as jnp
        import numpy as np
        B, T, D_IN, D_OUT = (16, 512, 512, 512)
        N_ADAPTERS, RANK = (8, 16)
        H = jnp.einsum('btd,od->bto', x, W)
        A_b = A[adapter_idx]
        B_b = Bm[adapter_idx]
        s_b = scalings[adapter_idx]
        xa = jnp.einsum('btd,brd->btr', x, A_b)
        delta = jnp.einsum('btr,bor->bto', xa, B_b)
        delta = jax.lax.stop_gradient(delta * s_b[:, None, None])
        return H + delta
    x = x + _L0_cond_ref(x, itok_B_1_198, L0_cond_weights)
    x = x + _L1_cond_ref(x, L1_cond_Wq, L1_cond_Wk, L1_cond_Wv, L1_cond_Wo, L1_cond_q_norm_scale, L1_cond_k_norm_scale, L1_cond_k_blocks, L1_cond_v_blocks, itok_Bx257_0_4111, itok_B_37_3939)
    x = x + _L2_cond_ref(x, itok_B_0_15, L2_cond_W, L2_cond_b)
    x = x + _L3_cond_ref(x, L3_cond_W, L3_cond_A, L3_cond_Bm, L3_cond_scalings, itok_B_0_6)
    return x

_drawn_inputs = setup_inputs


def setup_inputs(seed=0):
    import zlib

    import numpy as np

    out = dict(_drawn_inputs(seed))
    spreads = {'L2_cond_b': (0.10000000149011612, 0.6), 'L3_cond_scalings': (1.0, 0.6)}
    factors = {'L1_cond_Wk': 13.451,
     'L1_cond_q_norm_scale': 8.0,
     'L1_cond_k_norm_scale': 64.0,
     'L1_cond_k_blocks': 2.838,
     'L1_cond_Wv': 2.685}
    for name, (base, spread) in spreads.items():
        noise = np.random.default_rng([zlib.crc32(name.encode()), seed]).standard_normal(out[name].shape)
        drawn = base * np.exp(spread * noise) if base else spread * noise
        out[name] = jnp.asarray(drawn.astype(out[name].dtype))
    for name, factor in factors.items():
        out[name] = (out[name] * factor).astype(out[name].dtype)
    return out
```

```python
from contextlib import ExitStack

import concourse.bass as bass
from concourse import mybir

F32 = mybir.dt.float32
I32 = mybir.dt.int32
ALU = mybir.AluOpType
ACT = mybir.ActivationFunctionType
AXX = mybir.AxisListType.X

NB, T, D = 64, 64, 512
PAIRS = NB // 2
P = 128
KC = D // P
H, G, HD = 8, 4, 64
GP = G // 2
BLOCK, NBLK, NPOOL = 16, 257, 4112
WINDOW = 256
SCALE = 256.0 ** -0.5
EPS = 1e-6
SLOTS = 21
SPAN = SLOTS * BLOCK
CH = SPAN // 3
NCH = 3
WSLOTS = 5
NW = NB * WSLOTS
SLOT_MAX = NBLK - SLOTS
A_MAX = (NBLK * BLOCK - T) - BLOCK * SLOT_MAX
MASKW = SPAN + A_MAX
BIG = float(1 << 17)
NEG = -1e30
KVW = 2 * G * HD
E, NA, RANK, S0 = 16, 8, 16, 200
N_CONST = 16
PI = 3.141592653589793
C1, C2, C3 = 6.28125, 0.0019350051879882812, 3.019916e-07
MAGIC = 12582912.0


def at(tile, per_tile, i):
    return tile * per_tile + (i + 1)


def wait(eng, sem, value):
    if isinstance(value, int) and value <= 0:
        return
    eng.wait_ge(sem, value)


def wait_all(eng, passed, *pairs):
    for sem, value in pairs:
        wait(eng, sem, value)
    eng.sem_inc(passed, 1)


def build(nc, t, out):
    ctx = ExitStack()
    with ctx:
        def sb(name, shape, dt=F32):
            return ctx.enter_context(nc.sbuf_tensor(name, shape, dt))

        def sem(name):
            return ctx.enter_context(nc.semaphore(name))

        bank = [ctx.enter_context(nc.psum_tensor(f"bank{i}", [P, 512], F32)) for i in range(8)]

        x1_d = nc.dram_tensor("x1_scratch", [PAIRS, P, D], F32).ap()
        qt_d = nc.dram_tensor("qt_scratch", [PAIRS, P, D], F32).ap()
        kv_d = nc.dram_tensor("kv_scratch", [NB * T, KVW], F32).ap()
        tab_d = nc.dram_tensor("tab_scratch", [NB, SLOTS], F32).ap()
        tabw_d = nc.dram_tensor("tabw_scratch", [NB, WSLOTS], F32).ap()

        x_v = t["x"].rearrange("(n p) f -> n p f", p=P)
        kvd_v = kv_d.rearrange("(n p) f -> n p f", p=P)
        out_v = out.rearrange("(n p) f -> n p f", p=P)
        w2_v = t["w2"].rearrange("(e p) f -> e p f", p=P)

        ident = sb("ident", [P, P])
        mask = sb("mask", [P, MASKW])
        pm = sb("pm", [P, 1], I32)
        pmf = sb("pmf", [P, 1])
        idxT = sb("idxT", [CH, 2 * NCH, NB], I32)
        moff = sb("moff", [1, NB], I32)
        eid = sb("eid", [1, NB], I32)
        onehot = sb("onehot", [E, NB])
        adapt = sb("adapt", [P, NB])
        woT = sb("woT", [P, KC, D])
        w3T = sb("w3T", [P, KC, D])
        aT = sb("aT", [P, KC, P])
        bT = sb("bT", [P, D])
        b2 = sb("b2", [E, D])

        s_const = sem("const_ready")
        s_small = sem("small_in")
        s_pass_pool = sem("pool_passed")
        s_pass_dve = sem("dve_passed")
        s_prep = sem("prep_step")
        s_wqkv = sem("wqkv_in")
        s_wlate = sem("late_weights_in")
        s_tabout = sem("tables_out")
        s_tabin = sem("tables_back")
        s_cnt = sem("counts_ready")
        s_lw = sem("writers_ready")
        s_idxT = sem("indices_turned")
        s_idx = sem("indices_ready")
        s_w0i = sem("w0_index_ready")
        s_g = [sem(f"w0_in{i}") for i in range(4)]
        s_arg = sem("angles_ready")
        s_sin = sem("sines_ready")

        s_xin = sem("x_in")
        s_bd = sem("w0_block_ready")
        s_l0 = sem("l0_done")
        s_x1 = sem("x1_ready")
        s_xtp = sem("x1_turned")
        s_xt = sem("x1t_ready")
        s_qps = sem("q_done")
        s_kvps = sem("kv_done")
        s_qe = sem("q_copied")
        s_kve = sem("kv_copied")
        s_var = sem("variance_ready")
        s_sd = sem("deviation_ready")
        s_rope = sem("rope_step")
        s_qraw = sem("raw_qk_used")
        s_qr = sem("rotated_ready")
        s_qtp = sem("q_turned")
        s_qt = sem("qt_ready")
        s_x1o = sem("x1_out")
        s_qto = sem("qt_out")
        s_kvo = sem("kv_out")

        pa = ExitStack()
        with pa:
            def sa(name, shape, dt=F32):
                return pa.enter_context(nc.sbuf_tensor(name, shape, dt))

            wqkv = sa("wqkv", [P, KC, 1024])
            g0 = sa("g0", [P, PAIRS, T])
            g0i = sa("g0i", [P, PAIRS], I32)
            bd = sa("bd", [P, P])
            X = sa("X", [P, D])
            X1 = sa("X1", [P, D])
            XT = sa("XT", [P, KC, P])
            QK = sa("QK", [P, H + G, HD])
            SQ = sa("SQ", [P, H + G, HD])
            RT = sa("RT", [P, H + G, HD])
            KVR = sa("KVR", [P, KVW])
            QR = sa("QR", [P, H, HD])
            QT = sa("QT", [P, 2, KC, T])
            ss = sa("ss", [P, H + G])
            var = sa("var", [P, H + G])
            sd = sa("sd", [P, H + G])
            ri = sa("ri", [P, H + G])
            tab1 = sa("tab1", [P, 2, PAIRS, HD])
            tab2 = sa("tab2", [P, 2, PAIRS, HD])
            inv = sa("inv", [P, HD // 2])
            nsc = sa("nsc", [P, 2, HD])
            nscn = sa("nscn", [P, 2, HD])
            kvb = sa("kvb", [P, PAIRS], I32)
            cb = sa("cb", [P, PAIRS], I32)
            pos = sa("pos", [P, PAIRS])
            ang = sa("ang", [P, PAIRS, HD // 2])
            tr = sa("tr", [P, 2, PAIRS, HD // 2])
            trk = sa("trk", [P, 2, PAIRS, HD // 2])
            kvi = sa("kvi", [NB, 1], I32)
            kvf = sa("kvf", [NB, 1])
            ti = sa("ti", [NB, 1], I32)
            si = sa("si", [NB, 1], I32)
            slot0 = sa("slot0", [NB, 1])
            slotw = sa("slotw", [NB, 1])
            rw = sa("rw", [NB, 1])
            kri = sa("kri", [1, NB], I32)
            krf = sa("krf", [1, NB])
            kr2 = sa("kr2", [1, NB], I32)
            kr3 = sa("kr3", [1, NB])
            i257 = sa("i257", [NB, NW], I32)
            f257 = sa("f257", [NB, NW])
            i80i = sa("i80i", [NB, WSLOTS * BLOCK], I32)
            u80 = sa("u80", [NB, WSLOTS * BLOCK])
            v80 = sa("v80", [NB, WSLOTS * BLOCK])
            c80 = sa("c80", [NB, WSLOTS, BLOCK])
            uc = sa("uc", [NB, WSLOTS, BLOCK])
            bco = sa("bco", [NB, 1], I32)
            bcf = sa("bcf", [NB, 1])
            mxi = sa("mxi", [NB, WSLOTS], I32)
            mxf = sa("mxf", [NB, WSLOTS])
            sl21 = sa("sl21", [NB, SLOTS])
            sl5 = sa("sl5", [NB, WSLOTS])
            tabi = sa("tabi", [NB, NBLK], I32)
            tabf = sa("tabf", [NB, NBLK])
            junk = sa("junk", [NB, NBLK])
            tab21 = sa("tab21", [NB, SLOTS])
            tab5 = sa("tab5", [NB, WSLOTS])
            twb = sa("twb", [NB, NW])
            trb = sa("trb", [NB, NB, SLOTS])
            ew = sa("ew", [NB, NW])
            later = sa("later", [NB, WSLOTS, NW])
            mr = sa("mr", [NB, WSLOTS, NB * SLOTS])
            phys = sa("phys", [NB, SLOTS, BLOCK])
            has = sa("has", [NB, SPAN])
            oldi = sa("oldi", [NB, SPAN])
            newi = sa("newi", [NB, SPAN])
            idi = sa("idi", [E, NB], I32)
            idf = sa("idf", [E, NB])
            pe16i = sa("pe16i", [E, 1], I32)
            pe16 = sa("pe16", [E, 1])
            adi = sa("adi", [P, NB], I32)
            adf = sa("adf", [P, NB])
            pni = sa("pni", [P, 1], I32)
            pns = sa("pns", [P, 1], I32)
            pnf = sa("pnf", [P, 1])
            scal = sa("scal", [P, 1])

            N_SMALL = 13
            block = pa.enter_context(nc.Block())

            def bodies(eng, body):
                body(0)
                body(1)
                with eng.Fori(2, PAIRS - 2) as p:
                    body(p)
                body(PAIRS - 2)
                body(PAIRS - 1)
                body(PAIRS)

            def has_pair(q):
                return not isinstance(q, int) or 0 <= q < PAIRS

            PREP = {}

            @block.vector
            def _(dve):
                n = [0]

                def step(ins, name=None):
                    n[0] += 1
                    ins.then_inc(s_prep, 1)
                    if name:
                        PREP[name] = n[0]
                    dve.wait_ge(s_prep, n[0])

                v = nc.vector
                dve.wait_ge(s_small, 16 * N_SMALL)
                dve.wait_ge(s_const, N_CONST)
                step(v.tensor_copy(pmf[:, :], pm[:, :]))
                v.tensor_scalar(g0i[:, :], cb[:, :], float(T), pmf[:, 0:1], ALU.mult, ALU.add).then_inc(s_w0i, 1)
                step(v.tensor_scalar(pos[:, :], kvb[:, :], pmf[:, 0:1], None, ALU.add))
                step(v.tensor_tensor(ang[:, :, :], pos[:, :].unsqueeze(2).to_broadcast([P, PAIRS, HD // 2]),
                                     inv[:, :].unsqueeze(1).to_broadcast([P, PAIRS, HD // 2]), ALU.mult))
                for k, turn in ((0, 0.0), (1, 0.25)):
                    step(v.tensor_scalar(trk[:, k], ang[:, :, :], 1.0 / (2 * PI), turn, ALU.mult, ALU.add))
                    step(v.tensor_scalar(trk[:, k], trk[:, k], MAGIC, MAGIC, ALU.add, ALU.subtract))
                    step(v.scalar_tensor_tensor(tr[:, k], trk[:, k], -C1, ang[:, :, :], ALU.mult, ALU.add))
                    step(v.scalar_tensor_tensor(tr[:, k], trk[:, k], -C2, tr[:, k], ALU.mult, ALU.add))
                    step(v.scalar_tensor_tensor(tr[:, k], trk[:, k], -C3, tr[:, k], ALU.mult, ALU.add))
                    step(v.tensor_scalar(tr[:, k], tr[:, k], turn * 2 * PI, 3.1415925, ALU.add, ALU.min))
                    step(v.tensor_scalar(tr[:, k], tr[:, k], -3.1415925, None, ALU.max))
                v.tensor_scalar(nsc[:, :, :], nsc[:, :, :], 1.0, None, ALU.add).then_inc(s_arg, 1)
                dve.wait_ge(s_arg, 1)
                step(v.tensor_scalar(nscn[:, :, :], nsc[:, :, :], -1.0, None, ALU.mult))
                dve.wait_ge(s_sin, 1)
                hh = HD // 2
                for q in range(2):
                    def w(tile, a):
                        return tile[:, q, a:a + hh].unsqueeze(1).to_broadcast([P, PAIRS, hh])
                    step(v.tensor_tensor(tab1[:, q, :, 0:hh], trk[:, 1], w(nsc, 0), ALU.mult))
                    step(v.tensor_tensor(tab1[:, q, :, hh:HD], trk[:, 1], w(nsc, hh), ALU.mult))
                    step(v.tensor_tensor(tab2[:, q, :, 0:hh], trk[:, 0], w(nsc, 0), ALU.mult))
                    step(v.tensor_tensor(tab2[:, q, :, hh:HD], trk[:, 0], w(nscn, hh), ALU.mult))
                for i_, f_, j_, g_ in ((kvi, kvf, ti, slot0), (kri, krf, kr2, kr3)):
                    step(v.tensor_copy(f_[:, :], i_[:, :]))
                    step(v.tensor_scalar(j_[:, :], f_[:, :], float(1 - WINDOW), 0.0, ALU.add, ALU.max))
                    step(v.tensor_scalar(j_[:, :], j_[:, :], 4, None, ALU.arith_shift_right))
                    step(v.tensor_scalar(g_[:, :], j_[:, :], float(SLOT_MAX), None, ALU.min))
                step(v.tensor_scalar(si[:, :], kvi[:, :], 4, None, ALU.arith_shift_right))
                step(v.tensor_copy(slotw[:, :], si[:, :]))
                step(v.scalar_tensor_tensor(rw[:, :], slotw[:, :], -float(BLOCK), kvf[:, :], ALU.mult, ALU.add))
                step(v.scalar_tensor_tensor(krf[:, :], kr3[:, :], float(BLOCK), krf[:, :], ALU.mult, ALU.subtract))
                step(v.tensor_scalar(moff[:, :], krf[:, :], float(A_MAX), None, ALU.add))
                step(v.tensor_copy(f257[:, :], i257[:, :]))
                step(v.tensor_copy(tabf[:, :], tabi[:, :]))
                step(v.tensor_scalar(sl21[:, :], f257[:, 0:SLOTS], slot0[:, 0:1], None, ALU.add))
                step(v.tensor_scalar(sl5[:, :], f257[:, 0:WSLOTS], slotw[:, 0:1], None, ALU.add))
                for dst, sl, m in ((tab21, sl21, SLOTS), (tab5, sl5, WSLOTS)):
                    for i in range(m):
                        step(v.scalar_tensor_tensor(junk[:, :], f257[:, 0:NBLK], sl[:, i:i + 1], tabf[:, :],
                                                    ALU.is_equal, ALU.mult, accum_out=dst[:, i:i + 1]),
                             "tables")
                step(v.tensor_copy(u80[:, :], i80i[:, :]))
                step(v.tensor_scalar(u80[:, :], u80[:, :], rw[:, 0:1], None, ALU.subtract))
                step(v.tensor_scalar(v80[:, :], u80[:, :], 0.0, None, ALU.is_ge))
                step(v.scalar_tensor_tensor(v80[:, :], u80[:, :], float(T), v80[:, :], ALU.is_lt, ALU.mult))
                step(v.tensor_copy(bcf[:, :], bco[:, :]))
                step(v.tensor_copy(mxf[:, :], mxi[:, :]))
                step(v.scalar_tensor_tensor(c80[:, :, :].rearrange("p a b -> p (a b)"), u80[:, :], bcf[:, 0:1],
                                            v80[:, :], ALU.add, ALU.mult))
                dve.wait_ge(s_tabin, 32)
                for i in range(WSLOTS):
                    step(v.tensor_scalar(ew[:, :], twb[:, :], tab5[:, i:i + 1], None, ALU.is_equal))
                    step(v.scalar_tensor_tensor(later[:, i, :], f257[:, :], mxf[:, i:i + 1], ew[:, :],
                                                ALU.is_lt, ALU.mult), "later")
                for i in range(WSLOTS):
                    step(v.tensor_scalar(mr[:, i, :], trb[:, :, :].rearrange("p b s -> p (b s)"),
                                         tab5[:, i:i + 1], None, ALU.is_equal))
                dve.wait_ge(s_cnt, 1)
                step(v.scalar_tensor_tensor(uc[:, :, :].rearrange("p a b -> p (a b)"),
                                            bank[5][0:NB, 0:WSLOTS * BLOCK], 0.0,
                                            c80[:, :, :].rearrange("p a b -> p (a b)"),
                                            ALU.is_equal, ALU.mult), "uc")
                io = f257[:, 0:BLOCK].unsqueeze(1).to_broadcast([NB, SLOTS, BLOCK])
                step(v.scalar_tensor_tensor(phys[:, :, :], tab21[:, :].unsqueeze(2).to_broadcast([NB, SLOTS, BLOCK]),
                                            float(BLOCK), io, ALU.mult, ALU.add))
                dve.wait_ge(s_lw, 1)
                lw = bank[6][0:NB, 0:SPAN]
                step(v.tensor_scalar(has[:, :], lw, 0.0, BIG, ALU.is_gt, ALU.mult))
                step(v.tensor_tensor(oldi[:, :], has[:, :], phys[:, :, :].rearrange("p a b -> p (a b)"), ALU.add))
                step(v.tensor_scalar(has[:, :], lw, 0.0, BIG, ALU.is_equal, ALU.mult))
                step(v.scalar_tensor_tensor(newi[:, :], lw, -1.0, has[:, :], ALU.add, ALU.add), "idx")
                dve.wait_ge(s_idxT, 1)
                v.tensor_copy(idxT[:, :, :].rearrange("p a b -> p (a b)"),
                              bank[7][0:CH, 0:2 * NCH * NB]).then_inc(s_idx, 1)
                step(v.tensor_copy(pe16[:, :], pe16i[:, :]))
                step(v.tensor_copy(idf[:, :], idi[:, :]))
                step(v.tensor_scalar(onehot[:, :], idf[:, :], pe16[:, 0:1], None, ALU.is_equal))
                step(v.tensor_scalar(pns[:, :], pni[:, :], 4, None, ALU.arith_shift_right))
                step(v.tensor_copy(pnf[:, :], pns[:, :]))
                step(v.tensor_copy(adf[:, :], adi[:, :]))
                step(v.tensor_scalar(adapt[:, :], adf[:, :], pnf[:, 0:1], scal[:, 0:1], ALU.is_equal, ALU.mult))

                def first(q):
                    dve.wait_ge(s_xin, at(q, 16, 15))
                    dve.wait_ge(s_l0, at(q, 1, 0))
                    wait(dve, s_x1o, 16 * q)
                    wait(dve, s_xtp, q)
                    v.tensor_tensor(X1[:, :], bank[0][:, :], X[:, :], ALU.add).then_inc(s_x1, 1)

                def turned(q):
                    wait(dve, s_kvps, q)
                    dve.wait_ge(s_xtp, at(q, 1, 0))
                    v.tensor_copy(XT[:, :, :].rearrange("p a b -> p (a b)"), bank[1][:, :]).then_inc(s_xt, 1)

                def body(p):
                    if has_pair(p + 1):
                        turned(p + 1)
                    if has_pair(p - 1):
                        wait(dve, s_qto, 16 * (p - 1))
                        dve.wait_ge(s_qtp, at(p - 1, 1, 0))
                        v.tensor_copy(QT[:, :, :, :].rearrange("p b c t -> p c b t"),
                                      bank[4][:, :].rearrange("p (c b t) -> p c b t", c=KC, b=2)).then_inc(s_qt, 1)
                    if has_pair(p + 2):
                        first(p + 2)
                    if not has_pair(p):
                        return
                    R = 8
                    r = [0]

                    def rstep(ins):
                        ins.then_inc(s_rope, 1)
                        r[0] += 1
                        dve.wait_ge(s_rope, at(p, R, r[0] - 1))

                    dve.wait_ge(s_kve, at(p, 1, 0))
                    rstep(v.tensor_reduce(ss[:, :], SQ[:, :, :], AXX, ALU.add))
                    v.tensor_scalar(var[:, :], ss[:, :], 1.0 / HD, EPS, ALU.mult, ALU.add).then_inc(s_var, 1)
                    hh = HD // 2
                    pp = bass.ds(p, 1)
                    wait(dve, s_qtp, p)
                    wait(dve, s_kvo, 16 * p)
                    for q, (a, b) in enumerate(((0, H), (H, H + G))):
                        rstep(v.tensor_tensor(RT[:, a:b, :], QK[:, a:b, :],
                                              tab1[:, q, pp, :].to_broadcast([P, b - a, HD]), ALU.mult))
                    for q, (a, b) in enumerate(((0, H), (H, H + G))):
                        rstep(v.tensor_tensor(SQ[:, a:b, :], QK[:, a:b, :],
                                              tab2[:, q, pp, :].to_broadcast([P, b - a, HD]), ALU.mult))
                    rstep(v.tensor_tensor(RT[:, :, 0:hh], RT[:, :, 0:hh], SQ[:, :, hh:HD], ALU.add))
                    v.tensor_tensor(RT[:, :, hh:HD], RT[:, :, hh:HD], SQ[:, :, 0:hh], ALU.add).then_inc(s_qraw, 1)
                    dve.wait_ge(s_qraw, at(p, 1, 0))
                    dve.wait_ge(s_sd, at(p, 1, 0))
                    rstep(v.reciprocal(ri[:, :], sd[:, :]))
                    rstep(v.tensor_tensor(QR[:, :, :], RT[:, 0:H, :],
                                          ri[:, 0:H].unsqueeze(2).to_broadcast([P, H, HD]), ALU.mult))
                    v.tensor_tensor(KVR[:, 0:G * HD].rearrange("p (g d) -> p g d", g=G), RT[:, H:H + G, :],
                                    ri[:, H:H + G].unsqueeze(2).to_broadcast([P, G, HD]),
                                    ALU.mult).then_inc(s_qr, 1)
                    assert r[0] == R

                first(0)
                turned(0)
                first(1)
                bodies(dve, body)

            @block.sync
            def _(sp):
                for dst, src in (
                    (kvb[0:T, :], t["kv2"][0, :].partition_broadcast(T)),
                    (kvb[T:P, :], t["kv2"][1, :].partition_broadcast(T)),
                    (inv[:, :], t["inv"].partition_broadcast(P)),
                    (nsc[:, 0, :], t["qs"].partition_broadcast(P)),
                    (nsc[:, 1, :], t["ks"].partition_broadcast(P)),
                    (cb[0:T, :], t["cond2"][0, :].partition_broadcast(T)),
                    (cb[T:P, :], t["cond2"][1, :].partition_broadcast(T)),
                    (kvi[:, :], t["kv"].rearrange("(b o) -> b o", o=1)),
                    (kri[:, :], t["kv"].rearrange("(o b) -> o b", o=1)),
                    (tabi[:, :], t["tab"]),
                    (idi[:, :], t["id"].partition_broadcast(E)),
                    (adi[:, :], t["ad"].partition_broadcast(P)),
                    (scal[:, :], t["scal"]),
                ):
                    sp.dma_start(dst, src).then_inc(s_small, 16)
                sp.dma_start(wqkv[:, :, :], t["wqkv"].rearrange("(k p) n -> p k n", p=P)).then_inc(s_wqkv, 16)
                sp.dma_start(eid[:, :], t["id"].rearrange("(o b) -> o b", o=1)).then_inc(s_wlate, 16)
                sp.wait_ge(s_prep, PREP["tables"])
                sp.dma_start(tab_d, tab21[:, :]).then_inc(s_tabout, 16)
                sp.dma_start(tabw_d, tab5[:, :]).then_inc(s_tabout, 16)
                sp.wait_ge(s_tabout, 32)
                sp.dma_start(twb[:, :], tabw_d.rearrange("b s -> (b s)").partition_broadcast(NB)).then_inc(s_tabin, 16)
                sp.dma_start(trb[:, :, :].rearrange("p b s -> p (b s)"),
                             tab_d.rearrange("b s -> (b s)").partition_broadcast(NB)).then_inc(s_tabin, 16)
                for dst, src in (
                    (woT[:, :, :], t["woT"].rearrange("(k p) n -> p k n", p=P)),
                    (w3T[:, :, :], t["w3T"].rearrange("(k p) n -> p k n", p=P)),
                    (aT[:, :, :], t["aT"].rearrange("(k p) n -> p k n", p=P)),
                    (bT[:, :], t["bT"]),
                    (b2[:, :], t["b2"]),
                ):
                    sp.dma_start(dst, src).then_inc(s_wlate, 16)
                for q in range(2):
                    wait(sp, s_x1, q)
                    sp.dma_start(X[:, :], x_v[q]).then_inc(s_xin, 16)
                sp.wait_ge(s_x1, 1)
                sp.dma_start(x1_d[0], X1[:, :]).then_inc(s_x1o, 16)

                def body(p):
                    if has_pair(p + 1):
                        sp.wait_ge(s_x1, at(p + 1, 1, 0))
                        sp.dma_start(x1_d[bass.ds(p + 1, 1)], X1[:, :]).then_inc(s_x1o, 16)
                    if has_pair(p + 2):
                        sp.dma_start(X[:, :], x_v[bass.ds(p + 2, 1)]).then_inc(s_xin, 16)
                    if has_pair(p - 1):
                        sp.wait_ge(s_qr, at(p - 1, 1, 0))
                        sp.dma_start(kvd_v[bass.ds(p - 1, 1)], KVR[:, :]).then_inc(s_kvo, 16)
                        sp.wait_ge(s_qt, at(p - 1, 1, 0))
                        sp.dma_start(qt_d[bass.ds(p - 1, 1)],
                                     QT[:, :, :, :].rearrange("p b c t -> p (b c t)")).then_inc(s_qto, 16)

                bodies(sp, body)
                sp.wait_ge(s_x1o, 16 * PAIRS)
                sp.wait_ge(s_kvo, 16 * PAIRS)
                sp.wait_ge(s_qto, 16 * PAIRS)

            @block.gpsimd
            def _(pool):
                made = [0]

                def make(ins):
                    made[0] += 1
                    ins.then_inc(s_const, 1)
                    pool.wait_ge(s_const, made[0])

                for tile, step, base, up in ((pm[0:T, :], 0, 0, 1), (pm[T:P, :], 0, 0, 1), (i257[:, :], 1, 0, 0),
                                             (i80i[:, :], 1, 0, 0), (bco[:, :], 0, 1, T), (mxi[:, :], 1, 0, WSLOTS),
                                             (pe16i[:, :], 0, 0, 1), (pni[:, :], 0, 0, 1)):
                    make(nc.gpsimd.iota(tile, pattern=[[step, tile.shape[1]]], base=base, channel_multiplier=up))
                for tile in (bd, ident, mask):
                    make(nc.gpsimd.memset(tile[:, :], 0.0))
                make(nc.gpsimd.affine_select(out=ident[:, :], in_=ident[:, :], compare_op=ALU.not_equal, fill=1.0,
                                             base=0, pattern=[[-1, P]], channel_multiplier=1))
                for j in range(2):
                    m = mask[T * j:T * (j + 1), :]
                    make(nc.gpsimd.affine_select(out=m, in_=m, compare_op=ALU.is_ge, fill=NEG, base=A_MAX,
                                                 pattern=[[-1, MASKW]], channel_multiplier=1))
                    make(nc.gpsimd.affine_select(out=m, in_=m, compare_op=ALU.is_ge, fill=NEG,
                                                 base=WINDOW - 1 - A_MAX, pattern=[[1, MASKW]],
                                                 channel_multiplier=-1))
                assert made[0] == N_CONST
                pool.wait_ge(s_w0i, 1)
                for q in range(PAIRS):
                    pool.indirect_dma_start(out=g0[:, q, :], out_offset=None, in_=t["w0"],
                                            in_offset=bass.IndirectOffsetOnAxis(ap=g0i[:, q:q + 1], axis=0)
                                            ).then_inc(s_g[q % 4], 16)

                def block_of(q):
                    for half in range(2):
                        rows = slice(half * T, (half + 1) * T)
                        if half == 0:
                            wait_all(pool, s_pass_pool, (s_l0, q))
                        else:
                            wait_all(pool, s_pass_pool, (s_bd, at(q, 2, 0)))
                        nc.gpsimd.tensor_copy(bd[rows, rows], g0[rows, bass.ds(q, 1), :].rearrange("p o c -> p (o c)")
                                              ).then_inc(s_bd, 1)

                for i in range(4):
                    pool.wait_ge(s_g[i], 16 * (PAIRS // 4))
                block_of(0)
                with pool.Fori(1, PAIRS) as q:
                    block_of(q)

            @block.scalar
            def _(act):
                act.wait_ge(s_arg, 1)
                nc.scalar.activation(trk[:, :, :, :], tr[:, :, :, :], ACT.Sin).then_inc(s_sin, 1)

                def body(p):
                    if not has_pair(p):
                        return
                    act.wait_ge(s_qps, at(p, 1, 0))
                    wait(act, s_qraw, p)
                    bq = bank[2][:, :].rearrange("p (h d) -> p h d", h=H)
                    nc.scalar.activation(QK[:, 0:H, :], bq, ACT.Copy)
                    nc.scalar.activation(SQ[:, 0:H, :], bq, ACT.Square).then_inc(s_qe, 1)
                    act.wait_ge(s_kvps, at(p, 1, 0))
                    wait(act, s_kvo, 16 * p)
                    bk = bank[3][:, 0:G * HD].rearrange("p (g d) -> p g d", g=G)
                    nc.scalar.activation(QK[:, H:H + G, :], bk, ACT.Copy)
                    nc.scalar.activation(SQ[:, H:H + G, :], bk, ACT.Square)
                    nc.scalar.activation(KVR[:, G * HD:KVW], bank[3][:, G * HD:KVW], ACT.Copy).then_inc(s_kve, 1)
                    act.wait_ge(s_var, at(p, 1, 0))
                    nc.scalar.activation(sd[:, :], var[:, :], ACT.Sqrt).then_inc(s_sd, 1)

                bodies(act, body)

            @block.tensor
            def _(pe):
                mm = nc.tensor.matmul
                pe.wait_ge(s_prep, PREP["later"])
                pe.wait_ge(s_const, N_CONST)
                for i2 in range(WSLOTS):
                    for i in range(WSLOTS):
                        last = mm(bank[5][0:NB, i2 * BLOCK:(i2 + 1) * BLOCK],
                                  later[:, i, :].rearrange("p (b s) -> p b s", s=WSLOTS)[:, :, i2],
                                  v80[:, i * BLOCK:(i + 1) * BLOCK], start=(i == 0), stop=(i == WSLOTS - 1))
                last.then_inc(s_cnt, 1)
                pe.wait_ge(s_prep, PREP["uc"])
                for m in range(SLOTS):
                    for i in range(WSLOTS):
                        last = mm(bank[6][0:NB, m * BLOCK:(m + 1) * BLOCK],
                                  mr[:, i, :].rearrange("p (b s) -> p b s", s=SLOTS)[:, :, m],
                                  uc[:, i, :], start=(i == 0), stop=(i == WSLOTS - 1))
                last.then_inc(s_lw, 1)
                pe.wait_ge(s_prep, PREP["idx"])
                for k, tile in enumerate((oldi, newi)):
                    for c in range(NCH):
                        a = (k * NCH + c) * NB
                        last = nc.tensor.transpose(bank[7][0:CH, a:a + NB], tile[:, c * CH:(c + 1) * CH],
                                                   ident[0:NB, 0:NB])
                last.then_inc(s_idxT, 1)

                def l0(q):
                    pe.wait_ge(s_xin, at(q, 16, 15))
                    pe.wait_ge(s_bd, at(q, 2, 1))
                    wait(pe, s_x1, q)
                    mm(bank[0][:, :], bd[:, :], X[:, :], start=True, stop=True).then_inc(s_l0, 1)

                def xt(q):
                    pe.wait_ge(s_x1, at(q, 1, 0))
                    wait(pe, s_xt, q)
                    for k in range(KC):
                        last = nc.tensor.transpose(bank[1][:, k * P:(k + 1) * P], X1[:, k * P:(k + 1) * P],
                                                   ident[:, :])
                    last.then_inc(s_xtp, 1)

                def body(p):
                    if has_pair(p):
                        pe.wait_ge(s_xt, at(p, 1, 0))
                        wait(pe, s_qe, p)
                        for k in range(KC):
                            last = mm(bank[2][:, :], XT[:, k, :], wqkv[:, k, 0:512], start=(k == 0), stop=(k == KC - 1))
                        last.then_inc(s_qps, 1)
                        wait(pe, s_kve, p)
                        for k in range(KC):
                            last = mm(bank[3][:, :], XT[:, k, :], wqkv[:, k, 512:1024], start=(k == 0),
                                      stop=(k == KC - 1))
                        last.then_inc(s_kvps, 1)
                    if has_pair(p + 1):
                        xt(p + 1)
                    if has_pair(p - 1):
                        pe.wait_ge(s_qr, at(p - 1, 1, 0))
                        wait(pe, s_qt, p - 1)
                        for c in range(KC):
                            last = nc.tensor.transpose(bank[4][:, c * P:(c + 1) * P],
                                                       QR[:, 2 * c:2 * c + 2, :].rearrange("p a b -> p (a b)"),
                                                       ident[:, :])
                        last.then_inc(s_qtp, 1)
                    if has_pair(p + 2):
                        l0(p + 2)

                l0(0)
                xt(0)
                l0(1)
                pe.wait_ge(s_wqkv, 16)
                bodies(pe, body)

        pb = ExitStack()
        with pb:
            def sbt(name, shape, dt=F32):
                return pb.enter_context(nc.sbuf_tensor(name, shape, dt))

            KV = [sbt(f"KV{i}", [CH, NCH, KVW]) for i in range(2)]
            idxs = [sbt(f"idxs{i}", [CH, 2 * NCH], I32) for i in range(2)]
            FM = [sbt(f"FM{i}", [P, SPAN]) for i in range(2)]
            QB = [sbt(f"QB{i}", [P, KC, T]) for i in range(2)]
            KT = [sbt(f"KT{i}", [P, GP, SPAN]) for i in range(2)]
            SM = [sbt(f"SM{i}", [P, SPAN]) for i in range(2)]
            PR = [sbt(f"PR{i}", [P, SPAN]) for i in range(2)]
            PT = [sbt(f"PT{i}", [CH, NCH, P]) for i in range(2)]
            ON = [sbt(f"ON{i}", [P, G, HD]) for i in range(2)]
            OT = sbt("OT", [P, KC, 2, T])
            mx = sbt("mx", [P, 8])
            nb = sbt("nb", [P, 8])
            rs = sbt("rs", [P, 8])
            rinv = sbt("rinv", [P, 8])
            W2 = [sbt(f"W2{i}", [P, KC, D]) for i in range(2)]
            XB1 = sbt("XB1", [P, D])
            XB2 = sbt("XB2", [P, D])
            XB3 = sbt("XB3", [P, D])
            XO = sbt("XO", [P, D])
            XT2 = sbt("XT2", [P, KC, P])
            XT3 = sbt("XT3", [P, KC, P])
            OHS = sbt("OHS", [E, 2, T])
            XAM = sbt("XAM", [P, 2, T])

            s_reg = [sem(f"gather_args{i}") for i in range(2)]
            s_old = [sem(f"kv_old{i}") for i in range(2)]
            s_new = [sem(f"kv_new{i}") for i in range(2)]
            s_qin = [sem(f"qt_in{i}") for i in range(2)]
            s_x1in = sem("x1_in")
            s_w2in = [sem(f"w2_in{i}") for i in range(2)]
            s_ost = sem("out_stored")
            s_ktp = sem("keys_turned")
            s_kt = sem("kt_ready")
            s_s = sem("scores_done")
            s_mx = sem("max_ready")
            s_m = sem("masked_ready")
            s_e = sem("probs_ready")
            s_ptp = sem("probs_turned")
            s_pt = sem("pt_ready")
            s_pv = sem("pv_done")
            s_rinv = sem("sums_inverted")
            s_on = sem("heads_ready")
            s_otp = sem("heads_turned")
            s_ot = sem("ot_ready")
            s_o = sem("o_done")
            s_x2 = sem("x2_ready")
            s_x2p = sem("x2_turned")
            s_xt2 = sem("x2t_ready")
            s_oh = sem("onehot_ready")
            s_bias = sem("bias_done")
            s_l2 = sem("l2_done")
            s_x3 = sem("x3_ready")
            s_x3p = sem("x3_turned")
            s_xt3 = sem("x3t_ready")
            s_xa = sem("xa_done")
            s_xam = sem("xa_masked")
            s_l3 = sem("l3_done")
            s_xo = sem("out_ready")

            block = pb.enter_context(nc.Block())

            def bodies(eng, body):
                body(0, True, False)
                body(1, True, True)
                with eng.Fori(2, PAIRS - 1) as p:
                    body(p, True, True)
                body(PAIRS - 1, True, True)
                body(PAIRS, False, True)

            @block.gpsimd
            def _(pool):
                def body(p, attention, dense):
                    if not attention:
                        return
                    for b in range(2):
                        n = p * 2 + b
                        m0 = pool.value_load(moff[0:1, bass.ds(n, 1)], min_val=0, max_val=A_MAX)
                        wait_all(pool, s_pass_pool, (s_new[b], 16 * NCH * p))
                        nc.gpsimd.tensor_copy(idxs[b][:, :], idxT[:, :, bass.ds(n, 1)].rearrange("p a o -> p (a o)")
                                              ).then_inc(s_reg[b], 1)
                        wait_all(pool, s_pass_pool, (s_mx, 8 * (p - 1) + 4 * (b + 1)))
                        nc.gpsimd.tensor_copy(FM[b][:, :], mask[:, bass.ds(m0, SPAN)]).then_inc(s_reg[b], 1)
                        wait_all(pool, s_pass_pool, (s_pv, 8 * (p - 1) + 4 * (b + 1)), (s_reg[b], at(p, 2, 0)))
                        for c in range(NCH):
                            pool.indirect_dma_start(
                                out=KV[b][:, c, :], out_offset=None, in_=t["pool"],
                                in_offset=bass.IndirectOffsetOnAxis(ap=idxs[b][:, c:c + 1], axis=0),
                                bounds_check=NPOOL * BLOCK - 1, oob_is_err=False).then_inc(s_old[b], 16)
                        wait_all(pool, s_pass_pool, (s_old[b], at(p, 16 * NCH, 16 * NCH - 1)))
                        for c in range(NCH):
                            pool.indirect_dma_start(
                                out=KV[b][:, c, :], out_offset=None, in_=kv_d,
                                in_offset=bass.IndirectOffsetOnAxis(ap=idxs[b][:, NCH + c:NCH + c + 1], axis=0),
                                bounds_check=NB * T - 1, oob_is_err=False).then_inc(s_new[b], 16)

                bodies(pool, body)

            @block.sync
            def _(sp):
                sp.wait_ge(s_wlate, 16 * 6)

                def body(p, attention, dense):
                    q = p - 1
                    if dense:
                        wait(sp, s_x2, q)
                        sp.dma_start(XB1[:, :], x1_d[bass.ds(q, 1)]).then_inc(s_x1in, 16)
                    if attention:
                        wait(sp, s_s, 8 * (p - 1) + 4)
                        sp.dma_start(QB[0][:, :, :].rearrange("p c t -> p (c t)"),
                                     qt_d[bass.ds(p, 1), :, 0:256]).then_inc(s_qin[0], 16)
                    if dense:
                        for b in range(2):
                            e = sp.value_load(eid[0:1, bass.ds(q * 2 + b, 1)], min_val=0, max_val=E - 1)
                            wait(sp, s_l2, 2 * q - 1 + b)
                            sp.dma_start(W2[b][:, :, :].rearrange("p k n -> p (k n)"),
                                         w2_v[bass.ds(e, 1)]).then_inc(s_w2in[b], 16)
                    if attention:
                        wait(sp, s_s, 8 * (p - 1) + 8)
                        sp.dma_start(QB[1][:, :, :].rearrange("p c t -> p (c t)"),
                                     qt_d[bass.ds(p, 1), :, 256:512]).then_inc(s_qin[1], 16)
                    if dense:
                        sp.wait_ge(s_xo, at(q, 1, 0))
                        sp.dma_start(out_v[bass.ds(q, 1)], XO[:, :]).then_inc(s_ost, 16)

                bodies(sp, body)
                sp.wait_ge(s_ost, 16 * PAIRS)

            @block.scalar
            def _(act):
                def copy(dst, src):
                    return nc.scalar.activation(dst, src, ACT.Copy)

                def keys(q, b, gp):
                    act.wait_ge(s_ktp, at(q, 4, 2 * b + gp))
                    copy(KT[b][:, gp, :], bank[4][:, 0:SPAN]).then_inc(s_kt, 1)

                def exp(p, u):
                    act.wait_ge(s_m, at(p, 8, u))
                    wait(act, s_ptp, p * 8 + u - 1)
                    nc.scalar.activation(PR[u % 2][:, :], SM[u % 2][:, :], ACT.Exp, bias=nb[:, u:u + 1],
                                         scale=SCALE, accum_out=rs[:, u:u + 1]).then_inc(s_e, 1)

                def heads(p, b):
                    act.wait_ge(s_otp, at(p, 2, b))
                    copy(OT[:, :, b, :], bank[4][:, 0:256].rearrange("p (c t) -> p c t", c=KC)).then_inc(s_ot, 1)

                def body(p, attention, dense):
                    q = p - 1
                    if attention:
                        exp(p, 0)
                        keys(p, 1, 0)
                        exp(p, 1)
                    if dense:
                        act.wait_ge(s_x2p, at(q, 1, 0))
                        copy(XT2[:, :, :].rearrange("p k t -> p (k t)"), bank[4][:, :]).then_inc(s_xt2, 1)
                    if attention:
                        exp(p, 2)
                        exp(p, 3)
                        keys(p, 1, 1)
                        exp(p, 4)
                        exp(p, 5)
                    if dense:
                        act.wait_ge(s_x3p, at(q, 1, 0))
                        copy(XT3[:, :, :].rearrange("p k t -> p (k t)"), bank[4][:, :]).then_inc(s_xt3, 1)
                    if attention:
                        exp(p, 6)
                        heads(p, 0)
                        exp(p, 7)
                    if attention and not (isinstance(p, int) and p == PAIRS - 1):
                        keys(p + 1, 0, 0)
                        keys(p + 1, 0, 1)
                    if attention:
                        heads(p, 1)

                keys(0, 0, 0)
                keys(0, 0, 1)
                bodies(act, body)

            @block.vector
            def _(dve):
                v = nc.vector
                dve.wait_ge(s_const, N_CONST)

                def masked(p, u):
                    b = u // 4
                    wait_all(dve, s_pass_dve, (s_reg[b], at(p, 2, 1)), (s_e, p * 8 + u - 1),
                             (s_s, at(p, 8, u)))
                    v.tensor_tensor_reduce(out=SM[u % 2][:, :], in0=bank[u % 2][:, 0:SPAN], in1=FM[b][:, :],
                                           scale=1.0, scalar=-3e38, op0=ALU.add, op1=ALU.max,
                                           accum_out=mx[:, u:u + 1]).then_inc(s_mx, 1)
                    dve.wait_ge(s_mx, at(p, 8, u))
                    v.tensor_scalar(nb[:, u:u + 1], mx[:, u:u + 1], -SCALE, None, ALU.mult).then_inc(s_m, 1)

                def probs(p, u):
                    dve.wait_ge(s_ptp, at(p, 8, u))
                    wait(dve, s_pv, p * 8 + u - 1)
                    v.tensor_copy(PT[u % 2][:, :, :].rearrange("p c t -> p (c t)"),
                                  bank[2 + u % 2][0:CH, 0:NCH * P]).then_inc(s_pt, 1)

                def norm(p, b):
                    dve.wait_ge(s_e, at(p, 8, 4 * b + 3))
                    v.reciprocal(rinv[:, 4 * b:4 * b + 4], rs[:, 4 * b:4 * b + 4]).then_inc(s_rinv, 1)
                    dve.wait_ge(s_pv, at(p, 8, 4 * b + 3))
                    dve.wait_ge(s_rinv, at(p, 2, b))
                    v.tensor_tensor(ON[b][:, :, :], bank[5][:, 0:256].rearrange("p (g d) -> p g d", g=G),
                                    rinv[:, 4 * b:4 * b + 4].unsqueeze(2).to_broadcast([P, G, HD]),
                                    ALU.mult).then_inc(s_on, 1)

                def body(p, attention, dense):
                    q = p - 1
                    if dense:
                        wait_all(dve, s_pass_dve, (s_bias, q))
                        v.tensor_copy(OHS[:, :, :], onehot[:, bass.ds(q * 2, 2)].unsqueeze(2).to_broadcast([E, 2, T])
                                      ).then_inc(s_oh, 1)
                    for u in range(8):
                        if attention:
                            masked(p, u)
                            if u >= 1:
                                probs(p, u - 1)
                        if dense and u == 1:
                            dve.wait_ge(s_o, at(q, 1, 0))
                            dve.wait_ge(s_x1in, at(q, 16, 15))
                            v.tensor_tensor(XB2[:, :], bank[6][:, :], XB1[:, :], ALU.add).then_inc(s_x2, 1)
                        if dense and u == 4:
                            dve.wait_ge(s_l2, at(q, 2, 1))
                            dve.wait_ge(s_x2, at(q, 1, 0))
                            v.tensor_tensor(XB3[:, :], bank[7][:, :], XB2[:, :], ALU.add).then_inc(s_x3, 1)
                        if attention and u == 5:
                            norm(p, 0)
                        if dense and u == 6:
                            dve.wait_ge(s_xa, at(q, 1, 0))
                            v.tensor_tensor(XAM[:, :, :], bank[4][:, 0:P].rearrange("p (b t) -> p b t", b=2),
                                            adapt[:, bass.ds(q * 2, 2)].unsqueeze(2).to_broadcast([P, 2, T]),
                                            ALU.mult).then_inc(s_xam, 1)
                    if attention:
                        probs(p, 7)
                    if dense:
                        dve.wait_ge(s_l3, at(q, 1, 0))
                        dve.wait_ge(s_x3, at(q, 1, 0))
                        wait(dve, s_ost, 16 * q)
                        v.tensor_tensor(XO[:, :], bank[6][:, :], XB3[:, :], ALU.add).then_inc(s_xo, 1)
                    if attention:
                        norm(p, 1)

                bodies(dve, body)

            @block.tensor
            def _(pe):
                mm = nc.tensor.matmul

                def keys(q, b, gp):
                    if gp == 0:
                        pe.wait_ge(s_new[b], at(q, 16 * NCH, 16 * NCH - 1))
                    for c in range(NCH):
                        last = nc.tensor.transpose(bank[4][:, c * CH:(c + 1) * CH],
                                                   KV[b][:, c, gp * P:(gp + 1) * P], ident[0:CH, 0:CH])
                    last.then_inc(s_ktp, 1)

                def scores(p, u):
                    b, g = u // 4, u % 4
                    gp, g2 = g // 2, g % 2
                    rows = slice(g2 * HD, (g2 + 1) * HD)
                    if g == 0:
                        pe.wait_ge(s_qin[b], at(p, 16, 15))
                    if g2 == 0:
                        pe.wait_ge(s_kt, at(p, 4, 2 * b + gp))
                    wait(pe, s_mx, p * 8 + u - 1)
                    mm(bank[u % 2][:, 0:SPAN], QB[b][rows, 2 * gp:2 * gp + 2, :].rearrange("p c t -> p (c t)"),
                       KT[b][rows, gp, :], start=True, stop=True).then_inc(s_s, 1)

                def turn(p, u):
                    pe.wait_ge(s_e, at(p, 8, u))
                    wait(pe, s_pt, p * 8 + u - 1)
                    for c in range(NCH):
                        last = nc.tensor.transpose(bank[2 + u % 2][0:CH, c * P:(c + 1) * P],
                                                   PR[u % 2][:, c * CH:(c + 1) * CH], ident[:, :])
                    last.then_inc(s_ptp, 1)

                def values(p, u):
                    b, g = u // 4, u % 4
                    pe.wait_ge(s_pt, at(p, 8, u))
                    if g == 0:
                        wait(pe, s_on, 2 * p + b)
                    for c in range(NCH):
                        last = mm(bank[5][:, g * HD:(g + 1) * HD], PT[u % 2][:, c, :],
                                  KV[b][:, c, (G + g) * HD:(G + g + 1) * HD], start=(c == 0), stop=(c == NCH - 1))
                    last.then_inc(s_pv, 1)

                def heads(p, b):
                    pe.wait_ge(s_on, at(p, 2, b))
                    for gp in range(GP):
                        last = nc.tensor.transpose(bank[4][:, gp * P:(gp + 1) * P],
                                                   ON[b][:, 2 * gp:2 * gp + 2, :].rearrange("p g d -> p (g d)"),
                                                   ident[:, :])
                    last.then_inc(s_otp, 1)

                def body(p, attention, dense):
                    q = p - 1
                    more = attention and not (isinstance(p, int) and p == PAIRS - 1)

                    def slot(u):
                        if attention:
                            scores(p, u)

                    def after(u):
                        if attention and u >= 1:
                            turn(p, u - 1)
                        if attention and u >= 2:
                            values(p, u - 2)

                    slot(0)
                    if dense:
                        pe.wait_ge(s_ot, at(q, 2, 1))
                        wait(pe, s_xo, q)
                        for c in range(KC):
                            last = mm(bank[6][:, :], OT[:, c, :, :].rearrange("p b t -> p (b t)"), woT[:, c, :],
                                      start=(c == 0), stop=(c == KC - 1))
                        last.then_inc(s_o, 1)
                    after(0)
                    slot(1)
                    if attention:
                        wait(pe, s_ot, 2 * p)
                        if not dense:
                            pe.wait_ge(s_kt, at(p, 4, 1))
                        keys(p, 1, 0)
                    if dense:
                        pe.wait_ge(s_oh, at(q, 1, 0))
                        wait(pe, s_x3, q)
                        mm(bank[7][:, :], OHS[:, :, :].rearrange("p b t -> p (b t)"), b2[:, :], start=True,
                           stop=False, skip_group_check=True).then_inc(s_bias, 1)
                    after(1)
                    slot(2)
                    if dense:
                        if attention:
                            pe.wait_ge(s_kt, at(p, 4, 2))
                        pe.wait_ge(s_x2, at(q, 1, 0))
                        for k in range(KC):
                            last = nc.tensor.transpose(bank[4][:, k * P:(k + 1) * P], XB2[:, k * P:(k + 1) * P],
                                                       ident[:, :])
                        last.then_inc(s_x2p, 1)
                    after(2)
                    slot(3)

                    def expert(b):
                        pe.wait_ge(s_w2in[b], at(q, 16, 15))
                        for k in range(KC):
                            last = mm(bank[7][b * T:(b + 1) * T, :], XT2[:, k, b * T:(b + 1) * T], W2[b][:, k, :],
                                      start=False, stop=(k == KC - 1), skip_group_check=True)
                        last.then_inc(s_l2, 1)

                    if dense:
                        pe.wait_ge(s_xt2, at(q, 1, 0))
                        expert(0)
                    if attention:
                        wait(pe, s_xt2, p)
                        if not dense:
                            pe.wait_ge(s_kt, at(p, 4, 2))
                        keys(p, 1, 1)
                    after(3)
                    slot(4)
                    if dense:
                        expert(1)
                    after(4)
                    slot(5)
                    if dense:
                        pe.wait_ge(s_x3, at(q, 1, 0))
                        if attention:
                            pe.wait_ge(s_kt, at(p, 4, 3))
                        for k in range(KC):
                            last = nc.tensor.transpose(bank[4][:, k * P:(k + 1) * P], XB3[:, k * P:(k + 1) * P],
                                                       ident[:, :])
                        last.then_inc(s_x3p, 1)
                    after(5)
                    slot(6)
                    if dense:
                        pe.wait_ge(s_xt3, at(q, 1, 0))
                        for k in range(KC):
                            last = mm(bank[4][:, 0:P], aT[:, k, :], XT3[:, k, :], start=(k == 0), stop=(k == KC - 1))
                        last.then_inc(s_xa, 1)
                        pe.wait_ge(s_x2, at(q, 1, 0))
                        for k in range(KC):
                            mm(bank[6][:, :], XT3[:, k, :], w3T[:, k, :], start=(k == 0), stop=False)
                    after(6)
                    slot(7)
                    if dense:
                        pe.wait_ge(s_xam, at(q, 1, 0))
                        mm(bank[6][:, :], XAM[:, :, :].rearrange("p b t -> p (b t)"), bT[:, :], start=False,
                           stop=True).then_inc(s_l3, 1)
                    if attention:
                        if not dense:
                            pe.wait_ge(s_kt, at(p, 4, 3))
                        heads(p, 0)
                    after(7)
                    if attention:
                        turn(p, 7)
                        values(p, 6)
                    if more:
                        pe.wait_ge(s_ot, at(p, 2, 0))
                        keys(p + 1, 0, 0)
                    if attention:
                        values(p, 7)
                    if more:
                        pe.wait_ge(s_kt, at(p + 1, 4, 0))
                        keys(p + 1, 0, 1)
                    if attention:
                        if more:
                            pe.wait_ge(s_kt, at(p + 1, 4, 1))
                        else:
                            pe.wait_ge(s_ot, at(p, 2, 0))
                        heads(p, 1)

                keys(0, 0, 0)
                pe.wait_ge(s_kt, 1)
                keys(0, 0, 1)
                bodies(pe, body)


def kernel(**inputs):
    import numpy as np
    import concourse.bacc as bacc
    from concourse.bass_utils import run_bass_kernel_spmd

    a = {k: np.asarray(v) for k, v in inputs.items()}
    cond, tab, kv = a["itok_B_1_198"], a["itok_Bx257_0_4111"], a["itok_B_37_3939"]
    ident, adapter = a["itok_B_0_15"], a["itok_B_0_6"]
    order = [4 * gp + 2 * g2 + j for gp in range(GP) for j in range(2) for g2 in range(2)]
    wq = a["L1_cond_Wq"].reshape(H, HD, D)[order].reshape(H * HD, D)
    wo = a["L1_cond_Wo"].reshape(D, H, HD)[:, order].reshape(D, H * HD)

    def rows(pool):
        return pool.transpose(0, 2, 1, 3).reshape(NPOOL * BLOCK, G * HD)

    half = HD // 2
    arrays = {
        "x": a["x"].reshape(NB * T, D),
        "w0": a["L0_cond_weights"].reshape(S0 * T, T),
        "cond2": cond.reshape(PAIRS, 2).T,
        "kv2": kv.reshape(PAIRS, 2).T,
        "kv": kv,
        "tab": tab,
        "id": ident,
        "ad": adapter,
        "scal": np.repeat(a["L3_cond_scalings"], RANK).reshape(P, 1),
        "inv": (np.float32(1.0) / np.float32(10000.0) ** (np.arange(half, dtype=np.float32) / np.float32(half))),
        "qs": a["L1_cond_q_norm_scale"],
        "ks": a["L1_cond_k_norm_scale"],
        "wqkv": np.concatenate([wq, a["L1_cond_Wk"], a["L1_cond_Wv"]]).T,
        "woT": wo.T,
        "pool": np.concatenate([rows(a["L1_cond_k_blocks"]), rows(a["L1_cond_v_blocks"])], axis=1),
        "w2": a["L2_cond_W"].reshape(E, KC, P, D).transpose(0, 2, 1, 3).reshape(E * P, KC * D),
        "b2": a["L2_cond_b"],
        "w3T": a["L3_cond_W"].T,
        "aT": a["L3_cond_A"].reshape(NA * RANK, D).T,
        "bT": a["L3_cond_Bm"].transpose(0, 2, 1).reshape(NA * RANK, D),
    }
    arrays = {k: np.ascontiguousarray(v) for k, v in arrays.items()}
    nc = bacc.Bacc("TRN2", target_bir_lowering=False, num_devices=1)
    t = {k: nc.dram_tensor(f"in_{k}", v.shape, mybir.dt.from_np(v.dtype), kind="ExternalInput").ap()
         for k, v in arrays.items()}
    out = nc.dram_tensor("out_dram", (NB * T, D), F32, kind="ExternalOutput").ap()
    build(nc, t, out)
    r = run_bass_kernel_spmd(nc, [{f"in_{k}": v for k, v in arrays.items()}], core_ids=[0])
    return r.results[0]["out_dram"].reshape(NB, T, D)
```

```python
from contextlib import ExitStack

import concourse.bass as bass
from concourse import mybir

F32 = mybir.dt.float32
I32 = mybir.dt.int32
F32R = mybir.dt.float32r
ALU = mybir.AluOpType
ACT = mybir.ActivationFunctionType
AXX = mybir.AxisListType.X

NB, T, D = 64, 64, 512
PAIRS = NB // 2
P = 128
KC = D // P
H, G, HD = 8, 4, 64
GP = G // 2
BLOCK, NBLK, NPOOL = 16, 257, 4112
WINDOW = 256
SCALE = 256.0 ** -0.5
EPS = 1e-6
SLOTS = 21
SPAN = SLOTS * BLOCK
CH = SPAN // 3
NCH = 3
WSLOTS = 5
NW = NB * WSLOTS
SLOT_MAX = NBLK - SLOTS
A_MAX = (NBLK * BLOCK - T) - BLOCK * SLOT_MAX
MASKW = SPAN + A_MAX
BIG = float(1 << 17)
NEG = -1e30
KVW = 2 * G * HD
E, NA, RANK, S0 = 16, 8, 16, 200
N_CONST = 18
PI = 3.141592653589793
C1, C2 = 6.28125, 0.0019353071795864769
MAGIC = 12582912.0


class Pair:

    def __init__(self, i, par):
        self.i, self.par, self.n = i, par, i * 2 + par

    def move(self, by):
        return Pair(self.i + (self.par + by) // 2, (self.par + by) % 2)


def at(tile, per_tile, i):
    return tile * per_tile + (i + 1)


def wait(eng, sem, value):
    if isinstance(value, int) and value <= 0:
        return
    eng.wait_ge(sem, value)


def wait_all(eng, passed, *pairs):
    for sem, value in pairs:
        wait(eng, sem, value)
    eng.sem_inc(passed, 1)


def exact_products(mm, out, pairs, start, stop):
    todo = [(l, r) for lh, ll, rh, rl in pairs for l, r in ((lh, rh), (lh, rl), (ll, rh))]
    for i, (l, r) in enumerate(todo):
        last = mm(out, l, r, start=start and i == 0, stop=stop and i == len(todo) - 1)
    return last


def build(nc, t, out):
    ctx = ExitStack()
    with ctx:
        def sb(name, shape, dt=F32):
            return ctx.enter_context(nc.sbuf_tensor(name, shape, dt))

        def sem(name):
            return ctx.enter_context(nc.semaphore(name))

        bank = [ctx.enter_context(nc.psum_tensor(f"bank{i}", [P, 512], F32)) for i in range(8)]

        x1_d = nc.dram_tensor("x1_scratch", [PAIRS, P, D], F32).ap()
        qt_d = nc.dram_tensor("qt_scratch", [PAIRS, P, D], F32).ap()
        kv_d = nc.dram_tensor("kv_scratch", [NB * T, KVW], F32).ap()
        tab_d = nc.dram_tensor("tab_scratch", [NB, SLOTS], F32).ap()
        tabw_d = nc.dram_tensor("tabw_scratch", [NB, WSLOTS], F32).ap()

        x_v = t["x"].rearrange("(n p) f -> n p f", p=P)
        kvd_v = kv_d.rearrange("(n p) f -> n p f", p=P)
        out_v = out.rearrange("(n p) f -> n p f", p=P)
        w2_v = t["w2"].rearrange("(e p) f -> e p f", p=P)

        ident = sb("ident", [P, P])
        mask = sb("mask", [P, MASKW])
        pm = sb("pm", [P, 1], I32)
        pmf = sb("pmf", [P, 1])
        idxT = sb("idxT", [CH, 2 * NCH, NB], I32)
        moff = sb("moff", [1, NB], I32)
        eid = sb("eid", [1, NB], I32)
        onehot = sb("onehot", [2 * 32, NB])
        adapt = sb("adapt", [P, NB])
        NWL = KC * D * 2 + KC * P + D
        wlh = sb("wlh", [P, NWL], F32R)
        wll = sb("wll", [P, NWL], F32R)

        def late(tile, which):
            a, n = {"wo": (0, D), "w3": (KC * D, D), "a": (2 * KC * D, P), "b": (2 * KC * D + KC * P, D)}[which]
            k = 1 if which == "b" else KC
            return tile[:, a:a + k * n].rearrange("p (k n) -> p k n", k=k)

        bparts = sb("bparts", [2 * 32, D], F32R)

        s_const = sem("const_ready")
        s_small = sem("small_in")
        s_pass_pool = sem("pool_passed")
        s_pass_dve = sem("dve_passed")
        s_prep = sem("prep_step")
        s_wqkv = [sem(f"wqkv_in{k}") for k in range(KC)]
        s_wlate = sem("late_weights_in")
        s_tabout = sem("tables_out")
        s_tabin = sem("tables_back")
        s_cnt = sem("counts_ready")
        s_lw = sem("writers_ready")
        s_idxT = sem("indices_turned")
        s_idx = sem("indices_ready")
        s_w0i = sem("w0_index_ready")
        s_g = [sem(f"w0_in{i}") for i in range(4)]
        s_arg = sem("angles_ready")
        s_sin = sem("sines_ready")
        s_cond = sem("cond_in")
        s_wqh = sem("wqkv_high")
        s_wq = sem("wqkv_split")
        s_wlh = sem("late_high")
        s_wl = sem("late_split")
        s_xth = sem("x1t_high")
        s_sum = sem("rotation_summed")
        s_rsum = sem("rotation_half")
        s_ri = sem("norm_ready")

        s_xin = sem("x_in")
        s_bd = sem("w0_block_ready")
        s_l0 = sem("l0_done")
        s_x1 = sem("x1_ready")
        s_xtp = sem("x1_turned")
        s_xt = sem("x1t_ready")
        s_qps = sem("q_done")
        s_kvps = sem("kv_done")
        s_qe = sem("q_copied")
        s_kve = sem("kv_copied")
        s_var = sem("variance_ready")
        s_sd = sem("deviation_ready")
        s_rope = sem("rope_step")
        s_qr = sem("rotated_ready")
        s_qtp = sem("q_turned")
        s_qt = sem("qt_ready")
        s_x1o = sem("x1_out")
        s_qto = sem("qt_out")
        s_kvo = sem("kv_out")

        pa = ExitStack()
        with pa:
            def sa(name, shape, dt=F32):
                return pa.enter_context(nc.sbuf_tensor(name, shape, dt))

            wlr = sa("wlr", [P, NWL])
            wqkv = wlr[:, 0:KC * 1024].rearrange("p (k n) -> p k n", k=KC)
            wqh = sa("wqh", [P, KC, 1024], F32R)
            wql = sa("wql", [P, KC, 1024], F32R)
            b2r = sa("b2r", [2 * 32, D])
            g0 = sa("g0", [P, PAIRS, T])
            g0i = sa("g0i", [P, PAIRS], I32)
            bd = sa("bd", [P, P])
            X = sa("X", [P, D])
            X1 = sa("X1", [P, D])
            XTH = sa("XTH", [P, KC, P], F32R)
            XTL = sa("XTL", [P, KC, P], F32R)
            QK = sa("QK", [P, H + G, HD])
            SQ = sa("SQ", [P, H + G, HD])
            RT = sa("RT", [P, H + G, HD])
            KVR = sa("KVR", [P, KVW])
            QR = sa("QR", [P, H, HD])
            QT = sa("QT", [P, 2, KC, T])
            ss = sa("ss", [P, H + G])
            var = sa("var", [P, H + G])
            sd = sa("sd", [P, H + G])
            ri = sa("ri", [P, H + G])
            tab1 = sa("tab1", [P, 2, PAIRS, HD])
            tab2 = sa("tab2", [P, 2, PAIRS, HD])
            inv = sa("inv", [P, HD // 2])
            nsc = sa("nsc", [P, 2, HD])
            nscn = sa("nscn", [P, 2, HD])
            kvb = sa("kvb", [P, PAIRS], I32)
            cb = sa("cb", [P, PAIRS], I32)
            pos = sa("pos", [P, PAIRS])
            trig = sa("trig", [P, 5, PAIRS, HD // 2])
            ang, tr, trk = trig[:, 0], trig[:, 1:3], trig[:, 3:5]
            kvi = sa("kvi", [NB, 1], I32)
            kvf = sa("kvf", [NB, 1])
            ti = sa("ti", [NB, 1], I32)
            si = sa("si", [NB, 1], I32)
            slot0 = sa("slot0", [NB, 1])
            slotw = sa("slotw", [NB, 1])
            rw = sa("rw", [NB, 1])
            kri = sa("kri", [1, NB], I32)
            krf = sa("krf", [1, NB])
            kr2 = sa("kr2", [1, NB], I32)
            kr3 = sa("kr3", [1, NB])
            i257 = sa("i257", [NB, NW], I32)
            f257 = sa("f257", [NB, NW])
            i80i = sa("i80i", [NB, WSLOTS * BLOCK], I32)
            u80 = sa("u80", [NB, WSLOTS * BLOCK])
            v80 = sa("v80", [NB, WSLOTS * BLOCK])
            c80 = sa("c80", [NB, WSLOTS, BLOCK])
            uc = sa("uc", [NB, WSLOTS, BLOCK])
            bco = sa("bco", [NB, 1], I32)
            bcf = sa("bcf", [NB, 1])
            mxi = sa("mxi", [NB, WSLOTS], I32)
            mxf = sa("mxf", [NB, WSLOTS])
            sl21 = sa("sl21", [NB, SLOTS])
            sl5 = sa("sl5", [NB, WSLOTS])
            tabi = sa("tabi", [NB, NBLK], I32)
            tabf = sa("tabf", [NB, NBLK])
            junk = sa("junk", [NB, NBLK])
            tab21 = sa("tab21", [NB, SLOTS])
            tab5 = sa("tab5", [NB, WSLOTS])
            twb = sa("twb", [NB, NW])
            trb = sa("trb", [NB, NB, SLOTS])
            ew = sa("ew", [NB, NW])
            flat = trig[0:NB, :, :, :].rearrange("p a b c -> p (a b c)")
            MR = NB * SLOTS
            mr = [flat[:, i * MR:(i + 1) * MR] for i in range(3)] + [wlr[0:NB, i * MR:(i + 1) * MR] for i in range(2)]
            later = wlr[0:NB, 2 * MR:2 * MR + WSLOTS * NW].rearrange("p (a b) -> p a b", a=WSLOTS)
            has, oldi, newi = (flat[:, 3 * MR + i * SPAN:3 * MR + (i + 1) * SPAN] for i in range(3))
            phys = sa("phys", [NB, SLOTS, BLOCK])
            idi = sa("idi", [2 * 32, NB], I32)
            idf = sa("idf", [2 * 32, NB])
            pe16i = sa("pe16i", [2 * 32, 1], I32)
            pe16 = sa("pe16", [2 * 32, 1])
            adi = sa("adi", [P, NB], I32)
            adf = sa("adf", [P, NB])
            pni = sa("pni", [P, 1], I32)
            pns = sa("pns", [P, 1], I32)
            pnf = sa("pnf", [P, 1])
            scal = sa("scal", [P, 1])

            N_SMALL = 11
            block = pa.enter_context(nc.Block())

            def bodies(eng, body, between={}):
                cuts = sorted({1, PAIRS - 3, PAIRS - 2, PAIRS - 1, PAIRS} | set(between))
                begin = 0
                for cut in cuts:
                    if cut + 1 - begin <= 2:
                        for p in range(begin, cut + 1):
                            body(p)
                    else:
                        with eng.Fori(begin, cut + 1) as p:
                            body(p)
                    begin = cut + 1
                    if cut in between:
                        between[cut]()

            def has_pair(q):
                return not isinstance(q, int) or 0 <= q < PAIRS

            PREP = {}

            @block.vector
            def _(dve):
                n = [0]

                def step(ins, name=None):
                    n[0] += 1
                    ins.then_inc(s_prep, 1)
                    if name:
                        PREP[name] = n[0]
                    dve.wait_ge(s_prep, n[0])

                v = nc.vector
                dve.wait_ge(s_cond, 32)
                dve.wait_ge(s_const, 2)
                step(v.tensor_copy(pmf[:, :], pm[:, :]))
                v.tensor_scalar(g0i[:, :], cb[:, :], float(T), pmf[:, 0:1], ALU.mult, ALU.add).then_inc(s_w0i, 1)
                dve.wait_ge(s_small, 16 * N_SMALL)
                step(v.tensor_scalar(pos[:, :], kvb[:, :], pmf[:, 0:1], None, ALU.add))
                step(v.tensor_tensor(ang[:, :, :], pos[:, :].unsqueeze(2).to_broadcast([P, PAIRS, HD // 2]),
                                     inv[:, :].unsqueeze(1).to_broadcast([P, PAIRS, HD // 2]), ALU.mult))
                both = (0, 0.0), (1, 0.25)

                def each(ins_of):
                    for k, turn in both:
                        n[0] += 1
                        ins_of(k, turn).then_inc(s_prep, 1)
                    dve.wait_ge(s_prep, n[0])

                each(lambda k, turn: v.tensor_scalar(trk[:, k], ang[:, :, :], 1.0 / (2 * PI), turn, ALU.mult, ALU.add))
                each(lambda k, turn: v.tensor_scalar(trk[:, k], trk[:, k], MAGIC, MAGIC, ALU.add, ALU.subtract))
                each(lambda k, turn: v.scalar_tensor_tensor(tr[:, k], trk[:, k], -C1, ang[:, :, :], ALU.mult, ALU.add))
                each(lambda k, turn: v.scalar_tensor_tensor(tr[:, k], trk[:, k], -C2, tr[:, k], ALU.mult, ALU.add))
                each(lambda k, turn: v.tensor_scalar(tr[:, k], tr[:, k], turn * 2 * PI, 3.1415925, ALU.add, ALU.min))
                each(lambda k, turn: v.tensor_scalar(tr[:, k], tr[:, k], -3.1415925, None, ALU.max))
                v.tensor_scalar(nsc[:, :, :], nsc[:, :, :], 1.0, None, ALU.add).then_inc(s_arg, 1)
                dve.wait_ge(s_arg, 1)
                step(v.tensor_scalar(nscn[:, :, :], nsc[:, :, :], -1.0, None, ALU.mult))

                def tables(a, b):
                    hh = HD // 2
                    for q in range(2):
                        def w(tile, c):
                            return tile[:, q, c:c + hh].unsqueeze(1).to_broadcast([P, b - a, hh])
                        v.tensor_tensor(tab1[:, q, a:b, 0:hh], trk[:, 1, a:b], w(nsc, 0), ALU.mult)
                        v.tensor_tensor(tab1[:, q, a:b, hh:HD], trk[:, 1, a:b], w(nsc, hh), ALU.mult)
                        v.tensor_tensor(tab2[:, q, a:b, 0:hh], trk[:, 0, a:b], w(nsc, 0), ALU.mult)
                        step(v.tensor_tensor(tab2[:, q, a:b, hh:HD], trk[:, 0, a:b], w(nscn, hh), ALU.mult))

                def indices():
                    for i_, f_, j_, g_ in ((kvi, kvf, ti, slot0), (kri, krf, kr2, kr3)):
                        step(v.tensor_copy(f_[:, :], i_[:, :]))
                        yield
                        step(v.tensor_scalar(j_[:, :], f_[:, :], float(1 - WINDOW), 0.0, ALU.add, ALU.max))
                        yield
                        step(v.tensor_scalar(j_[:, :], j_[:, :], 4, None, ALU.arith_shift_right))
                        yield
                        step(v.tensor_scalar(g_[:, :], j_[:, :], float(SLOT_MAX), None, ALU.min))
                        yield
                    step(v.tensor_scalar(si[:, :], kvi[:, :], 4, None, ALU.arith_shift_right))
                    yield
                    step(v.tensor_copy(slotw[:, :], si[:, :]))
                    yield
                    step(v.scalar_tensor_tensor(rw[:, :], slotw[:, :], -float(BLOCK), kvf[:, :], ALU.mult, ALU.add))
                    yield
                    step(v.scalar_tensor_tensor(krf[:, :], kr3[:, :], float(BLOCK), krf[:, :], ALU.mult, ALU.subtract))
                    yield
                    step(v.tensor_scalar(moff[:, :], krf[:, :], float(A_MAX), None, ALU.add))
                    yield
                    step(v.tensor_copy(f257[:, :], i257[:, :]))
                    yield
                    step(v.tensor_copy(tabf[:, :], tabi[:, :]))
                    yield
                    step(v.tensor_scalar(sl21[:, :], f257[:, 0:SLOTS], slot0[:, 0:1], None, ALU.add))
                    yield
                    step(v.tensor_scalar(sl5[:, :], f257[:, 0:WSLOTS], slotw[:, 0:1], None, ALU.add))
                    yield
                    for dst, sl, m in ((tab21, sl21, SLOTS), (tab5, sl5, WSLOTS)):
                        for i in range(m):
                            step(v.scalar_tensor_tensor(junk[:, :], f257[:, 0:NBLK], sl[:, i:i + 1], tabf[:, :],
                                                        ALU.is_equal, ALU.mult, accum_out=dst[:, i:i + 1]),
                                 "tables")
                            yield
                    step(v.tensor_copy(u80[:, :], i80i[:, :]))
                    yield
                    step(v.tensor_scalar(u80[:, :], u80[:, :], rw[:, 0:1], None, ALU.subtract))
                    yield
                    step(v.tensor_scalar(v80[:, :], u80[:, :], 0.0, None, ALU.is_ge))
                    yield
                    step(v.scalar_tensor_tensor(v80[:, :], u80[:, :], float(T), v80[:, :], ALU.is_lt, ALU.mult))
                    yield
                    step(v.tensor_copy(bcf[:, :], bco[:, :]))
                    yield
                    step(v.tensor_copy(mxf[:, :], mxi[:, :]))
                    yield
                    step(v.scalar_tensor_tensor(c80[:, :, :].rearrange("p a b -> p (a b)"), u80[:, :], bcf[:, 0:1],
                                                v80[:, :], ALU.add, ALU.mult))
                    yield
                    dve.wait_ge(s_tabin, 32)
                    dve.wait_ge(s_wq, KC)
                    for i in range(WSLOTS):
                        step(v.tensor_scalar(ew[:, :], twb[:, :], tab5[:, i:i + 1], None, ALU.is_equal))
                        yield
                        step(v.scalar_tensor_tensor(later[:, i, :], f257[:, :], mxf[:, i:i + 1], ew[:, :],
                                                    ALU.is_lt, ALU.mult), "later")
                        yield
                    for i in range(WSLOTS):
                        step(v.tensor_scalar(mr[i], trb[:, :, :].rearrange("p b s -> p (b s)"),
                                             tab5[:, i:i + 1], None, ALU.is_equal))
                        yield
                    dve.wait_ge(s_cnt, 1)
                    step(v.scalar_tensor_tensor(uc[:, :, :].rearrange("p a b -> p (a b)"),
                                                bank[5][0:NB, 0:WSLOTS * BLOCK], 0.0,
                                                c80[:, :, :].rearrange("p a b -> p (a b)"),
                                                ALU.is_equal, ALU.mult), "uc")
                    yield
                    io = f257[:, 0:BLOCK].unsqueeze(1).to_broadcast([NB, SLOTS, BLOCK])
                    step(v.scalar_tensor_tensor(phys[:, :, :], tab21[:, :].unsqueeze(2).to_broadcast([NB, SLOTS, BLOCK]),
                                                float(BLOCK), io, ALU.mult, ALU.add))
                    yield
                    dve.wait_ge(s_lw, 1)
                    lw = bank[6][0:NB, 0:SPAN]
                    step(v.tensor_scalar(has[:, :], lw, 0.0, BIG, ALU.is_gt, ALU.mult))
                    yield
                    step(v.tensor_tensor(oldi[:, :], has[:, :], phys[:, :, :].rearrange("p a b -> p (a b)"), ALU.add))
                    yield
                    step(v.tensor_scalar(has[:, :], lw, 0.0, BIG, ALU.is_equal, ALU.mult))
                    yield
                    step(v.scalar_tensor_tensor(newi[:, :], lw, -1.0, has[:, :], ALU.add, ALU.add), "idx")
                    yield
                    dve.wait_ge(s_idxT, 1)
                    v.tensor_copy(idxT[:, :, :].rearrange("p a b -> p (a b)"),
                                  bank[7][0:CH, 0:2 * NCH * NB]).then_inc(s_idx, 1)
                    step(v.tensor_copy(pe16[:, :], pe16i[:, :]))
                    yield
                    step(v.tensor_copy(idf[:, :], idi[:, :]))
                    yield
                    step(v.tensor_scalar(onehot[:, :], idf[:, :], pe16[:, 0:1], None, ALU.is_equal))
                    yield
                    step(v.tensor_scalar(pns[:, :], pni[:, :], 4, None, ALU.arith_shift_right))
                    yield
                    step(v.tensor_copy(pnf[:, :], pns[:, :]))
                    yield
                    step(v.tensor_copy(adf[:, :], adi[:, :]))
                    yield
                    step(v.tensor_scalar(adapt[:, :], adf[:, :], pnf[:, 0:1], scal[:, 0:1], ALU.is_equal, ALU.mult))
                    yield

                def first(q):
                    dve.wait_ge(s_xin, at(q, 16, 15))
                    dve.wait_ge(s_l0, at(q, 1, 0))
                    wait(dve, s_x1o, 16 * q)
                    wait(dve, s_xtp, q)
                    v.tensor_tensor(X1[:, :], bank[0][:, :], X[:, :], ALU.add).then_inc(s_x1, 1)

                def turned(q):
                    dve.wait_ge(s_xth, at(q, 1, 0))
                    v.tensor_tensor(XTL[:, :, :].rearrange("p a b -> p (a b)"), bank[1][:, :],
                                    XTH[:, :, :].rearrange("p a b -> p (a b)").bitcast(F32),
                                    ALU.subtract).then_inc(s_xt, 1)

                def body(p):
                    if has_pair(p + 1):
                        turned(p + 1)
                    if has_pair(p + 2):
                        first(p + 2)
                    if not has_pair(p):
                        return
                    R = 5
                    pp = bass.ds(p, 1)
                    dve.wait_ge(s_kve, at(p, 1, 0))
                    wait(dve, s_qr, p)
                    v.tensor_reduce(ss[:, :], SQ[:, :, :], AXX, ALU.add).then_inc(s_rope, 1)
                    for q, (a, b) in enumerate(((0, H), (H, H + G))):
                        v.tensor_tensor(RT[:, a:b, :], QK[:, a:b, :],
                                        tab1[:, q, pp, :].to_broadcast([P, b - a, HD]), ALU.mult).then_inc(s_rope, 1)
                    dve.wait_ge(s_rope, at(p, R, 0))
                    v.tensor_scalar(var[:, :], ss[:, :], 1.0 / HD, EPS, ALU.mult, ALU.add).then_inc(s_var, 1)
                    for q, (a, b) in enumerate(((0, H), (H, H + G))):
                        v.tensor_tensor(SQ[:, a:b, :], QK[:, a:b, :],
                                        tab2[:, q, pp, :].to_broadcast([P, b - a, HD]), ALU.mult).then_inc(s_rope, 1)
                    dve.wait_ge(s_rope, at(p, R, R - 1))
                    dve.wait_ge(s_sd, at(p, 1, 0))
                    v.reciprocal(ri[:, :], sd[:, :]).then_inc(s_ri, 1)

                def split(high, low, raw):
                    return v.tensor_tensor(low, raw, high.bitcast(F32), ALU.subtract)

                first(0)
                for k in range(KC):
                    dve.wait_ge(s_wqh, k + 1)
                    split(wqh[:, k, :], wql[:, k, :], wqkv[:, k, :]).then_inc(s_wq, 1)
                turned(0)
                first(1)
                dve.wait_ge(s_sin, 1)
                tables(0, 8)
                work = indices()

                def go_on(n_steps):
                    def run():
                        for _ in range(n_steps):
                            next(work)
                    return run

                def late_low(i):
                    def run():
                        dve.wait_ge(s_wlh, i + 1)
                        part = slice(i * 1024, (i + 1) * 1024)
                        split(wlh[:, part], wll[:, part], wlr[:, part]).then_inc(s_wl, 1)
                        if i == 4:
                            dve.wait_ge(s_wlh, 6)
                            low = slice(32, 32 + E)
                            split(bparts[low, :], bparts[low, :], b2r[low, :]).then_inc(s_wl, 1)
                    return run

                between = {1: lambda: tables(8, 16), 3: lambda: tables(16, 24), 5: lambda: tables(24, 32)}
                between.update({p: go_on(8) for p in (6, 7, 8, 9, 10)} | {11: go_on(3), 14: go_on(7)})
                between.update({p: go_on(5) for p in (16, 17, 18)})
                between.update({20: go_on(2), 24: go_on(4), 28: go_on(7)})
                between.update({p: late_low(i) for i, p in enumerate((26, 27, 29, 30, 31))})
                bodies(dve, body, between)
                assert next(work, "end") == "end"

            @block.sync
            def _(sp):
                sp.dma_start(cb[0:T, :], t["cond2"][0, :].partition_broadcast(T)).then_inc(s_cond, 16)
                sp.dma_start(cb[T:P, :], t["cond2"][1, :].partition_broadcast(T)).then_inc(s_cond, 16)
                sp.dma_start(X[:, :], x_v[0]).then_inc(s_xin, 16)
                for dst, src in (
                    (kvb[0:T, :], t["kv2"][0, :].partition_broadcast(T)),
                    (kvb[T:P, :], t["kv2"][1, :].partition_broadcast(T)),
                    (inv[:, :], t["inv"].partition_broadcast(P)),
                    (nsc[:, 0, :], t["qs"].partition_broadcast(P)),
                    (nsc[:, 1, :], t["ks"].partition_broadcast(P)),
                    (kvi[:, :], t["kv"].rearrange("(b o) -> b o", o=1)),
                    (kri[:, :], t["kv"].rearrange("(o b) -> o b", o=1)),
                    (tabi[:, :], t["tab"]),
                    (idi[:, :], t["id"].partition_broadcast(2 * 32)),
                    (adi[:, :], t["ad"].partition_broadcast(P)),
                    (scal[:, :], t["scal"]),
                ):
                    sp.dma_start(dst, src).then_inc(s_small, 16)
                for k in range(KC):
                    sp.dma_start(wqkv[:, k, :], t["wqkv"][k * P:(k + 1) * P, :]).then_inc(s_wqkv[k], 16)
                sp.dma_start(eid[:, :], t["id"].rearrange("(o b) -> o b", o=1)).then_inc(s_wlate, 16)
                sp.wait_ge(s_x1, 1)
                sp.dma_start(X[:, :], x_v[1]).then_inc(s_xin, 16)
                sp.dma_start(x1_d[0], X1[:, :]).then_inc(s_x1o, 16)
                def body(p):
                    if has_pair(p + 1):
                        sp.wait_ge(s_x1, at(p + 1, 1, 0))
                        sp.dma_start(x1_d[bass.ds(p + 1, 1)], X1[:, :]).then_inc(s_x1o, 16)
                    if has_pair(p + 2):
                        sp.dma_start(X[:, :], x_v[bass.ds(p + 2, 1)]).then_inc(s_xin, 16)
                    if has_pair(p - 1):
                        sp.wait_ge(s_qr, at(p - 1, 1, 0))
                        sp.dma_start(kvd_v[bass.ds(p - 1, 1)], KVR[:, :]).then_inc(s_kvo, 16)
                        sp.wait_ge(s_qt, at(p - 1, 1, 0))
                        sp.dma_start(qt_d[bass.ds(p - 1, 1)],
                                     QT[:, :, :, :].rearrange("p b c t -> p (b c t)")).then_inc(s_qto, 16)

                def tables_round():
                    sp.wait_ge(s_prep, PREP["tables"])
                    sp.dma_start(tab_d, tab21[:, :]).then_inc(s_tabout, 16)
                    sp.dma_start(tabw_d, tab5[:, :]).then_inc(s_tabout, 16)
                    sp.wait_ge(s_tabout, 32)
                    sp.dma_start(twb[:, :], tabw_d.rearrange("b s -> (b s)").partition_broadcast(NB)
                                 ).then_inc(s_tabin, 16)
                    sp.dma_start(trb[:, :, :].rearrange("p b s -> p (b s)"),
                                 tab_d.rearrange("b s -> (b s)").partition_broadcast(NB)).then_inc(s_tabin, 16)

                def late_weights():
                    sp.wait_ge(s_const, N_CONST)
                    sp.wait_ge(s_lw, 1)
                    for dst, src in (
                        (late(wlr, "wo"), t["woT"].rearrange("(k p) n -> p k n", p=P)),
                        (late(wlr, "w3"), t["w3T"].rearrange("(k p) n -> p k n", p=P)),
                        (late(wlr, "a"), t["aT"].rearrange("(k p) n -> p k n", p=P)),
                        (late(wlr, "b")[:, 0, :], t["bT"]),
                        (b2r[0:E, :], t["b2"]),
                        (b2r[32:32 + E, :], t["b2"]),
                    ):
                        sp.dma_start(dst, src).then_inc(s_wlate, 16)

                bodies(sp, body, {13: tables_round, 23: late_weights})
                sp.wait_ge(s_x1o, 16 * PAIRS)
                sp.wait_ge(s_kvo, 16 * PAIRS)
                sp.wait_ge(s_qto, 16 * PAIRS)

            @block.gpsimd
            def _(pool):
                made = [0]

                def make(ins):
                    made[0] += 1
                    ins.then_inc(s_const, 1)
                    pool.wait_ge(s_const, made[0])

                for tile, step, base, up in ((pm[0:T, :], 0, 0, 1), (pm[T:P, :], 0, 0, 1), (i257[:, :], 1, 0, 0),
                                             (i80i[:, :], 1, 0, 0), (bco[:, :], 0, 1, T), (mxi[:, :], 1, 0, WSLOTS),
                                             (pe16i[0:32, :], 0, 0, 1),
                                             (pe16i[32:64, :], 0, 0, 1), (pni[:, :], 0, 0, 1)):
                    make(nc.gpsimd.iota(tile, pattern=[[step, tile.shape[1]]], base=base, channel_multiplier=up))
                for tile in (bd, ident, mask, b2r):
                    make(nc.gpsimd.memset(tile[:, :], 0.0))
                make(nc.gpsimd.affine_select(out=ident[:, :], in_=ident[:, :], compare_op=ALU.not_equal, fill=1.0,
                                             base=0, pattern=[[-1, P]], channel_multiplier=1))
                for j in range(2):
                    m = mask[T * j:T * (j + 1), :]
                    make(nc.gpsimd.affine_select(out=m, in_=m, compare_op=ALU.is_ge, fill=NEG, base=A_MAX,
                                                 pattern=[[-1, MASKW]], channel_multiplier=1))
                    make(nc.gpsimd.affine_select(out=m, in_=m, compare_op=ALU.is_ge, fill=NEG,
                                                 base=WINDOW - 1 - A_MAX, pattern=[[1, MASKW]],
                                                 channel_multiplier=-1))
                assert made[0] == N_CONST
                pool.wait_ge(s_w0i, 1)
                for q in range(PAIRS):
                    pool.indirect_dma_start(out=g0[:, q, :], out_offset=None, in_=t["w0"],
                                            in_offset=bass.IndirectOffsetOnAxis(ap=g0i[:, q:q + 1], axis=0)
                                            ).then_inc(s_g[q % 4], 16)

                def block_of(q):
                    for half in range(2):
                        rows = slice(half * T, (half + 1) * T)
                        if half == 0:
                            wait_all(pool, s_pass_pool, (s_l0, q))
                        else:
                            wait_all(pool, s_pass_pool, (s_bd, at(q, 2, 0)))
                        nc.gpsimd.tensor_copy(bd[rows, rows], g0[rows, bass.ds(q, 1), :].rearrange("p o c -> p (o c)")
                                              ).then_inc(s_bd, 1)

                for i in range(4):
                    pool.wait_ge(s_g[i], 16 * (PAIRS // 4))
                block_of(0)
                block_of(1)

                def body(p):
                    if has_pair(p + 2):
                        block_of(p + 2)
                    if not has_pair(p):
                        return
                    hh = HD // 2
                    g = nc.gpsimd
                    pool.wait_ge(s_rope, at(p, 5, 4))
                    g.tensor_tensor(RT[:, :, 0:hh], RT[:, :, 0:hh], SQ[:, :, hh:HD], ALU.add).then_inc(s_rsum, 1)
                    pool.wait_ge(s_rsum, at(p, 1, 0))
                    g.tensor_tensor(RT[:, :, hh:HD], RT[:, :, hh:HD], SQ[:, :, 0:hh], ALU.add).then_inc(s_sum, 1)
                    pool.wait_ge(s_sum, at(p, 1, 0))
                    pool.wait_ge(s_ri, at(p, 1, 0))
                    wait(pool, s_qtp, p)
                    wait(pool, s_kvo, 16 * p)
                    g.tensor_tensor(QR[:, :, :], RT[:, 0:H, :], ri[:, 0:H].unsqueeze(2).to_broadcast([P, H, HD]),
                                    ALU.mult)
                    g.tensor_tensor(KVR[:, 0:G * HD].rearrange("p (g d) -> p g d", g=G), RT[:, H:H + G, :],
                                    ri[:, H:H + G].unsqueeze(2).to_broadcast([P, G, HD]),
                                    ALU.mult).then_inc(s_qr, 1)

                bodies(pool, body)

            @block.scalar
            def _(act):
                def copy(dst, src):
                    return nc.scalar.activation(dst, src, ACT.Copy)

                def turned(q):
                    act.wait_ge(s_xtp, at(q, 1, 0))
                    wait(act, s_kvps, q)
                    copy(XTH[:, :, :].rearrange("p a b -> p (a b)"), bank[1][:, :]).then_inc(s_xth, 1)

                for k in range(KC):
                    act.wait_ge(s_wqkv[k], 16)
                    copy(wqh[:, k, :], wqkv[:, k, :]).then_inc(s_wqh, 1)
                turned(0)
                act.wait_ge(s_arg, 1)
                nc.scalar.activation(trk, tr, ACT.Sin).then_inc(s_sin, 1)

                def late_high(i):
                    def run():
                        act.wait_ge(s_wlate, 16 * 7)
                        part = slice(i * 1024, (i + 1) * 1024)
                        copy(wlh[:, part], wlr[:, part]).then_inc(s_wlh, 1)
                        if i == 4:
                            copy(bparts[:, :], b2r[:, :]).then_inc(s_wlh, 1)
                    return run

                def body(p):
                    if has_pair(p):
                        act.wait_ge(s_qps, at(p, 1, 0))
                        wait(act, s_rope, 5 * p)
                        wait(act, s_sum, p)
                        bq = bank[2][:, :].rearrange("p (h d) -> p h d", h=H)
                        copy(QK[:, 0:H, :], bq)
                        nc.scalar.activation(SQ[:, 0:H, :], bq, ACT.Square).then_inc(s_qe, 1)
                    if has_pair(p + 1):
                        turned(p + 1)
                    if has_pair(p):
                        act.wait_ge(s_kvps, at(p, 1, 0))
                        wait(act, s_kvo, 16 * p)
                        bk = bank[3][:, 0:G * HD].rearrange("p (g d) -> p g d", g=G)
                        copy(QK[:, H:H + G, :], bk)
                        nc.scalar.activation(SQ[:, H:H + G, :], bk, ACT.Square)
                        copy(KVR[:, G * HD:KVW], bank[3][:, G * HD:KVW]).then_inc(s_kve, 1)
                    if has_pair(p - 1):
                        wait(act, s_qto, 16 * (p - 1))
                        act.wait_ge(s_qtp, at(p - 1, 1, 0))
                        copy(QT[:, :, :, :].rearrange("p b c t -> p c b t"),
                             bank[4][:, :].rearrange("p (c b t) -> p c b t", c=KC, b=2)).then_inc(s_qt, 1)
                    if has_pair(p):
                        act.wait_ge(s_var, at(p, 1, 0))
                        nc.scalar.activation(sd[:, :], var[:, :], ACT.Sqrt).then_inc(s_sd, 1)

                bodies(act, body, {p: late_high(i) for i, p in enumerate((25, 26, 27, 28, 29))})

            @block.tensor
            def _(pe):
                mm = nc.tensor.matmul
                def counts():
                    pe.wait_ge(s_prep, PREP["later"])
                    for i2 in range(WSLOTS):
                        for i in range(WSLOTS):
                            last = mm(bank[5][0:NB, i2 * BLOCK:(i2 + 1) * BLOCK],
                                      later[:, i, :].rearrange("p (b s) -> p b s", s=WSLOTS)[:, :, i2],
                                      v80[:, i * BLOCK:(i + 1) * BLOCK], start=(i == 0), stop=(i == WSLOTS - 1))
                    last.then_inc(s_cnt, 1)

                def writers():
                    pe.wait_ge(s_prep, PREP["uc"])
                    for m in range(SLOTS):
                        for i in range(WSLOTS):
                            last = mm(bank[6][0:NB, m * BLOCK:(m + 1) * BLOCK],
                                      mr[i].rearrange("p (b s) -> p b s", s=SLOTS)[:, :, m],
                                      uc[:, i, :], start=(i == 0), stop=(i == WSLOTS - 1))
                    last.then_inc(s_lw, 1)

                def turn_indices():
                    pe.wait_ge(s_prep, PREP["idx"])
                    for k, tile in enumerate((oldi, newi)):
                        for c in range(NCH):
                            a = (k * NCH + c) * NB
                            last = nc.tensor.transpose(bank[7][0:CH, a:a + NB], tile[:, c * CH:(c + 1) * CH],
                                                       ident[0:NB, 0:NB])
                    last.then_inc(s_idxT, 1)

                def l0(q):
                    pe.wait_ge(s_xin, at(q, 16, 15))
                    pe.wait_ge(s_bd, at(q, 2, 1))
                    wait(pe, s_x1, q)
                    mm(bank[0][:, :], bd[:, :], X[:, :], start=True, stop=True).then_inc(s_l0, 1)

                def xt(q):
                    pe.wait_ge(s_x1, at(q, 1, 0))
                    wait(pe, s_xt, q)
                    for k in range(KC):
                        last = nc.tensor.transpose(bank[1][:, k * P:(k + 1) * P], X1[:, k * P:(k + 1) * P],
                                                   ident[:, :])
                    last.then_inc(s_xtp, 1)

                def body(p):
                    if has_pair(p):
                        pe.wait_ge(s_xt, at(p, 1, 0))
                        wait(pe, s_qe, p)
                        exact_products(mm, bank[2][:, :], [(XTH[:, k, :], XTL[:, k, :], wqh[:, k, 0:512],
                                                            wql[:, k, 0:512]) for k in range(KC)],
                                       True, True).then_inc(s_qps, 1)
                        wait(pe, s_kve, p)
                        exact_products(mm, bank[3][:, :], [(XTH[:, k, :], XTL[:, k, :], wqh[:, k, 512:1024],
                                                            wql[:, k, 512:1024]) for k in range(KC)],
                                       True, True).then_inc(s_kvps, 1)
                    if has_pair(p + 1):
                        xt(p + 1)
                    if has_pair(p - 1):
                        pe.wait_ge(s_qr, at(p - 1, 1, 0))
                        wait(pe, s_qt, p - 1)
                        for c in range(KC):
                            last = nc.tensor.transpose(bank[4][:, c * P:(c + 1) * P],
                                                       QR[:, 2 * c:2 * c + 2, :].rearrange("p a b -> p (a b)"),
                                                       ident[:, :])
                        last.then_inc(s_qtp, 1)
                    if has_pair(p + 2):
                        l0(p + 2)

                pe.wait_ge(s_const, N_CONST)
                l0(0)
                xt(0)
                l0(1)
                pe.wait_ge(s_wq, KC)
                bodies(pe, body, {19: counts, 22: writers, 26: turn_indices})

        pb = ExitStack()
        with pb:
            def sbt(name, shape, dt=F32):
                return pb.enter_context(nc.sbuf_tensor(name, shape, dt))

            KV = [sbt(f"KV{i}", [CH, NCH, KVW]) for i in range(4)]
            idxs = [sbt(f"idxs{i}", [CH, 2 * NCH], I32) for i in range(4)]
            FM = [sbt(f"FM{i}", [P, SPAN]) for i in range(4)]
            QB = [sbt(f"QB{i}", [P, 2, KC, T]) for i in range(2)]
            KT = [sbt(f"KT{i}", [P, GP, SPAN]) for i in range(2)]
            SM = [sbt(f"SM{i}", [P, SPAN]) for i in range(2)]
            PR = [sbt(f"PR{i}", [P, SPAN]) for i in range(2)]
            PT = [sbt(f"PT{i}", [CH, NCH, P]) for i in range(2)]
            ON = [sbt(f"ON{i}", [P, G, HD]) for i in range(2)]
            OTH = sbt("OTH", [P, KC, 2, T], F32R)
            OTL = sbt("OTL", [P, KC, 2, T], F32R)
            mx = sbt("mx", [P, 8])
            nb = sbt("nb", [P, 8])
            rs = sbt("rs", [P, 8])
            rinv = sbt("rinv", [P, 8])
            W2 = [sbt(f"W2{i}", [P, KC * D]) for i in range(2)]
            W2H = [sbt(f"W2H{i}", [P, KC * D], F32R) for i in range(2)]
            W2L = [sbt(f"W2L{i}", [P, KC * D], F32R) for i in range(2)]
            XB1 = sbt("XB1", [P, D])
            XB2 = sbt("XB2", [P, D])
            XB3 = sbt("XB3", [P, D])
            XO = sbt("XO", [P, D])
            XT2 = sbt("XT2", [P, KC, 2, 2, T], F32R)
            XTH3 = sbt("XTH3", [P, KC, P], F32R)
            XTL3 = sbt("XTL3", [P, KC, P], F32R)
            OHS = sbt("OHS", [2 * 32, 2, P], F32R)
            XAM = sbt("XAM", [P, 2, T])
            XAH = sbt("XAH", [P, P], F32R)
            XAL = sbt("XAL", [P, P], F32R)

            s_reg = [sem(f"gather_args{i}") for i in range(4)]
            s_old = [sem(f"kv_old{i}") for i in range(4)]
            s_new = [sem(f"kv_new{i}") for i in range(4)]
            s_qin = [sem(f"qt_in{i}") for i in range(2)]
            s_x1in = sem("x1_in")
            s_w2in = [sem(f"w2_in{i}") for i in range(2)]
            s_w2h = [sem(f"w2_high{i}") for i in range(2)]
            s_w2l = [sem(f"w2_split{i}") for i in range(2)]
            s_ost = sem("out_stored")
            s_ktp = sem("keys_turned")
            s_kt = sem("kt_ready")
            s_s = sem("scores_done")
            s_mx = sem("max_ready")
            s_m = sem("masked_ready")
            s_e = sem("probs_ready")
            s_ptp = sem("probs_turned")
            s_pt = [sem(f"pt_ready{i}") for i in range(2)]
            s_pv = sem("pv_done")
            s_rinv = sem("sums_inverted")
            s_on = sem("heads_ready")
            s_otp = sem("heads_turned")
            s_oth = sem("ot_high")
            s_ot = sem("ot_ready")
            s_o = sem("o_done")
            s_x2 = sem("x2_ready")
            s_x2p = sem("x2_turned")
            s_xt2h = sem("x2t_high")
            s_xt2 = sem("x2t_ready")
            s_ohz = sem("onehot_cleared")
            s_oh = sem("onehot_ready")
            s_l2 = sem("l2_done")
            s_x3a = sem("x3_half")
            s_x3 = sem("x3_ready")
            s_x3p = sem("x3_turned")
            s_xt3h = sem("x3t_high")
            s_xt3 = sem("x3t_ready")
            s_xa = sem("xa_done")
            s_xam = sem("xa_masked")
            s_xah = sem("xa_high")
            s_xal = sem("xa_split")
            s_l3 = sem("l3_done")
            s_xo = sem("out_ready")
            L2BANK = (bank[7], bank[6])

            block = pb.enter_context(nc.Block())

            def bodies(eng, body):
                body(Pair(0, 0), True, False)
                body(Pair(0, 1), True, True)
                with eng.Fori(1, PAIRS // 2 - 1) as i:
                    body(Pair(i, 0), True, True)
                    body(Pair(i, 1), True, True)
                body(Pair(PAIRS // 2 - 1, 0), True, True)
                body(Pair(PAIRS // 2 - 1, 1), True, True)
                body(Pair(PAIRS // 2, 0), False, True)

            def last_pair(pr):
                return isinstance(pr.n, int) and pr.n == PAIRS - 1

            @block.gpsimd
            def _(pool):
                def body(pr, attention, dense):
                    if not attention:
                        return
                    p = pr.n
                    for b in range(2):
                        k = 2 * pr.par + b
                        used = 8 * (p - 2) + 4 * (b + 1)
                        n = p * 2 + b
                        m0 = pool.value_load(moff[0:1, bass.ds(n, 1)], min_val=0, max_val=A_MAX)
                        wait_all(pool, s_pass_pool, (s_new[k], 16 * NCH * pr.i))
                        nc.gpsimd.tensor_copy(idxs[k][:, :], idxT[:, :, bass.ds(n, 1)].rearrange("p a o -> p (a o)")
                                              ).then_inc(s_reg[k], 1)
                        wait_all(pool, s_pass_pool, (s_mx, used))
                        nc.gpsimd.tensor_copy(FM[k][:, :], mask[:, bass.ds(m0, SPAN)]).then_inc(s_reg[k], 1)
                        wait_all(pool, s_pass_pool, (s_pv, used), (s_reg[k], at(pr.i, 2, 0)))
                        for c in range(NCH):
                            pool.indirect_dma_start(
                                out=KV[k][:, c, :], out_offset=None, in_=t["pool"],
                                in_offset=bass.IndirectOffsetOnAxis(ap=idxs[k][:, c:c + 1], axis=0),
                                bounds_check=NPOOL * BLOCK - 1, oob_is_err=False).then_inc(s_old[k], 16)
                        wait_all(pool, s_pass_pool, (s_old[k], at(pr.i, 16 * NCH, 16 * NCH - 1)))
                        for c in range(NCH):
                            pool.indirect_dma_start(
                                out=KV[k][:, c, :], out_offset=None, in_=kv_d,
                                in_offset=bass.IndirectOffsetOnAxis(ap=idxs[k][:, NCH + c:NCH + c + 1], axis=0),
                                bounds_check=NB * T - 1, oob_is_err=False).then_inc(s_new[k], 16)

                bodies(pool, body)

            @block.sync
            def _(sp):
                def queries(pr):
                    wait(sp, s_s, 8 * (pr.n - 1))
                    sp.dma_start(QB[pr.par][:, :, :, :].rearrange("p b c t -> p (b c t)"),
                                 qt_d[bass.ds(pr.n, 1)]).then_inc(s_qin[pr.par], 16)

                def store(q):
                    sp.wait_ge(s_xo, at(q, 1, 0))
                    sp.dma_start(out_v[bass.ds(q, 1)], XO[:, :]).then_inc(s_ost, 16)

                queries(Pair(0, 0))

                def body(pr, attention, dense):
                    q = pr.n - 1
                    if dense:
                        wait(sp, s_x2, q)
                        sp.dma_start(XB1[:, :], x1_d[bass.ds(q, 1)]).then_inc(s_x1in, 16)
                        for b in range(2):
                            e = sp.value_load(eid[0:1, bass.ds(q * 2 + b, 1)], min_val=0, max_val=E - 1)
                            wait(sp, s_w2l[b], q)
                            sp.dma_start(W2[b][:, :], w2_v[bass.ds(e, 1)]).then_inc(s_w2in[b], 16)
                    if attention and not last_pair(pr):
                        queries(pr.move(1))
                    if dense and not (isinstance(q, int) and q == 0):
                        store(q - 1)

                bodies(sp, body)
                store(PAIRS - 1)
                sp.wait_ge(s_ost, 16 * PAIRS)

            @block.scalar
            def _(act):
                def copy(dst, src):
                    return nc.scalar.activation(dst, src, ACT.Copy)

                def keys(pr, b, gp):
                    act.wait_ge(s_ktp, at(pr.n, 4, 2 * b + gp))
                    copy(KT[b][:, gp, :], bank[4][:, 0:SPAN]).then_inc(s_kt, 1)

                def exp(p, u):
                    act.wait_ge(s_m, at(p, 8, u))
                    wait(act, s_ptp, p * 8 + u - 1)
                    nc.scalar.activation(PR[u % 2][:, :], SM[u % 2][:, :], ACT.Exp, bias=nb[:, u:u + 1],
                                         scale=SCALE, accum_out=rs[:, u:u + 1]).then_inc(s_e, 1)

                def probs(p, u):
                    act.wait_ge(s_ptp, at(p, 8, u))
                    wait(act, s_pv, p * 8 + u - 1)
                    copy(PT[u % 2][:, :, :].rearrange("p c t -> p (c t)"),
                         bank[2 + u % 2][0:CH, 0:NCH * P]).then_inc(s_pt[u % 2], 1)

                def heads(p, b):
                    act.wait_ge(s_otp, at(p, 2, b))
                    copy(OTH[:, :, b, :], bank[4][:, 0:256].rearrange("p (c t) -> p c t", c=KC)).then_inc(s_oth, 1)

                def expert(q, b):
                    act.wait_ge(s_w2in[b], at(q, 16, 15))
                    wait(act, s_l2, 2 * q - 1 + b)
                    copy(W2H[b][:, :], W2[b][:, :]).then_inc(s_w2h[b], 1)

                def body(pr, attention, dense):
                    p, q = pr.n, pr.n - 1
                    if attention:
                        exp(p, 0)
                        exp(p, 1)
                    if dense:
                        heads(q, 1)
                        expert(q, 0)
                    if attention:
                        exp(p, 2)
                        probs(p, 1)
                        keys(pr, 1, 0)
                        exp(p, 3)
                    if dense:
                        act.wait_ge(s_x2p, at(q, 1, 0))
                        for b in range(2):
                            last = copy(XT2[:, :, b, 0, :], bank[4][:, :].rearrange("p (k b t) -> p k b t", b=2, t=T)
                                        [:, :, b, :])
                        last.then_inc(s_xt2h, 1)
                        expert(q, 1)
                    if attention:
                        keys(pr, 1, 1)
                        exp(p, 4)
                        probs(p, 3)
                        exp(p, 5)
                        exp(p, 6)
                        probs(p, 5)
                    if dense:
                        act.wait_ge(s_x3p, at(q, 1, 0))
                        copy(XTH3[:, :, :].rearrange("p k t -> p (k t)"), bank[4][:, :]).then_inc(s_xt3h, 1)
                    if attention:
                        heads(p, 0)
                        exp(p, 7)
                        probs(p, 7)
                        if not last_pair(pr):
                            keys(pr.move(1), 0, 0)
                            keys(pr.move(1), 0, 1)

                keys(Pair(0, 0), 0, 0)
                keys(Pair(0, 0), 0, 1)
                bodies(act, body)

            @block.vector
            def _(dve):
                v = nc.vector
                v.memset(OHS[:, :, :].bitcast(F32), 0.0).then_inc(s_ohz, 1)
                dve.wait_ge(s_ohz, 1)

                def low(dst, exact, high):
                    return v.tensor_tensor(dst, exact, high.bitcast(F32), ALU.subtract)

                def masked(pr, u):
                    p, k = pr.n, 2 * pr.par + u // 4
                    wait_all(dve, s_pass_dve, (s_reg[k], at(pr.i, 2, 1)), (s_e, p * 8 + u - 1), (s_s, at(p, 8, u)))
                    v.tensor_tensor_reduce(out=SM[u % 2][:, :], in0=bank[u % 2][:, 0:SPAN], in1=FM[k][:, :],
                                           scale=1.0, scalar=-3e38, op0=ALU.add, op1=ALU.max,
                                           accum_out=mx[:, u:u + 1]).then_inc(s_mx, 1)
                    dve.wait_ge(s_mx, at(p, 8, u))
                    v.tensor_scalar(nb[:, u:u + 1], mx[:, u:u + 1], -SCALE, None, ALU.mult).then_inc(s_m, 1)

                def probs(p, u):
                    dve.wait_ge(s_ptp, at(p, 8, u))
                    wait(dve, s_pv, p * 8 + u - 1)
                    v.tensor_copy(PT[u % 2][:, :, :].rearrange("p c t -> p (c t)"),
                                  bank[2 + u % 2][0:CH, 0:NCH * P]).then_inc(s_pt[u % 2], 1)

                def norm(p, b):
                    dve.wait_ge(s_e, at(p, 8, 4 * b + 3))
                    v.reciprocal(rinv[:, 4 * b:4 * b + 4], rs[:, 4 * b:4 * b + 4]).then_inc(s_rinv, 1)
                    dve.wait_ge(s_pv, at(p, 8, 4 * b + 3))
                    dve.wait_ge(s_rinv, at(p, 2, b))
                    v.tensor_tensor(ON[b][:, :, :], bank[5][:, 0:256].rearrange("p (g d) -> p g d", g=G),
                                    rinv[:, 4 * b:4 * b + 4].unsqueeze(2).to_broadcast([P, G, HD]),
                                    ALU.mult).then_inc(s_on, 1)

                def heads(p, b):
                    dve.wait_ge(s_oth, at(p, 2, b))
                    low(OTL[:, :, b, :], bank[4][:, 0:256].rearrange("p (c t) -> p c t", c=KC),
                        OTH[:, :, b, :]).then_inc(s_ot, 1)

                def expert(q, b):
                    dve.wait_ge(s_w2h[b], at(q, 1, 0))
                    low(W2L[b][:, :], W2[b][:, :], W2H[b][:, :]).then_inc(s_w2l[b], 1)

                def x3(q, b):
                    rows = slice(b * T, (b + 1) * T)
                    dve.wait_ge(s_l2, at(q, 2, b))
                    v.tensor_tensor(XB3[rows, :], L2BANK[b][0:T, :], XB2[rows, :], ALU.add).then_inc(s_x3a, 1)
                    dve.wait_ge(s_x3a, at(q, 2, b))
                    v.tensor_tensor(XB3[rows, :], L2BANK[b][T:P, :], XB3[rows, :], ALU.add).then_inc(s_x3, 1)

                def body(pr, attention, dense):
                    p, q = pr.n, pr.n - 1
                    if dense:
                        for rows, cols in ((slice(0, 32), slice(0, T)), (slice(32, 64), slice(T, P))):
                            wait_all(dve, s_pass_dve, (s_l2, 2 * q))
                            v.tensor_copy(OHS[rows, :, cols],
                                          onehot[rows, bass.ds(q * 2, 2)].unsqueeze(2).to_broadcast([32, 2, T])
                                          ).then_inc(s_oh, 1)
                        norm(q, 1)
                    if attention:
                        masked(pr, 0)
                        masked(pr, 1)
                    if dense:
                        heads(q, 1)
                    if attention:
                        probs(p, 0)
                    if dense:
                        expert(q, 0)
                        dve.wait_ge(s_o, at(q, 1, 0))
                        dve.wait_ge(s_x1in, at(q, 16, 15))
                        v.tensor_tensor(XB2[:, :], bank[6][:, :], XB1[:, :], ALU.add).then_inc(s_x2, 1)
                    if attention:
                        masked(pr, 2)
                        masked(pr, 3)
                        probs(p, 2)
                    if dense:
                        dve.wait_ge(s_xt2h, at(q, 1, 0))
                        for b in range(2):
                            last = low(XT2[:, :, b, 1, :],
                                       bank[4][:, :].rearrange("p (k b t) -> p k b t", b=2, t=T)[:, :, b, :],
                                       XT2[:, :, b, 0, :])
                        last.then_inc(s_xt2, 1)
                    if attention:
                        masked(pr, 4)
                    if dense:
                        expert(q, 1)
                    if attention:
                        masked(pr, 5)
                        probs(p, 4)
                    if dense:
                        dve.wait_ge(s_x2, at(q, 1, 0))
                        x3(q, 0)
                    if attention:
                        norm(p, 0)
                        masked(pr, 6)
                    if dense:
                        x3(q, 1)
                        dve.wait_ge(s_xt3h, at(q, 1, 0))
                        low(XTL3[:, :, :].rearrange("p k t -> p (k t)"), bank[4][:, :],
                            XTH3[:, :, :].rearrange("p k t -> p (k t)")).then_inc(s_xt3, 1)
                    if attention:
                        heads(p, 0)
                        masked(pr, 7)
                        probs(p, 6)
                    if dense:
                        dve.wait_ge(s_xa, at(q, 1, 0))
                        v.tensor_tensor(XAM[:, :, :], bank[4][:, 0:P].rearrange("p (b t) -> p b t", b=2),
                                        adapt[:, bass.ds(q * 2, 2)].unsqueeze(2).to_broadcast([P, 2, T]),
                                        ALU.mult).then_inc(s_xam, 1)
                        xam = XAM[:, :, :].rearrange("p b t -> p (b t)")
                        dve.wait_ge(s_xam, at(q, 1, 0))
                        v.tensor_copy(XAH[:, :], xam).then_inc(s_xah, 1)
                        dve.wait_ge(s_xah, at(q, 1, 0))
                        low(XAL[:, :], xam, XAH[:, :]).then_inc(s_xal, 1)
                        dve.wait_ge(s_l3, at(q, 1, 0))
                        dve.wait_ge(s_x3, at(q, 2, 1))
                        wait(dve, s_ost, 16 * q)
                        v.tensor_tensor(XO[:, :], bank[6][:, :], XB3[:, :], ALU.add).then_inc(s_xo, 1)

                bodies(dve, body)

            @block.tensor
            def _(pe):
                mm = nc.tensor.matmul
                wo_h, wo_l, w3_h, w3_l = late(wlh, "wo"), late(wll, "wo"), late(wlh, "w3"), late(wll, "w3")
                a_h, a_l, b_h, b_l = late(wlh, "a"), late(wll, "a"), late(wlh, "b"), late(wll, "b")

                def turn_x(tile, s_done):
                    for k in range(KC):
                        last = nc.tensor.transpose(bank[4][:, k * P:(k + 1) * P], tile[:, k * P:(k + 1) * P],
                                                   ident[:, :])
                    last.then_inc(s_done, 1)

                def keys(pr, b, gp):
                    k = 2 * pr.par + b
                    if gp == 0:
                        pe.wait_ge(s_new[k], at(pr.i, 16 * NCH, 16 * NCH - 1))
                    for c in range(NCH):
                        last = nc.tensor.transpose(bank[4][:, c * CH:(c + 1) * CH],
                                                   KV[k][:, c, gp * P:(gp + 1) * P], ident[0:CH, 0:CH])
                    last.then_inc(s_ktp, 1)

                def scores(pr, u):
                    p, b, g = pr.n, u // 4, u % 4
                    gp, g2 = g // 2, g % 2
                    rows = slice(g2 * HD, (g2 + 1) * HD)
                    if u == 0:
                        pe.wait_ge(s_qin[pr.par], at(pr.i, 16, 15))
                    if g2 == 0:
                        pe.wait_ge(s_kt, at(p, 4, 2 * b + gp))
                    wait(pe, s_mx, p * 8 + u - 1)
                    mm(bank[u % 2][:, 0:SPAN],
                       QB[pr.par][rows, b, 2 * gp:2 * gp + 2, :].rearrange("p c t -> p (c t)"),
                       KT[b][rows, gp, :], start=True, stop=True).then_inc(s_s, 1)

                def turn(p, u):
                    pe.wait_ge(s_e, at(p, 8, u))
                    wait(pe, s_pt[u % 2], p * 4 + u // 2)
                    for c in range(NCH):
                        last = nc.tensor.transpose(bank[2 + u % 2][0:CH, c * P:(c + 1) * P],
                                                   PR[u % 2][:, c * CH:(c + 1) * CH], ident[:, :])
                    last.then_inc(s_ptp, 1)

                def values(pr, u):
                    p, b, g = pr.n, u // 4, u % 4
                    pe.wait_ge(s_pt[u % 2], at(p, 4, u // 2))
                    if g == 0:
                        wait(pe, s_on, 2 * p + b)
                    for c in range(NCH):
                        last = mm(bank[5][:, g * HD:(g + 1) * HD], PT[u % 2][:, c, :],
                                  KV[2 * pr.par + b][:, c, (G + g) * HD:(G + g + 1) * HD],
                                  start=(c == 0), stop=(c == NCH - 1))
                    last.then_inc(s_pv, 1)

                def heads(p, b):
                    pe.wait_ge(s_on, at(p, 2, b))
                    for gp in range(GP):
                        last = nc.tensor.transpose(bank[4][:, gp * P:(gp + 1) * P],
                                                   ON[b][:, 2 * gp:2 * gp + 2, :].rearrange("p g d -> p (g d)"),
                                                   ident[:, :])
                    last.then_inc(s_otp, 1)

                def output(q):
                    pe.wait_ge(s_ot, at(q, 2, 1))
                    wait(pe, s_xo, q)
                    tok = [x[:, :, :, :].rearrange("p c b t -> p c (b t)") for x in (OTH, OTL)]
                    exact_products(mm, bank[6][:, :], [(tok[0][:, c, :], tok[1][:, c, :], wo_h[:, c, :], wo_l[:, c, :])
                                                       for c in range(KC)], True, True).then_inc(s_o, 1)

                def bias(q, b):
                    pe.wait_ge(s_oh, at(q, 2, 1))
                    if b == 0:
                        wait(pe, s_x3, 2 * q)
                    else:
                        pe.wait_ge(s_x2, at(q, 1, 0))
                    mm(L2BANK[b][:, :], OHS[:, b, :], bparts[:, :], start=True, stop=False)

                def expert(q, b):
                    bias(q, b)
                    pe.wait_ge(s_xt2, at(q, 1, 0))
                    pe.wait_ge(s_w2l[b], at(q, 1, 0))
                    for k in range(KC):
                        for i, w in enumerate((W2H[b], W2L[b])):
                            last = mm(L2BANK[b][:, :], XT2[:, k, b, :, :].rearrange("p h t -> p (h t)"),
                                      w[:, k * D:(k + 1) * D], start=False, stop=(k == KC - 1 and i == 1))
                    last.then_inc(s_l2, 1)

                def body(pr, attention, dense):
                    p, q = pr.n, pr.n - 1
                    more = attention and not last_pair(pr)
                    if attention:
                        scores(pr, 0)
                        scores(pr, 1)
                    if dense:
                        if attention:
                            pe.wait_ge(s_kt, at(p, 4, 1))
                        heads(q, 1)
                    if attention:
                        turn(p, 0)
                    if dense:
                        output(q)
                    if attention:
                        scores(pr, 2)
                        turn(p, 1)
                        values(pr, 0)
                        if not dense:
                            pe.wait_ge(s_kt, at(p, 4, 1))
                        keys(pr, 1, 0)
                        scores(pr, 3)
                        turn(p, 2)
                        values(pr, 1)
                    if dense:
                        pe.wait_ge(s_x2, at(q, 1, 0))
                        if attention:
                            pe.wait_ge(s_kt, at(p, 4, 2))
                        turn_x(XB2, s_x2p)
                    if attention:
                        if dense:
                            pe.wait_ge(s_xt2, at(q, 1, 0))
                        else:
                            pe.wait_ge(s_kt, at(p, 4, 2))
                        keys(pr, 1, 1)
                        scores(pr, 4)
                        turn(p, 3)
                        values(pr, 2)
                    if dense:
                        expert(q, 0)
                    if attention:
                        scores(pr, 5)
                        turn(p, 4)
                        values(pr, 3)
                    if dense:
                        expert(q, 1)
                    if attention:
                        scores(pr, 6)
                        turn(p, 5)
                        values(pr, 4)
                    if dense:
                        pe.wait_ge(s_x3, at(q, 2, 1))
                        if attention:
                            pe.wait_ge(s_kt, at(p, 4, 3))
                        turn_x(XB3, s_x3p)
                        pe.wait_ge(s_xt3, at(q, 1, 0))
                    if attention:
                        if not dense:
                            pe.wait_ge(s_kt, at(p, 4, 3))
                        heads(p, 0)
                        scores(pr, 7)
                        turn(p, 6)
                        values(pr, 5)
                    if dense:
                        if attention:
                            pe.wait_ge(s_ot, at(p, 2, 0))
                        x3t = [(XTH3[:, k, :], XTL3[:, k, :]) for k in range(KC)]
                        exact_products(mm, bank[4][:, 0:P], [(a_h[:, k, :], a_l[:, k, :], *x3t[k]) for k in range(KC)],
                                       True, True).then_inc(s_xa, 1)
                        exact_products(mm, bank[6][:, :], [(*x3t[k], w3_h[:, k, :], w3_l[:, k, :]) for k in range(KC)],
                                       True, False)
                    if attention:
                        turn(p, 7)
                        values(pr, 6)
                    if more:
                        pe.wait_ge(s_xam, at(q, 1, 0)) if dense else pe.wait_ge(s_ot, at(p, 2, 0))
                        keys(pr.move(1), 0, 0)
                    if dense:
                        pe.wait_ge(s_xal, at(q, 1, 0))
                        exact_products(mm, bank[6][:, :], [(XAH[:, :], XAL[:, :], b_h[:, 0, :], b_l[:, 0, :])],
                                       False, True).then_inc(s_l3, 1)
                    if more:
                        pe.wait_ge(s_kt, at(pr.move(1).n, 4, 0))
                        keys(pr.move(1), 0, 1)
                    if attention:
                        values(pr, 7)

                keys(Pair(0, 0), 0, 0)
                pe.wait_ge(s_kt, 1)
                keys(Pair(0, 0), 0, 1)
                bodies(pe, body)


def kernel(**inputs):
    import numpy as np
    import concourse.bacc as bacc
    from concourse.bass_utils import run_bass_kernel_spmd

    a = {k: np.asarray(v) for k, v in inputs.items()}
    cond, tab, kv = a["itok_B_1_198"], a["itok_Bx257_0_4111"], a["itok_B_37_3939"]
    ident, adapter = a["itok_B_0_15"], a["itok_B_0_6"]
    order = [4 * gp + 2 * g2 + j for gp in range(GP) for j in range(2) for g2 in range(2)]
    wq = a["L1_cond_Wq"].reshape(H, HD, D)[order].reshape(H * HD, D)
    wo = a["L1_cond_Wo"].reshape(D, H, HD)[:, order].reshape(D, H * HD)

    def rows(pool):
        return pool.transpose(0, 2, 1, 3).reshape(NPOOL * BLOCK, G * HD)

    half = HD // 2
    arrays = {
        "x": a["x"].reshape(NB * T, D),
        "w0": a["L0_cond_weights"].reshape(S0 * T, T),
        "cond2": cond.reshape(PAIRS, 2).T,
        "kv2": kv.reshape(PAIRS, 2).T,
        "kv": kv,
        "tab": tab,
        "id": ident,
        "ad": adapter,
        "scal": np.repeat(a["L3_cond_scalings"], RANK).reshape(P, 1),
        "inv": (np.float32(1.0) / np.float32(10000.0) ** (np.arange(half, dtype=np.float32) / np.float32(half))),
        "qs": a["L1_cond_q_norm_scale"],
        "ks": a["L1_cond_k_norm_scale"],
        "wqkv": np.concatenate([wq, a["L1_cond_Wk"], a["L1_cond_Wv"]]).T,
        "woT": wo.T,
        "pool": np.concatenate([rows(a["L1_cond_k_blocks"]), rows(a["L1_cond_v_blocks"])], axis=1),
        "w2": a["L2_cond_W"].reshape(E, KC, P, D).transpose(0, 2, 1, 3).reshape(E * P, KC * D),
        "b2": a["L2_cond_b"],
        "w3T": a["L3_cond_W"].T,
        "aT": a["L3_cond_A"].reshape(NA * RANK, D).T,
        "bT": a["L3_cond_Bm"].transpose(0, 2, 1).reshape(NA * RANK, D),
    }
    arrays = {k: np.ascontiguousarray(v) for k, v in arrays.items()}
    nc = bacc.Bacc("TRN2", target_bir_lowering=False, num_devices=1)
    t = {k: nc.dram_tensor(f"in_{k}", v.shape, mybir.dt.from_np(v.dtype), kind="ExternalInput").ap()
         for k, v in arrays.items()}
    out = nc.dram_tensor("out_dram", (NB * T, D), F32, kind="ExternalOutput").ap()
    build(nc, t, out)
    r = run_bass_kernel_spmd(nc, [{f"in_{k}": v for k, v in arrays.items()}], core_ids=[0])
    return r.results[0]["out_dram"].reshape(NB, T, D)
```

```python
from contextlib import ExitStack

import concourse.bass as bass
from concourse import mybir

F32 = mybir.dt.float32
I32 = mybir.dt.int32
F32R = mybir.dt.float32r
ALU = mybir.AluOpType
ACT = mybir.ActivationFunctionType
AXX = mybir.AxisListType.X

NB, T, D = 64, 64, 512
PAIRS = NB // 2
P = 128
KC = D // P
H, G, HD = 8, 4, 64
GP = G // 2
BLOCK, NBLK, NPOOL = 16, 257, 4112
WINDOW = 256
SCALE = 256.0 ** -0.5
EPS = 1e-6
SLOTS = 21
SPAN = SLOTS * BLOCK
CH = SPAN // 3
NCH = 3
WSLOTS = 5
NW = NB * WSLOTS
SLOT_MAX = NBLK - SLOTS
A_MAX = (NBLK * BLOCK - T) - BLOCK * SLOT_MAX
MASKW = SPAN + A_MAX
BIG = float(1 << 17)
NEG = -1e30
KVW = 2 * G * HD
E, NA, RANK, S0 = 16, 8, 16, 200
BD_CLEARED = 10
N_CONST = 18
PI = 3.141592653589793
C1, C2 = 6.28125, 0.0019353071795864769
MAGIC = 12582912.0


class Pair:

    def __init__(self, i, par):
        self.i, self.par, self.n = i, par, i * 2 + par

    def move(self, by):
        return Pair(self.i + (self.par + by) // 2, (self.par + by) % 2)


def at(tile, per_tile, i):
    return tile * per_tile + (i + 1)


def wait(eng, sem, value):
    if isinstance(value, int) and value <= 0:
        return
    eng.wait_ge(sem, value)


def wait_all(eng, passed, *pairs):
    for sem, value in pairs:
        wait(eng, sem, value)
    eng.sem_inc(passed, 1)


def exact_products(mm, out, pairs, start, stop):
    todo = [(l, r) for lh, ll, rh, rl in pairs for l, r in ((lh, rh), (lh, rl), (ll, rh))]
    for i, (l, r) in enumerate(todo):
        last = mm(out, l, r, start=start and i == 0, stop=stop and i == len(todo) - 1)
    return last


def build(nc, t, out):
    ctx = ExitStack()
    with ctx:
        def sb(name, shape, dt=F32):
            return ctx.enter_context(nc.sbuf_tensor(name, shape, dt))

        def sem(name):
            return ctx.enter_context(nc.semaphore(name))

        bank = [ctx.enter_context(nc.psum_tensor(f"bank{i}", [P, 512], F32)) for i in range(8)]

        x1_d = nc.dram_tensor("x1_scratch", [PAIRS, P, D], F32).ap()
        qt_d = nc.dram_tensor("qt_scratch", [PAIRS, P, D], F32).ap()
        kv_d = nc.dram_tensor("kv_scratch", [NB * T, KVW], F32).ap()
        tab_d = nc.dram_tensor("tab_scratch", [NB, SLOTS], F32).ap()
        tabw_d = nc.dram_tensor("tabw_scratch", [NB, WSLOTS], F32).ap()

        x_v = t["x"].rearrange("(n p) f -> n p f", p=P)
        kvd_v = kv_d.rearrange("(n p) f -> n p f", p=P)
        out_v = out.rearrange("(n p) f -> n p f", p=P)
        w0_v = t["w0"].rearrange("(s c) d -> s c d", c=T)
        w2_v = t["w2"].rearrange("(e p) f -> e p f", p=P)

        ident = sb("ident", [P, P])
        mask = sb("mask", [P, MASKW])
        pm = sb("pm", [P, 1], I32)
        pmf = sb("pmf", [P, 1])
        idxT = sb("idxT", [CH, 2 * NCH, NB], I32)
        moff = sb("moff", [1, NB], I32)
        eid = sb("eid", [1, NB], I32)
        onehot = sb("onehot", [2 * 32, NB])
        adapt = sb("adapt", [P, NB])
        NWL = KC * D * 2 + KC * P + D
        wlh = sb("wlh", [P, NWL], F32R)
        wll = sb("wll", [P, NWL], F32R)

        def late(tile, which):
            a, n = {"wo": (0, D), "w3": (KC * D, D), "a": (2 * KC * D, P), "b": (2 * KC * D + KC * P, D)}[which]
            k = 1 if which == "b" else KC
            return tile[:, a:a + k * n].rearrange("p (k n) -> p k n", k=k)

        bparts = sb("bparts", [2 * 32, D], F32R)

        s_const = sem("const_ready")
        s_small = sem("small_in")
        s_pass_pool = sem("pool_passed")
        s_pass_dve = sem("dve_passed")
        s_prep = sem("prep_step")
        s_wqkv = [sem(f"wqkv_in{k}") for k in range(KC)]
        s_wlate = sem("late_weights_in")
        s_tabout = sem("tables_out")
        s_tabin = sem("tables_back")
        s_cnt = sem("counts_ready")
        s_lw = sem("writers_ready")
        s_idxT = sem("indices_turned")
        s_idx = sem("indices_ready")
        s_arg = sem("angles_ready")
        s_sin = sem("sines_ready")
        s_cond = sem("cond_in")
        s_ve = sem("values_out_of_psum")
        s_wqh = sem("wqkv_high")
        s_wq = sem("wqkv_split")
        s_wlh = sem("late_high")
        s_wl = sem("late_split")
        s_xth = sem("x1t_high")
        s_sum = sem("rotation_summed")
        s_rsum = sem("rotation_half")
        s_ri = sem("norm_ready")

        s_xin = sem("x_in")
        s_bd = sem("w0_block_ready")
        s_l0 = sem("l0_done")
        s_x1 = sem("x1_ready")
        s_xtp = sem("x1_turned")
        s_xt = sem("x1t_ready")
        s_qps = sem("q_done")
        s_kvps = sem("kv_done")
        s_qe = sem("q_copied")
        s_kve = sem("kv_copied")
        s_var = sem("variance_ready")
        s_sd = sem("deviation_ready")
        s_rope = sem("rope_step")
        s_qr = sem("rotated_ready")
        s_qtp = sem("q_turned")
        s_qt = sem("qt_ready")
        s_x1o = sem("x1_out")
        s_qto = sem("qt_out")
        s_kvo = sem("kv_out")

        pa = ExitStack()
        with pa:
            def sa(name, shape, dt=F32):
                return pa.enter_context(nc.sbuf_tensor(name, shape, dt))

            wlr = sa("wlr", [P, NWL])
            wqkv = wlr[:, 0:KC * 1024].rearrange("p (k n) -> p k n", k=KC)
            wqh = sa("wqh", [P, KC, 1024], F32R)
            wql = sa("wql", [P, KC, 1024], F32R)
            b2r = sa("b2r", [2 * 32, D])
            bd = sa("bd", [P, P])
            X = sa("X", [P, D])
            X1 = sa("X1", [P, D])
            XTH = sa("XTH", [P, KC, P], F32R)
            XTL = sa("XTL", [P, KC, P], F32R)
            QK = sa("QK", [P, H + G, HD])
            SQ = sa("SQ", [P, H + G, HD])
            RT = sa("RT", [P, H + G, HD])
            SW = sa("SW", [P, H + G, HD])
            KVR = sa("KVR", [P, KVW])
            QR = sa("QR", [P, H, HD])
            QT = sa("QT", [P, 2, KC, T])
            ss = sa("ss", [P, H + G])
            var = sa("var", [P, H + G])
            sd = sa("sd", [P, H + G])
            ri = sa("ri", [P, H + G])
            tab1 = sa("tab1", [P, 2, PAIRS, HD])
            tab2 = sa("tab2", [P, 2, PAIRS, HD])
            inv = sa("inv", [P, HD // 2])
            nsc = sa("nsc", [P, 2, HD])
            nscn = sa("nscn", [P, 2, HD])
            kvb = sa("kvb", [P, PAIRS], I32)
            cond = sa("cond", [1, NB], I32)
            pos = sa("pos", [P, PAIRS])
            trig = sa("trig", [P, 5, PAIRS, HD // 2])
            ang, tr, trk = trig[:, 0], trig[:, 1:3], trig[:, 3:5]
            kvi = sa("kvi", [NB, 1], I32)
            kvf = sa("kvf", [NB, 1])
            ti = sa("ti", [NB, 1], I32)
            si = sa("si", [NB, 1], I32)
            slot0 = sa("slot0", [NB, 1])
            slotw = sa("slotw", [NB, 1])
            rw = sa("rw", [NB, 1])
            kri = sa("kri", [1, NB], I32)
            krf = sa("krf", [1, NB])
            kr2 = sa("kr2", [1, NB], I32)
            kr3 = sa("kr3", [1, NB])
            i257 = sa("i257", [NB, NW], I32)
            f257 = sa("f257", [NB, NW])
            i80i = sa("i80i", [NB, WSLOTS * BLOCK], I32)
            u80 = sa("u80", [NB, WSLOTS * BLOCK])
            v80 = sa("v80", [NB, WSLOTS * BLOCK])
            c80 = sa("c80", [NB, WSLOTS, BLOCK])
            uc = sa("uc", [NB, WSLOTS, BLOCK])
            bco = sa("bco", [NB, 1], I32)
            bcf = sa("bcf", [NB, 1])
            mxi = sa("mxi", [NB, WSLOTS], I32)
            mxf = sa("mxf", [NB, WSLOTS])
            sl21 = sa("sl21", [NB, SLOTS])
            sl5 = sa("sl5", [NB, WSLOTS])
            tabi = sa("tabi", [NB, NBLK], I32)
            tabf = sa("tabf", [NB, NBLK])
            tab21 = sa("tab21", [NB, SLOTS])
            tab5 = sa("tab5", [NB, WSLOTS])
            twb = sa("twb", [NB, NW])
            trb = sa("trb", [NB, NB, SLOTS])
            flat = trig[0:NB, :, :, :].rearrange("p a b c -> p (a b c)")
            MR = NB * SLOTS
            mr = [flat[:, i * MR:(i + 1) * MR] for i in range(3)] + [wlr[0:NB, i * MR:(i + 1) * MR] for i in range(2)]
            later = wlr[0:NB, 2 * MR:2 * MR + WSLOTS * NW].rearrange("p (a b) -> p a b", a=WSLOTS)
            LATER_END = 2 * MR + WSLOTS * NW
            junk = wlr[0:NB, LATER_END:LATER_END + NBLK]
            ew = wlr[0:NB, LATER_END + NBLK:LATER_END + NBLK + NW]
            has, oldi, newi = (flat[:, 3 * MR + i * SPAN:3 * MR + (i + 1) * SPAN] for i in range(3))
            phys = sa("phys", [NB, SLOTS, BLOCK])
            idi = sa("idi", [2 * 32, NB], I32)
            idf = sa("idf", [2 * 32, NB])
            pe16i = sa("pe16i", [2 * 32, 1], I32)
            pe16 = sa("pe16", [2 * 32, 1])
            adi = sa("adi", [P, NB], I32)
            adf = sa("adf", [P, NB])
            pni = sa("pni", [P, 1], I32)
            pns = sa("pns", [P, 1], I32)
            pnf = sa("pnf", [P, 1])
            scal = sa("scal", [P, 1])

            N_SMALL = 11
            block = pa.enter_context(nc.Block())

            def bodies(eng, body, between={}):
                cuts = sorted({1, PAIRS - 3, PAIRS - 2, PAIRS - 1, PAIRS} | set(between))
                begin = 0
                for cut in cuts:
                    if cut + 1 - begin <= 2:
                        for p in range(begin, cut + 1):
                            body(p)
                    else:
                        with eng.Fori(begin, cut + 1) as p:
                            body(p)
                    begin = cut + 1
                    if cut in between:
                        between[cut]()

            def has_pair(q):
                return not isinstance(q, int) or 0 <= q < PAIRS

            PREP = {}

            @block.vector
            def _(dve):
                n = [0]

                def step(ins, name=None):
                    n[0] += 1
                    ins.then_inc(s_prep, 1)
                    if name:
                        PREP[name] = n[0]
                    dve.wait_ge(s_prep, n[0])

                v = nc.vector
                dve.wait_ge(s_const, 2)
                step(v.tensor_copy(pmf[:, :], pm[:, :]))
                dve.wait_ge(s_small, 16 * N_SMALL)
                step(v.tensor_scalar(pos[:, :], kvb[:, :], pmf[:, 0:1], None, ALU.add))
                step(v.tensor_tensor(ang[:, :, :], pos[:, :].unsqueeze(2).to_broadcast([P, PAIRS, HD // 2]),
                                     inv[:, :].unsqueeze(1).to_broadcast([P, PAIRS, HD // 2]), ALU.mult))
                both = (0, 0.0), (1, 0.25)

                def each(ins_of):
                    for k, turn in both:
                        n[0] += 1
                        ins_of(k, turn).then_inc(s_prep, 1)
                    dve.wait_ge(s_prep, n[0])

                each(lambda k, turn: v.tensor_scalar(trk[:, k], ang[:, :, :], 1.0 / (2 * PI), turn, ALU.mult, ALU.add))
                each(lambda k, turn: v.tensor_scalar(trk[:, k], trk[:, k], MAGIC, MAGIC, ALU.add, ALU.subtract))
                each(lambda k, turn: v.scalar_tensor_tensor(tr[:, k], trk[:, k], -C1, ang[:, :, :], ALU.mult, ALU.add))
                each(lambda k, turn: v.scalar_tensor_tensor(tr[:, k], trk[:, k], -C2, tr[:, k], ALU.mult, ALU.add))
                each(lambda k, turn: v.tensor_scalar(tr[:, k], tr[:, k], turn * 2 * PI, 3.1415925, ALU.add, ALU.min))
                each(lambda k, turn: v.tensor_scalar(tr[:, k], tr[:, k], -3.1415925, None, ALU.max))
                v.tensor_scalar(nsc[:, :, :], nsc[:, :, :], 1.0, None, ALU.add).then_inc(s_arg, 1)
                dve.wait_ge(s_arg, 1)
                step(v.tensor_scalar(nscn[:, :, :], nsc[:, :, :], -1.0, None, ALU.mult))

                def tables(a, b):
                    hh = HD // 2
                    for q in range(2):
                        def w(tile, c):
                            return tile[:, q, c:c + hh].unsqueeze(1).to_broadcast([P, b - a, hh])
                        v.tensor_tensor(tab1[:, q, a:b, 0:hh], trk[:, 1, a:b], w(nsc, 0), ALU.mult)
                        v.tensor_tensor(tab1[:, q, a:b, hh:HD], trk[:, 1, a:b], w(nsc, hh), ALU.mult)
                        v.tensor_tensor(tab2[:, q, a:b, 0:hh], trk[:, 0, a:b], w(nsc, 0), ALU.mult)
                        step(v.tensor_tensor(tab2[:, q, a:b, hh:HD], trk[:, 0, a:b], w(nscn, hh), ALU.mult))

                def indices():
                    dve.wait_ge(s_wq, KC)
                    for i_, f_, j_, g_ in ((kvi, kvf, ti, slot0), (kri, krf, kr2, kr3)):
                        step(v.tensor_copy(f_[:, :], i_[:, :]))
                        yield
                        step(v.tensor_scalar(j_[:, :], f_[:, :], float(1 - WINDOW), 0.0, ALU.add, ALU.max))
                        yield
                        step(v.tensor_scalar(j_[:, :], j_[:, :], 4, None, ALU.arith_shift_right))
                        yield
                        step(v.tensor_scalar(g_[:, :], j_[:, :], float(SLOT_MAX), None, ALU.min))
                        yield
                    step(v.tensor_scalar(si[:, :], kvi[:, :], 4, None, ALU.arith_shift_right))
                    yield
                    step(v.tensor_copy(slotw[:, :], si[:, :]))
                    yield
                    step(v.scalar_tensor_tensor(rw[:, :], slotw[:, :], -float(BLOCK), kvf[:, :], ALU.mult, ALU.add))
                    yield
                    step(v.scalar_tensor_tensor(krf[:, :], kr3[:, :], float(BLOCK), krf[:, :], ALU.mult, ALU.subtract))
                    yield
                    step(v.tensor_scalar(moff[:, :], krf[:, :], float(A_MAX), None, ALU.add))
                    yield
                    step(v.tensor_copy(f257[:, :], i257[:, :]))
                    yield
                    step(v.tensor_copy(tabf[:, :], tabi[:, :]))
                    yield
                    step(v.tensor_scalar(sl21[:, :], f257[:, 0:SLOTS], slot0[:, 0:1], None, ALU.add))
                    yield
                    step(v.tensor_scalar(sl5[:, :], f257[:, 0:WSLOTS], slotw[:, 0:1], None, ALU.add))
                    yield
                    for dst, sl, m in ((tab21, sl21, SLOTS), (tab5, sl5, WSLOTS)):
                        for i in range(m):
                            step(v.scalar_tensor_tensor(junk[:, :], f257[:, 0:NBLK], sl[:, i:i + 1], tabf[:, :],
                                                        ALU.is_equal, ALU.mult, accum_out=dst[:, i:i + 1]),
                                 "tables")
                            yield
                    step(v.tensor_copy(u80[:, :], i80i[:, :]))
                    yield
                    step(v.tensor_scalar(u80[:, :], u80[:, :], rw[:, 0:1], None, ALU.subtract))
                    yield
                    step(v.tensor_scalar(v80[:, :], u80[:, :], 0.0, None, ALU.is_ge))
                    yield
                    step(v.scalar_tensor_tensor(v80[:, :], u80[:, :], float(T), v80[:, :], ALU.is_lt, ALU.mult))
                    yield
                    step(v.tensor_copy(bcf[:, :], bco[:, :]))
                    yield
                    step(v.tensor_copy(mxf[:, :], mxi[:, :]))
                    yield
                    step(v.scalar_tensor_tensor(c80[:, :, :].rearrange("p a b -> p (a b)"), u80[:, :], bcf[:, 0:1],
                                                v80[:, :], ALU.add, ALU.mult))
                    yield
                    dve.wait_ge(s_tabin, 32)
                    for i in range(WSLOTS):
                        step(v.tensor_scalar(ew[:, :], twb[:, :], tab5[:, i:i + 1], None, ALU.is_equal))
                        yield
                        step(v.scalar_tensor_tensor(later[:, i, :], f257[:, :], mxf[:, i:i + 1], ew[:, :],
                                                    ALU.is_lt, ALU.mult), "later")
                        yield
                    for i in range(WSLOTS):
                        step(v.tensor_scalar(mr[i], trb[:, :, :].rearrange("p b s -> p (b s)"),
                                             tab5[:, i:i + 1], None, ALU.is_equal))
                        yield
                    dve.wait_ge(s_cnt, 1)
                    step(v.scalar_tensor_tensor(uc[:, :, :].rearrange("p a b -> p (a b)"),
                                                bank[5][0:NB, 0:WSLOTS * BLOCK], 0.0,
                                                c80[:, :, :].rearrange("p a b -> p (a b)"),
                                                ALU.is_equal, ALU.mult), "uc")
                    yield
                    io = f257[:, 0:BLOCK].unsqueeze(1).to_broadcast([NB, SLOTS, BLOCK])
                    step(v.scalar_tensor_tensor(phys[:, :, :], tab21[:, :].unsqueeze(2).to_broadcast([NB, SLOTS, BLOCK]),
                                                float(BLOCK), io, ALU.mult, ALU.add))
                    yield
                    dve.wait_ge(s_lw, 1)
                    lw = bank[6][0:NB, 0:SPAN]
                    step(v.tensor_scalar(has[:, :], lw, 0.0, BIG, ALU.is_gt, ALU.mult))
                    yield
                    step(v.tensor_tensor(oldi[:, :], has[:, :], phys[:, :, :].rearrange("p a b -> p (a b)"), ALU.add))
                    yield
                    step(v.tensor_scalar(has[:, :], lw, 0.0, BIG, ALU.is_equal, ALU.mult))
                    yield
                    step(v.scalar_tensor_tensor(newi[:, :], lw, -1.0, has[:, :], ALU.add, ALU.add), "idx")
                    yield
                    dve.wait_ge(s_idxT, 1)
                    v.tensor_copy(idxT[:, :, :].rearrange("p a b -> p (a b)"),
                                  bank[7][0:CH, 0:2 * NCH * NB]).then_inc(s_idx, 1)
                    step(v.tensor_copy(pe16[:, :], pe16i[:, :]))
                    yield
                    step(v.tensor_copy(idf[:, :], idi[:, :]))
                    yield
                    step(v.tensor_scalar(onehot[:, :], idf[:, :], pe16[:, 0:1], None, ALU.is_equal))
                    yield
                    step(v.tensor_scalar(pns[:, :], pni[:, :], 4, None, ALU.arith_shift_right))
                    yield
                    step(v.tensor_copy(pnf[:, :], pns[:, :]))
                    yield
                    step(v.tensor_copy(adf[:, :], adi[:, :]))
                    yield
                    step(v.tensor_scalar(adapt[:, :], adf[:, :], pnf[:, 0:1], scal[:, 0:1], ALU.is_equal, ALU.mult))
                    yield

                def first(q):
                    dve.wait_ge(s_xin, at(q, 16, 15))
                    dve.wait_ge(s_l0, at(q, 1, 0))
                    wait(dve, s_x1o, 16 * q)
                    wait(dve, s_xtp, q)
                    v.tensor_tensor(X1[:, :], bank[0][:, :], X[:, :], ALU.add).then_inc(s_x1, 1)

                def turned(q):
                    dve.wait_ge(s_xth, at(q, 1, 0))
                    v.tensor_tensor(XTL[:, :, :].rearrange("p a b -> p (a b)"), bank[1][:, :],
                                    XTH[:, :, :].rearrange("p a b -> p (a b)").bitcast(F32),
                                    ALU.subtract).then_inc(s_xt, 1)

                R = 5

                def rotated(p, a, b, q, which):
                    dst, tab = ((RT, tab1), (SW, tab2))[which - 1]
                    v.tensor_tensor(dst[:, a:b, :], QK[:, a:b, :],
                                    tab[:, q, bass.ds(p, 1), :].to_broadcast([P, b - a, HD]),
                                    ALU.mult).then_inc(s_rope, 1)

                def body(p):
                    if has_pair(p):
                        dve.wait_ge(s_qe, at(p, 1, 0))
                        wait(dve, s_sum, p)
                        rotated(p, 0, H, 0, 2)
                        wait(dve, s_qr, p)
                        rotated(p, 0, H, 0, 1)
                    if has_pair(p + 1):
                        turned(p + 1)
                    if not has_pair(p):
                        return
                    dve.wait_ge(s_kve, at(p, 1, 0))
                    rotated(p, H, H + G, 1, 1)
                    rotated(p, H, H + G, 1, 2)
                    v.tensor_reduce(ss[:, :], SQ[:, :, :], AXX, ALU.add).then_inc(s_rope, 1)
                    dve.wait_ge(s_rope, at(p, R, R - 1))
                    v.tensor_scalar(var[:, :], ss[:, :], 1.0 / HD, EPS, ALU.mult, ALU.add).then_inc(s_var, 1)
                    if has_pair(p + 2):
                        first(p + 2)
                    dve.wait_ge(s_sd, at(p, 1, 0))
                    v.reciprocal(ri[:, :], sd[:, :]).then_inc(s_ri, 1)

                def split(high, low, raw):
                    return v.tensor_tensor(low, raw, high.bitcast(F32), ALU.subtract)

                first(0)
                for k in range(KC):
                    dve.wait_ge(s_wqh, k + 1)
                    split(wqh[:, k, :], wql[:, k, :], wqkv[:, k, :]).then_inc(s_wq, 1)
                turned(0)
                first(1)
                dve.wait_ge(s_sin, 1)
                tables(0, 8)
                work = indices()

                def go_on(n_steps):
                    def run():
                        for _ in range(n_steps):
                            next(work)
                    return run

                def late_low(i):
                    def run():
                        dve.wait_ge(s_wlh, i + 1)
                        part = slice(i * 1024, (i + 1) * 1024)
                        split(wlh[:, part], wll[:, part], wlr[:, part]).then_inc(s_wl, 1)
                        if i == 4:
                            dve.wait_ge(s_wlh, 6)
                            low = slice(32, 32 + E)
                            split(bparts[low, :], bparts[low, :], b2r[low, :]).then_inc(s_wl, 1)
                    return run

                between = {1: lambda: tables(8, 16), 3: lambda: tables(16, 24), 5: lambda: tables(24, 32)}
                between.update({p: go_on(8) for p in (6, 7, 8, 9, 10)} | {11: go_on(3), 14: go_on(7)})
                between.update({p: go_on(5) for p in (16, 17, 18)})
                between.update({20: go_on(2), 24: go_on(4), 28: go_on(7)})
                between.update({p: late_low(i) for i, p in enumerate((27, 29, 30, 31, 32))})
                bodies(dve, body, between)
                assert next(work, "end") == "end"

            @block.sync
            def _(sp):
                sp.dma_start(cond[:, :], t["cond"].rearrange("(o b) -> o b", o=1)).then_inc(s_cond, 16)
                sp.dma_start(X[:, :], x_v[0]).then_inc(s_xin, 16)
                for dst, src in (
                    (kvb[0:T, :], t["kv2"][0, :].partition_broadcast(T)),
                    (kvb[T:P, :], t["kv2"][1, :].partition_broadcast(T)),
                    (inv[:, :], t["inv"].partition_broadcast(P)),
                    (nsc[:, 0, :], t["qs"].partition_broadcast(P)),
                    (nsc[:, 1, :], t["ks"].partition_broadcast(P)),
                    (kvi[:, :], t["kv"].rearrange("(b o) -> b o", o=1)),
                    (kri[:, :], t["kv"].rearrange("(o b) -> o b", o=1)),
                    (tabi[:, :], t["tab"]),
                    (idi[:, :], t["id"].partition_broadcast(2 * 32)),
                    (adi[:, :], t["ad"].partition_broadcast(P)),
                    (scal[:, :], t["scal"]),
                ):
                    sp.dma_start(dst, src).then_inc(s_small, 16)

                def blocks(q):
                    numbers = [sp.value_load(cond[0:1, bass.ds(q * 2 + half, 1)], min_val=0, max_val=S0 - 1)
                               for half in range(2)]
                    wait(sp, s_l0, q)
                    for half, number in enumerate(numbers):
                        part = slice(half * T, (half + 1) * T)
                        sp.dma_start(bd[part, part], w0_v[bass.ds(number, 1)]).then_inc(s_bd, 16)

                sp.wait_ge(s_cond, 16)
                sp.wait_ge(s_const, BD_CLEARED)
                blocks(0)
                for k in range(KC):
                    sp.dma_start(wqkv[:, k, :], t["wqkv"][k * P:(k + 1) * P, :]).then_inc(s_wqkv[k], 16)
                sp.dma_start(eid[:, :], t["id"].rearrange("(o b) -> o b", o=1)).then_inc(s_wlate, 16)
                sp.wait_ge(s_x1, 1)
                sp.dma_start(X[:, :], x_v[1]).then_inc(s_xin, 16)
                sp.dma_start(x1_d[0], X1[:, :]).then_inc(s_x1o, 16)
                blocks(1)

                def store_qt(q):
                    sp.wait_ge(s_qt, at(q, 1, 0))
                    sp.dma_start(qt_d[bass.ds(q, 1)], QT[:, :, :, :].rearrange("p b c t -> p (b c t)")
                                 ).then_inc(s_qto, 16)

                def body(p):
                    if has_pair(p + 2):
                        blocks(p + 2)
                    if has_pair(p + 1):
                        sp.wait_ge(s_x1, at(p + 1, 1, 0))
                        sp.dma_start(x1_d[bass.ds(p + 1, 1)], X1[:, :]).then_inc(s_x1o, 16)
                    if has_pair(p + 2):
                        sp.dma_start(X[:, :], x_v[bass.ds(p + 2, 1)]).then_inc(s_xin, 16)
                    if has_pair(p - 2):
                        store_qt(p - 2)
                    if has_pair(p - 1):
                        sp.wait_ge(s_qr, at(p - 1, 1, 0))
                        sp.wait_ge(s_ve, at(p - 1, 1, 0))
                        sp.dma_start(kvd_v[bass.ds(p - 1, 1)], KVR[:, :]).then_inc(s_kvo, 16)

                def tables_out():
                    sp.wait_ge(s_prep, PREP["tables"])
                    sp.dma_start(tab_d, tab21[:, :]).then_inc(s_tabout, 16)
                    sp.dma_start(tabw_d, tab5[:, :]).then_inc(s_tabout, 16)

                def tables_in():
                    sp.wait_ge(s_tabout, 32)
                    sp.dma_start(twb[:, :], tabw_d.rearrange("b s -> (b s)").partition_broadcast(NB)
                                 ).then_inc(s_tabin, 16)
                    sp.dma_start(trb[:, :, :].rearrange("p b s -> p (b s)"),
                                 tab_d.rearrange("b s -> (b s)").partition_broadcast(NB)).then_inc(s_tabin, 16)

                def late_weights(*loads):
                    def run():
                        sp.wait_ge(s_lw, 1)
                        for dst, src in loads:
                            sp.dma_start(dst, src).then_inc(s_wlate, 16)
                    return run

                sp.wait_ge(s_const, N_CONST)
                bodies(sp, body, {
                    13: tables_out,
                    14: tables_in,
                    23: late_weights((late(wlr, "wo"), t["woT"].rearrange("(k p) n -> p k n", p=P))),
                    24: late_weights((late(wlr, "w3"), t["w3T"].rearrange("(k p) n -> p k n", p=P))),
                    25: late_weights((late(wlr, "a"), t["aT"].rearrange("(k p) n -> p k n", p=P)),
                                     (late(wlr, "b")[:, 0, :], t["bT"]),
                                     (b2r[0:E, :], t["b2"]),
                                     (b2r[32:32 + E, :], t["b2"]))})
                store_qt(PAIRS - 1)
                sp.wait_ge(s_x1o, 16 * PAIRS)
                sp.wait_ge(s_kvo, 16 * PAIRS)
                sp.wait_ge(s_qto, 16 * PAIRS)

            @block.gpsimd
            def _(pool):
                made = [0]

                def make(ins):
                    made[0] += 1
                    ins.then_inc(s_const, 1)
                    pool.wait_ge(s_const, made[0])

                for tile, step, base, up in ((pm[0:T, :], 0, 0, 1), (pm[T:P, :], 0, 0, 1), (i257[:, :], 1, 0, 0),
                                             (i80i[:, :], 1, 0, 0), (bco[:, :], 0, 1, T), (mxi[:, :], 1, 0, WSLOTS),
                                             (pe16i[0:32, :], 0, 0, 1),
                                             (pe16i[32:64, :], 0, 0, 1), (pni[:, :], 0, 0, 1)):
                    make(nc.gpsimd.iota(tile, pattern=[[step, tile.shape[1]]], base=base, channel_multiplier=up))
                for tile in (bd, ident, mask, b2r):
                    make(nc.gpsimd.memset(tile[:, :], 0.0))
                make(nc.gpsimd.affine_select(out=ident[:, :], in_=ident[:, :], compare_op=ALU.not_equal, fill=1.0,
                                             base=0, pattern=[[-1, P]], channel_multiplier=1))
                for j in range(2):
                    m = mask[T * j:T * (j + 1), :]
                    make(nc.gpsimd.affine_select(out=m, in_=m, compare_op=ALU.is_ge, fill=NEG, base=A_MAX,
                                                 pattern=[[-1, MASKW]], channel_multiplier=1))
                    make(nc.gpsimd.affine_select(out=m, in_=m, compare_op=ALU.is_ge, fill=NEG,
                                                 base=WINDOW - 1 - A_MAX, pattern=[[1, MASKW]],
                                                 channel_multiplier=-1))
                assert made[0] == N_CONST
                def body(p):
                    if not has_pair(p):
                        return
                    hh = HD // 2
                    g = nc.gpsimd
                    pool.wait_ge(s_rope, at(p, 5, 3))
                    g.tensor_tensor(RT[:, :, 0:hh], RT[:, :, 0:hh], SW[:, :, hh:HD], ALU.add).then_inc(s_rsum, 1)
                    pool.wait_ge(s_rsum, at(p, 1, 0))
                    g.tensor_tensor(RT[:, :, hh:HD], RT[:, :, hh:HD], SW[:, :, 0:hh], ALU.add).then_inc(s_sum, 1)
                    pool.wait_ge(s_sum, at(p, 1, 0))
                    pool.wait_ge(s_ri, at(p, 1, 0))
                    wait(pool, s_qtp, p)
                    wait(pool, s_kvo, 16 * p)
                    g.tensor_tensor(QR[:, :, :], RT[:, 0:H, :], ri[:, 0:H].unsqueeze(2).to_broadcast([P, H, HD]),
                                    ALU.mult)
                    g.tensor_tensor(KVR[:, 0:G * HD].rearrange("p (g d) -> p g d", g=G), RT[:, H:H + G, :],
                                    ri[:, H:H + G].unsqueeze(2).to_broadcast([P, G, HD]),
                                    ALU.mult).then_inc(s_qr, 1)

                bodies(pool, body)

            @block.scalar
            def _(act):
                def copy(dst, src):
                    return nc.scalar.activation(dst, src, ACT.Copy)

                def turned(q):
                    act.wait_ge(s_xtp, at(q, 1, 0))
                    wait(act, s_kvps, q)
                    copy(XTH[:, :, :].rearrange("p a b -> p (a b)"), bank[1][:, :]).then_inc(s_xth, 1)

                for k in range(KC):
                    act.wait_ge(s_wqkv[k], 16)
                    copy(wqh[:, k, :], wqkv[:, k, :]).then_inc(s_wqh, 1)
                turned(0)
                act.wait_ge(s_arg, 1)
                nc.scalar.activation(trk, tr, ACT.Sin).then_inc(s_sin, 1)

                def late_high(i):
                    def run():
                        act.wait_ge(s_wlate, 16 * 7)
                        part = slice(i * 1024, (i + 1) * 1024)
                        copy(wlh[:, part], wlr[:, part]).then_inc(s_wlh, 1)
                        if i == 4:
                            copy(bparts[:, :], b2r[:, :]).then_inc(s_wlh, 1)
                    return run

                def body(p):
                    if has_pair(p):
                        act.wait_ge(s_qps, at(p, 1, 0))
                        wait(act, s_rope, 5 * p)
                        bq = bank[2][:, :].rearrange("p (h d) -> p h d", h=H)
                        copy(QK[:, 0:H, :], bq)
                        nc.scalar.activation(SQ[:, 0:H, :], bq, ACT.Square).then_inc(s_qe, 1)
                        act.wait_ge(s_kvps, at(p, 1, 0))
                        bk = bank[3][:, 0:G * HD].rearrange("p (g d) -> p g d", g=G)
                        copy(QK[:, H:H + G, :], bk)
                        nc.scalar.activation(SQ[:, H:H + G, :], bk, ACT.Square).then_inc(s_kve, 1)
                    if has_pair(p + 1):
                        turned(p + 1)
                    if has_pair(p - 1):
                        wait(act, s_qto, 16 * (p - 1))
                        act.wait_ge(s_qtp, at(p - 1, 1, 0))
                        copy(QT[:, :, :, :].rearrange("p b c t -> p c b t"),
                             bank[4][:, :].rearrange("p (c b t) -> p c b t", c=KC, b=2)).then_inc(s_qt, 1)
                    if has_pair(p):
                        act.wait_ge(s_var, at(p, 1, 0))
                        nc.scalar.activation(sd[:, :], var[:, :], ACT.Sqrt).then_inc(s_sd, 1)
                        wait(act, s_kvo, 16 * p)
                        copy(KVR[:, G * HD:KVW], bank[3][:, G * HD:KVW]).then_inc(s_ve, 1)

                bodies(act, body, {p: late_high(i) for i, p in enumerate((26, 27, 28, 29, 30))})

            @block.tensor
            def _(pe):
                mm = nc.tensor.matmul
                def counts():
                    pe.wait_ge(s_prep, PREP["later"])
                    for i2 in range(WSLOTS):
                        for i in range(WSLOTS):
                            last = mm(bank[5][0:NB, i2 * BLOCK:(i2 + 1) * BLOCK],
                                      later[:, i, :].rearrange("p (b s) -> p b s", s=WSLOTS)[:, :, i2],
                                      v80[:, i * BLOCK:(i + 1) * BLOCK], start=(i == 0), stop=(i == WSLOTS - 1))
                    last.then_inc(s_cnt, 1)

                def writers():
                    pe.wait_ge(s_prep, PREP["uc"])
                    for m in range(SLOTS):
                        for i in range(WSLOTS):
                            last = mm(bank[6][0:NB, m * BLOCK:(m + 1) * BLOCK],
                                      mr[i].rearrange("p (b s) -> p b s", s=SLOTS)[:, :, m],
                                      uc[:, i, :], start=(i == 0), stop=(i == WSLOTS - 1))
                    last.then_inc(s_lw, 1)

                def turn_indices():
                    pe.wait_ge(s_prep, PREP["idx"])
                    for k, tile in enumerate((oldi, newi)):
                        for c in range(NCH):
                            a = (k * NCH + c) * NB
                            last = nc.tensor.transpose(bank[7][0:CH, a:a + NB], tile[:, c * CH:(c + 1) * CH],
                                                       ident[0:NB, 0:NB])
                    last.then_inc(s_idxT, 1)

                def l0(q):
                    pe.wait_ge(s_xin, at(q, 16, 15))
                    pe.wait_ge(s_bd, at(q, 32, 31))
                    wait(pe, s_x1, q)
                    mm(bank[0][:, :], bd[:, :], X[:, :], start=True, stop=True).then_inc(s_l0, 1)

                def xt(q):
                    pe.wait_ge(s_x1, at(q, 1, 0))
                    wait(pe, s_xt, q)
                    for k in range(KC):
                        last = nc.tensor.transpose(bank[1][:, k * P:(k + 1) * P], X1[:, k * P:(k + 1) * P],
                                                   ident[:, :])
                    last.then_inc(s_xtp, 1)

                def body(p):
                    if has_pair(p):
                        pe.wait_ge(s_xt, at(p, 1, 0))
                        wait(pe, s_qe, p)
                        exact_products(mm, bank[2][:, :], [(XTH[:, k, :], XTL[:, k, :], wqh[:, k, 0:512],
                                                            wql[:, k, 0:512]) for k in range(KC)],
                                       True, True).then_inc(s_qps, 1)
                        wait(pe, s_ve, p)
                        exact_products(mm, bank[3][:, :], [(XTH[:, k, :], XTL[:, k, :], wqh[:, k, 512:1024],
                                                            wql[:, k, 512:1024]) for k in range(KC)],
                                       True, True).then_inc(s_kvps, 1)
                    if has_pair(p + 1):
                        xt(p + 1)
                    if has_pair(p + 2):
                        l0(p + 2)
                    if has_pair(p - 1):
                        pe.wait_ge(s_qr, at(p - 1, 1, 0))
                        wait(pe, s_qt, p - 1)
                        for c in range(KC):
                            last = nc.tensor.transpose(bank[4][:, c * P:(c + 1) * P],
                                                       QR[:, 2 * c:2 * c + 2, :].rearrange("p a b -> p (a b)"),
                                                       ident[:, :])
                        last.then_inc(s_qtp, 1)

                pe.wait_ge(s_const, N_CONST)
                l0(0)
                xt(0)
                l0(1)
                pe.wait_ge(s_wq, KC)
                bodies(pe, body, {19: counts, 22: writers, 26: turn_indices})

        pb = ExitStack()
        with pb:
            def sbt(name, shape, dt=F32):
                return pb.enter_context(nc.sbuf_tensor(name, shape, dt))

            KV = [sbt(f"KV{i}", [CH, NCH, KVW]) for i in range(4)]
            idxs = [sbt(f"idxs{i}", [CH, 2 * NCH], I32) for i in range(4)]
            FM = [sbt(f"FM{i}", [P, SPAN]) for i in range(4)]
            QB = [sbt(f"QB{i}", [P, 2, KC, T]) for i in range(2)]
            KT = [sbt(f"KT{i}", [P, GP, SPAN]) for i in range(2)]
            SM = [sbt(f"SM{i}", [P, SPAN]) for i in range(2)]
            PR = [sbt(f"PR{i}", [P, SPAN]) for i in range(2)]
            PT = [sbt(f"PT{i}", [CH, NCH, P]) for i in range(2)]
            ON = [sbt(f"ON{i}", [P, G, HD]) for i in range(2)]
            OTH = sbt("OTH", [P, KC, 2, T], F32R)
            OTL = sbt("OTL", [P, KC, 2, T], F32R)
            mx = sbt("mx", [P, 8])
            nb = sbt("nb", [P, 8])
            rs = sbt("rs", [P, 8])
            rinv = sbt("rinv", [P, 8])
            W2 = [sbt(f"W2{i}", [P, KC * D]) for i in range(2)]
            W2H = [sbt(f"W2H{i}", [P, KC * D], F32R) for i in range(2)]
            W2L = [sbt(f"W2L{i}", [P, KC * D], F32R) for i in range(2)]
            XB1 = sbt("XB1", [P, D])
            XB2 = sbt("XB2", [P, D])
            XB3 = sbt("XB3", [P, D])
            XO = sbt("XO", [P, D])
            XT2 = sbt("XT2", [P, KC, 2, 2, T], F32R)
            XTH3 = sbt("XTH3", [P, KC, P], F32R)
            XTL3 = sbt("XTL3", [P, KC, P], F32R)
            OHS = sbt("OHS", [2 * 32, 2, P], F32R)
            XAM = sbt("XAM", [P, 2, T])
            XAH = sbt("XAH", [P, P], F32R)
            XAL = sbt("XAL", [P, P], F32R)

            s_reg = [sem(f"gather_args{i}") for i in range(4)]
            s_old = [sem(f"kv_old{i}") for i in range(4)]
            s_new = [sem(f"kv_new{i}") for i in range(4)]
            s_qin = [sem(f"qt_in{i}") for i in range(2)]
            s_x1in = sem("x1_in")
            s_w2in = [sem(f"w2_in{i}") for i in range(2)]
            s_w2h = [sem(f"w2_high{i}") for i in range(2)]
            s_w2l = [sem(f"w2_split{i}") for i in range(2)]
            s_ost = sem("out_stored")
            s_ktp = sem("keys_turned")
            s_kt = sem("kt_ready")
            s_s = sem("scores_done")
            s_mx = sem("max_ready")
            s_m = sem("masked_ready")
            s_e = sem("probs_ready")
            s_ptp = sem("probs_turned")
            s_pt = sem("pt_ready")
            s_pv = sem("pv_done")
            s_rinv = sem("sums_inverted")
            s_on = sem("heads_ready")
            s_otp = sem("heads_turned")
            s_oth = sem("ot_high")
            s_ot = sem("ot_ready")
            s_o = sem("o_done")
            s_x2 = sem("x2_ready")
            s_x2p = sem("x2_turned")
            s_xt2h = sem("x2t_high")
            s_xt2 = sem("x2t_ready")
            s_ohz = sem("onehot_cleared")
            s_oh = sem("onehot_ready")
            s_l2 = sem("l2_done")
            s_x3a = sem("x3_half")
            s_x3 = sem("x3_ready")
            s_x3p = sem("x3_turned")
            s_xt3h = sem("x3t_high")
            s_xt3 = sem("x3t_ready")
            s_xa = sem("xa_done")
            s_xam = sem("xa_masked")
            s_xah = sem("xa_high")
            s_xal = sem("xa_split")
            s_l3 = sem("l3_done")
            s_xo = sem("out_ready")
            L2BANK = (bank[7], bank[6])

            block = pb.enter_context(nc.Block())

            def bodies(eng, body):
                for n in range(4):
                    body(Pair(n // 2, n % 2), True, n >= 1, n >= 2)
                with eng.Fori(2, PAIRS // 2 - 1) as i:
                    body(Pair(i, 0), True, True, True)
                    body(Pair(i, 1), True, True, True)
                for n in range(PAIRS - 2, PAIRS + 2):
                    body(Pair(n // 2, n % 2), n < PAIRS, n <= PAIRS, True)

            def last_pair(pr):
                return isinstance(pr.n, int) and pr.n == PAIRS - 1

            @block.gpsimd
            def _(pool):
                def body(pr, attention, dense, adapted):
                    if not attention:
                        return
                    p = pr.n

                    def used(b):
                        return 8 * (p - 2) + 4 * (b + 1)

                    def held(b):
                        k, n = 2 * pr.par + b, p * 2 + b
                        wait_all(pool, s_pass_pool, (s_new[k], 16 * NCH * pr.i))
                        nc.gpsimd.tensor_copy(idxs[k][:, :], idxT[:, :, bass.ds(n, 1)].rearrange("p a o -> p (a o)")
                                              ).then_inc(s_reg[k], 1)
                        wait_all(pool, s_pass_pool, (s_pv, used(b)), (s_reg[k], at(pr.i, 2, 0)))
                        for c in range(NCH):
                            pool.indirect_dma_start(
                                out=KV[k][:, c, :], out_offset=None, in_=t["pool"],
                                in_offset=bass.IndirectOffsetOnAxis(ap=idxs[k][:, c:c + 1], axis=0),
                                bounds_check=NPOOL * BLOCK - 1, oob_is_err=False).then_inc(s_old[k], 16)

                    def fresh(b):
                        k, n = 2 * pr.par + b, p * 2 + b
                        m0 = pool.value_load(moff[0:1, bass.ds(n, 1)], min_val=0, max_val=A_MAX)
                        wait_all(pool, s_pass_pool, (s_mx, used(b)))
                        nc.gpsimd.tensor_copy(FM[k][:, :], mask[:, bass.ds(m0, SPAN)]).then_inc(s_reg[k], 1)
                        wait_all(pool, s_pass_pool, (s_old[k], at(pr.i, 16 * NCH, 16 * NCH - 1)))
                        for c in range(NCH):
                            pool.indirect_dma_start(
                                out=KV[k][:, c, :], out_offset=None, in_=kv_d,
                                in_offset=bass.IndirectOffsetOnAxis(ap=idxs[k][:, NCH + c:NCH + c + 1], axis=0),
                                bounds_check=NB * T - 1, oob_is_err=False).then_inc(s_new[k], 16)

                    if isinstance(p, int) and p == 0:
                        held(0)
                        held(1)
                        fresh(0)
                        fresh(1)
                    else:
                        for b in range(2):
                            held(b)
                            fresh(b)

                bodies(pool, body)

            @block.sync
            def _(sp):
                def queries(pr):
                    wait(sp, s_s, 8 * (pr.n - 1))
                    sp.dma_start(QB[pr.par][:, :, :, :].rearrange("p b c t -> p (b c t)"),
                                 qt_d[bass.ds(pr.n, 1)]).then_inc(s_qin[pr.par], 16)

                def store(q):
                    sp.wait_ge(s_xo, at(q, 1, 0))
                    sp.dma_start(out_v[bass.ds(q, 1)], XO[:, :]).then_inc(s_ost, 16)

                queries(Pair(0, 0))

                def body(pr, attention, dense, adapted):
                    p = pr.n

                    def weights(b):
                        e = sp.value_load(eid[0:1, bass.ds(p * 2 + b, 1)], min_val=0, max_val=E - 1)
                        wait(sp, s_w2l[b], KC * p)
                        sp.dma_start(W2[b][:, :], w2_v[bass.ds(e, 1)]).then_inc(s_w2in[b], 16)

                    if isinstance(p, int) and p == 0:
                        sp.wait_ge(s_new[1], 16 * NCH)
                    if attention:
                        weights(0)
                    if adapted:
                        store(p - 2)
                    if not attention:
                        return
                    wait(sp, s_x2, p)
                    sp.dma_start(XB1[:, :], x1_d[bass.ds(p, 1)]).then_inc(s_x1in, 16)
                    if not last_pair(pr):
                        queries(pr.move(1))
                    weights(1)

                bodies(sp, body)
                sp.wait_ge(s_ost, 16 * PAIRS)

            @block.scalar
            def _(act):
                def copy(dst, src):
                    return nc.scalar.activation(dst, src, ACT.Copy)

                def keys(pr, b, gp):
                    act.wait_ge(s_ktp, at(pr.n, 4, 2 * b + gp))
                    copy(KT[b][:, gp, :], bank[4][:, 0:SPAN]).then_inc(s_kt, 1)

                def exp(p, u):
                    act.wait_ge(s_m, at(p, 8, u))
                    wait(act, s_ptp, p * 8 + u - 1)
                    nc.scalar.activation(PR[u % 2][:, :], SM[u % 2][:, :], ACT.Exp, bias=nb[:, u:u + 1],
                                         scale=SCALE, accum_out=rs[:, u:u + 1]).then_inc(s_e, 1)

                def probs(p, u):
                    act.wait_ge(s_ptp, at(p, 8, u))
                    wait(act, s_pv, p * 8 + u - 1)
                    copy(PT[u % 2][:, :, :].rearrange("p c t -> p (c t)"),
                         bank[2 + u % 2][0:CH, 0:NCH * P]).then_inc(s_pt, 1)

                def heads(p, b):
                    act.wait_ge(s_otp, at(p, 2, b))
                    copy(OTH[:, :, b, :], bank[4][:, 0:256].rearrange("p (c t) -> p c t", c=KC)).then_inc(s_oth, 1)

                def high(q, b, k):
                    if k == 0:
                        act.wait_ge(s_w2in[b], at(q, 16, 15))
                        wait(act, s_l2, 2 * q - 1 + b)
                    part = slice(k * D, (k + 1) * D)
                    copy(W2H[b][:, part], W2[b][:, part]).then_inc(s_w2h[b], 1)

                def body(pr, attention, dense, adapted):
                    p, q, r = pr.n, pr.n - 1, pr.n - 2
                    if attention:
                        exp(p, 0)
                    if dense:
                        probs(q, 7)
                    if adapted:
                        act.wait_ge(s_x3p, at(r, 1, 0))
                        copy(XTH3[:, :, :].rearrange("p k t -> p (k t)"), bank[7][:, :]).then_inc(s_xt3h, 1)
                    if attention:
                        exp(p, 1)
                        probs(p, 0)
                        keys(pr, 1, 0)
                        exp(p, 2)
                        probs(p, 1)
                    if dense:
                        heads(q, 1)
                        high(q, 1, 0)
                    if attention:
                        exp(p, 3)
                        probs(p, 2)
                    if dense:
                        high(q, 1, 1)
                        high(q, 1, 2)
                    if attention:
                        keys(pr, 1, 1)
                        exp(p, 4)
                        probs(p, 3)
                    if dense:
                        act.wait_ge(s_x2p, at(q, 1, 0))
                        copy(XT2[:, :, :, 0, :], bank[7][:, :].rearrange("p (k b t) -> p k b t", b=2, t=T)
                             ).then_inc(s_xt2h, 1)
                    if attention:
                        exp(p, 5)
                        probs(p, 4)
                    if dense:
                        high(q, 1, 3)
                    if attention:
                        if not last_pair(pr):
                            keys(pr.move(1), 0, 0)
                        exp(p, 6)
                        probs(p, 5)
                        heads(p, 0)
                        for k in range(KC):
                            high(p, 0, k)
                        exp(p, 7)
                        probs(p, 6)
                        if not last_pair(pr):
                            keys(pr.move(1), 0, 1)

                keys(Pair(0, 0), 0, 0)
                keys(Pair(0, 0), 0, 1)
                bodies(act, body)

            @block.vector
            def _(dve):
                v = nc.vector
                v.memset(OHS[:, :, :].bitcast(F32), 0.0).then_inc(s_ohz, 1)
                dve.wait_ge(s_ohz, 1)

                def low(dst, exact, high):
                    return v.tensor_tensor(dst, exact, high.bitcast(F32), ALU.subtract)

                def masked(pr, u):
                    p, k = pr.n, 2 * pr.par + u // 4
                    wait_all(dve, s_pass_dve, (s_reg[k], at(pr.i, 2, 1)), (s_e, p * 8 + u - 1), (s_s, at(p, 8, u)))
                    v.tensor_tensor_reduce(out=SM[u % 2][:, :], in0=bank[u % 2][:, 0:SPAN], in1=FM[k][:, :],
                                           scale=1.0, scalar=-3e38, op0=ALU.add, op1=ALU.max,
                                           accum_out=mx[:, u:u + 1]).then_inc(s_mx, 1)
                    dve.wait_ge(s_mx, at(p, 8, u))
                    v.tensor_scalar(nb[:, u:u + 1], mx[:, u:u + 1], -SCALE, None, ALU.mult).then_inc(s_m, 1)

                def norm(p, b):
                    dve.wait_ge(s_e, at(p, 8, 4 * b + 3))
                    v.reciprocal(rinv[:, 4 * b:4 * b + 4], rs[:, 4 * b:4 * b + 4]).then_inc(s_rinv, 1)
                    dve.wait_ge(s_pv, at(p, 8, 4 * b + 3))
                    dve.wait_ge(s_rinv, at(p, 2, b))
                    v.tensor_tensor(ON[b][:, :, :], bank[5][:, 0:256].rearrange("p (g d) -> p g d", g=G),
                                    rinv[:, 4 * b:4 * b + 4].unsqueeze(2).to_broadcast([P, G, HD]),
                                    ALU.mult).then_inc(s_on, 1)

                def heads(p, b):
                    dve.wait_ge(s_oth, at(p, 2, b))
                    low(OTL[:, :, b, :], bank[4][:, 0:256].rearrange("p (c t) -> p c t", c=KC),
                        OTH[:, :, b, :]).then_inc(s_ot, 1)

                def lowest(q, b, k):
                    dve.wait_ge(s_w2h[b], at(q, KC, k))
                    part = slice(k * D, (k + 1) * D)
                    low(W2L[b][:, part], W2[b][:, part], W2H[b][:, part]).then_inc(s_w2l[b], 1)

                def x3(q, b):
                    rows = slice(b * T, (b + 1) * T)
                    dve.wait_ge(s_l2, at(q, 2, b))
                    v.tensor_tensor(XB3[rows, :], L2BANK[b][0:T, :], XB2[rows, :], ALU.add).then_inc(s_x3a, 1)
                    dve.wait_ge(s_x3a, at(q, 2, b))
                    v.tensor_tensor(XB3[rows, :], L2BANK[b][T:P, :], XB3[rows, :], ALU.add).then_inc(s_x3, 1)

                def body(pr, attention, dense, adapted):
                    p, q, r = pr.n, pr.n - 1, pr.n - 2
                    if attention:
                        masked(pr, 0)
                    if adapted:
                        dve.wait_ge(s_xt3h, at(r, 1, 0))
                        low(XTL3[:, :, :].rearrange("p k t -> p (k t)"), bank[7][:, :],
                            XTH3[:, :, :].rearrange("p k t -> p (k t)")).then_inc(s_xt3, 1)
                    if attention:
                        masked(pr, 1)
                    if dense:
                        norm(q, 1)
                        for k in range(KC):
                            lowest(q, 0, k)
                    if attention:
                        masked(pr, 2)
                    if adapted:
                        dve.wait_ge(s_xa, at(r, 1, 0))
                        v.tensor_tensor(XAM[:, :, :], bank[7][:, 0:P].rearrange("p (b t) -> p b t", b=2),
                                        adapt[:, bass.ds(r * 2, 2)].unsqueeze(2).to_broadcast([P, 2, T]),
                                        ALU.mult).then_inc(s_xam, 1)
                        xam = XAM[:, :, :].rearrange("p b t -> p (b t)")
                        dve.wait_ge(s_xam, at(r, 1, 0))
                        v.tensor_copy(XAH[:, :], xam).then_inc(s_xah, 1)
                        dve.wait_ge(s_xah, at(r, 1, 0))
                        low(XAL[:, :], xam, XAH[:, :]).then_inc(s_xal, 1)
                    if dense:
                        heads(q, 1)
                    if adapted:
                        dve.wait_ge(s_l3, at(r, 1, 0))
                        dve.wait_ge(s_x3, at(r, 2, 1))
                        wait(dve, s_ost, 16 * r)
                        v.tensor_tensor(XO[:, :], bank[6][:, :], XB3[:, :], ALU.add).then_inc(s_xo, 1)
                    if attention:
                        masked(pr, 3)
                    if dense:
                        lowest(q, 1, 0)
                        for rows, cols in ((slice(0, 32), slice(0, T)), (slice(32, 64), slice(T, P))):
                            wait_all(dve, s_pass_dve, (s_l2, 2 * q))
                            v.tensor_copy(OHS[rows, :, cols],
                                          onehot[rows, bass.ds(q * 2, 2)].unsqueeze(2).to_broadcast([32, 2, T])
                                          ).then_inc(s_oh, 1)
                        lowest(q, 1, 1)
                        lowest(q, 1, 2)
                        dve.wait_ge(s_o, at(q, 1, 0))
                        dve.wait_ge(s_x1in, at(q, 16, 15))
                        v.tensor_tensor(XB2[:, :], bank[6][:, :], XB1[:, :], ALU.add).then_inc(s_x2, 1)
                    if attention:
                        masked(pr, 4)
                    if dense:
                        dve.wait_ge(s_xt2h, at(q, 1, 0))
                        low(XT2[:, :, :, 1, :], bank[7][:, :].rearrange("p (k b t) -> p k b t", b=2, t=T),
                            XT2[:, :, :, 0, :]).then_inc(s_xt2, 1)
                    if attention:
                        masked(pr, 5)
                    if attention:
                        norm(p, 0)
                    if dense:
                        lowest(q, 1, 3)
                    if attention:
                        masked(pr, 6)
                    if dense:
                        dve.wait_ge(s_x2, at(q, 1, 0))
                        x3(q, 0)
                    if attention:
                        heads(p, 0)
                        masked(pr, 7)
                    if dense:
                        x3(q, 1)

                bodies(dve, body)

            @block.tensor
            def _(pe):
                mm = nc.tensor.matmul
                wo_h, wo_l, w3_h, w3_l = late(wlh, "wo"), late(wll, "wo"), late(wlh, "w3"), late(wll, "w3")
                a_h, a_l, b_h, b_l = late(wlh, "a"), late(wll, "a"), late(wlh, "b"), late(wll, "b")

                def turn_x(tile, s_done):
                    for k in range(KC):
                        last = nc.tensor.transpose(bank[7][:, k * P:(k + 1) * P], tile[:, k * P:(k + 1) * P],
                                                   ident[:, :])
                    last.then_inc(s_done, 1)

                def keys(pr, b, gp):
                    k = 2 * pr.par + b
                    if gp == 0:
                        pe.wait_ge(s_new[k], at(pr.i, 16 * NCH, 16 * NCH - 1))
                    for c in range(NCH):
                        last = nc.tensor.transpose(bank[4][:, c * CH:(c + 1) * CH],
                                                   KV[k][:, c, gp * P:(gp + 1) * P], ident[0:CH, 0:CH])
                    last.then_inc(s_ktp, 1)

                def scores(pr, u):
                    p, b, g = pr.n, u // 4, u % 4
                    gp, g2 = g // 2, g % 2
                    rows = slice(g2 * HD, (g2 + 1) * HD)
                    if u == 0:
                        pe.wait_ge(s_qin[pr.par], at(pr.i, 16, 15))
                    if g2 == 0:
                        pe.wait_ge(s_kt, at(p, 4, 2 * b + gp))
                    wait(pe, s_mx, p * 8 + u - 1)
                    mm(bank[u % 2][:, 0:SPAN],
                       QB[pr.par][rows, b, 2 * gp:2 * gp + 2, :].rearrange("p c t -> p (c t)"),
                       KT[b][rows, gp, :], start=True, stop=True).then_inc(s_s, 1)

                def turn(p, u):
                    pe.wait_ge(s_e, at(p, 8, u))
                    wait(pe, s_pt, p * 8 + u - 1)
                    for c in range(NCH):
                        last = nc.tensor.transpose(bank[2 + u % 2][0:CH, c * P:(c + 1) * P],
                                                   PR[u % 2][:, c * CH:(c + 1) * CH], ident[:, :])
                    last.then_inc(s_ptp, 1)

                def values(pr, u):
                    p, b, g = pr.n, u // 4, u % 4
                    pe.wait_ge(s_pt, at(p, 8, u))
                    if g == 0:
                        wait(pe, s_on, 2 * p + b)
                    for c in range(NCH):
                        last = mm(bank[5][:, g * HD:(g + 1) * HD], PT[u % 2][:, c, :],
                                  KV[2 * pr.par + b][:, c, (G + g) * HD:(G + g + 1) * HD],
                                  start=(c == 0), stop=(c == NCH - 1))
                    last.then_inc(s_pv, 1)

                def heads(p, b):
                    pe.wait_ge(s_on, at(p, 2, b))
                    for gp in range(GP):
                        last = nc.tensor.transpose(bank[4][:, gp * P:(gp + 1) * P],
                                                   ON[b][:, 2 * gp:2 * gp + 2, :].rearrange("p g d -> p (g d)"),
                                                   ident[:, :])
                    last.then_inc(s_otp, 1)

                def output(q):
                    pe.wait_ge(s_ot, at(q, 2, 1))
                    wait(pe, s_xo, q)
                    tok = [x[:, :, :, :].rearrange("p c b t -> p c (b t)") for x in (OTH, OTL)]
                    exact_products(mm, bank[6][:, :], [(tok[0][:, c, :], tok[1][:, c, :], wo_h[:, c, :], wo_l[:, c, :])
                                                       for c in range(KC)], True, True).then_inc(s_o, 1)

                def bias(q, b):
                    mm(L2BANK[b][:, :], OHS[:, b, :], bparts[:, :], start=True, stop=False)

                def expert(q, b):
                    if b == 0:
                        pe.wait_ge(s_oh, at(q, 2, 1))
                        bias(q, 1)
                        pe.wait_ge(s_xt2, at(q, 1, 0))
                        bias(q, 0)
                    for k in range(KC):
                        pe.wait_ge(s_w2l[b], at(q, KC, k))
                        for i, w in enumerate((W2H[b], W2L[b])):
                            last = mm(L2BANK[b][:, :], XT2[:, k, b, :, :].rearrange("p h t -> p (h t)"),
                                      w[:, k * D:(k + 1) * D], start=False, stop=(k == KC - 1 and i == 1))
                    last.then_inc(s_l2, 1)

                x3t = [(XTH3[:, k, :], XTL3[:, k, :]) for k in range(KC)]

                def dense3(a, b, start):
                    exact_products(mm, bank[6][:, :], [(*x3t[k], w3_h[:, k, :], w3_l[:, k, :]) for k in range(a, b)],
                                   start, False)

                def body(pr, attention, dense, adapted):
                    p, q, r = pr.n, pr.n - 1, pr.n - 2
                    before, more = pr.move(-1), attention and not last_pair(pr)

                    if attention:
                        scores(pr, 0)
                    if dense:
                        turn(q, 7)
                        values(before, 6)
                    if adapted:
                        pe.wait_ge(s_x3, at(r, 2, 1))
                        turn_x(XB3, s_x3p)
                    if attention:
                        scores(pr, 1)
                        turn(p, 0)
                    if dense:
                        values(before, 7)
                    if attention:
                        pe.wait_ge(s_kt, at(p, 4, 1))
                        keys(pr, 1, 0)
                    if adapted:
                        pe.wait_ge(s_xt3, at(r, 1, 0))
                        exact_products(mm, bank[7][:, 0:P], [(a_h[:, k, :], a_l[:, k, :], *x3t[k]) for k in range(KC)],
                                       True, True).then_inc(s_xa, 1)
                        dense3(0, 2, True)
                    if attention:
                        scores(pr, 2)
                        turn(p, 1)
                        values(pr, 0)
                    if dense:
                        pe.wait_ge(s_kt, at(p, 4, 2)) if attention else pe.wait_ge(s_ot, at(q, 2, 0))
                        heads(q, 1)
                    if adapted:
                        dense3(2, KC, False)
                        pe.wait_ge(s_xal, at(r, 1, 0))
                        exact_products(mm, bank[6][:, :], [(XAH[:, :], XAL[:, :], b_h[:, 0, :], b_l[:, 0, :])],
                                       False, True).then_inc(s_l3, 1)
                    if attention:
                        scores(pr, 3)
                        turn(p, 2)
                        values(pr, 1)
                    if dense:
                        output(q)
                    if attention:
                        pe.wait_ge(s_ot, at(q, 2, 1)) if dense else pe.wait_ge(s_kt, at(p, 4, 2))
                        keys(pr, 1, 1)
                        scores(pr, 4)
                        turn(p, 3)
                        values(pr, 2)
                    if dense:
                        pe.wait_ge(s_x2, at(q, 1, 0))
                        if adapted:
                            pe.wait_ge(s_xam, at(r, 1, 0))
                        turn_x(XB2, s_x2p)
                    if attention:
                        scores(pr, 5)
                        turn(p, 4)
                        values(pr, 3)
                    if more:
                        pe.wait_ge(s_kt, at(p, 4, 3))
                        keys(pr.move(1), 0, 0)
                    if dense:
                        expert(q, 0)
                    if attention:
                        scores(pr, 6)
                        turn(p, 5)
                        values(pr, 4)
                        pe.wait_ge(s_kt, at(p + 1, 4, 0)) if more else pe.wait_ge(s_kt, at(p, 4, 3))
                        heads(p, 0)
                    if dense:
                        expert(q, 1)
                    if attention:
                        scores(pr, 7)
                        turn(p, 6)
                        values(pr, 5)
                    if more:
                        pe.wait_ge(s_ot, at(p, 2, 0))
                        keys(pr.move(1), 0, 1)

                keys(Pair(0, 0), 0, 0)
                pe.wait_ge(s_kt, 1)
                keys(Pair(0, 0), 0, 1)
                bodies(pe, body)


def kernel(**inputs):
    import numpy as np
    import concourse.bacc as bacc
    from concourse.bass_utils import run_bass_kernel_spmd

    a = {k: np.asarray(v) for k, v in inputs.items()}
    cond, tab, kv = a["itok_B_1_198"], a["itok_Bx257_0_4111"], a["itok_B_37_3939"]
    ident, adapter = a["itok_B_0_15"], a["itok_B_0_6"]
    order = [4 * gp + 2 * g2 + j for gp in range(GP) for j in range(2) for g2 in range(2)]
    wq = a["L1_cond_Wq"].reshape(H, HD, D)[order].reshape(H * HD, D)
    wo = a["L1_cond_Wo"].reshape(D, H, HD)[:, order].reshape(D, H * HD)

    def rows(pool):
        return pool.transpose(0, 2, 1, 3).reshape(NPOOL * BLOCK, G * HD)

    half = HD // 2
    arrays = {
        "x": a["x"].reshape(NB * T, D),
        "w0": a["L0_cond_weights"].reshape(S0 * T, T),
        "cond": cond,
        "kv2": kv.reshape(PAIRS, 2).T,
        "kv": kv,
        "tab": tab,
        "id": ident,
        "ad": adapter,
        "scal": np.repeat(a["L3_cond_scalings"], RANK).reshape(P, 1),
        "inv": (np.float32(1.0) / np.float32(10000.0) ** (np.arange(half, dtype=np.float32) / np.float32(half))),
        "qs": a["L1_cond_q_norm_scale"],
        "ks": a["L1_cond_k_norm_scale"],
        "wqkv": np.concatenate([wq, a["L1_cond_Wk"], a["L1_cond_Wv"]]).T,
        "woT": wo.T,
        "pool": np.concatenate([rows(a["L1_cond_k_blocks"]), rows(a["L1_cond_v_blocks"])], axis=1),
        "w2": a["L2_cond_W"].reshape(E, KC, P, D).transpose(0, 2, 1, 3).reshape(E * P, KC * D),
        "b2": a["L2_cond_b"],
        "w3T": a["L3_cond_W"].T,
        "aT": a["L3_cond_A"].reshape(NA * RANK, D).T,
        "bT": a["L3_cond_Bm"].transpose(0, 2, 1).reshape(NA * RANK, D),
    }
    arrays = {k: np.ascontiguousarray(v) for k, v in arrays.items()}
    nc = bacc.Bacc("TRN2", target_bir_lowering=False, num_devices=1)
    t = {k: nc.dram_tensor(f"in_{k}", v.shape, mybir.dt.from_np(v.dtype), kind="ExternalInput").ap()
         for k, v in arrays.items()}
    out = nc.dram_tensor("out_dram", (NB * T, D), F32, kind="ExternalOutput").ap()
    build(nc, t, out)
    r = run_bass_kernel_spmd(nc, [{f"in_{k}": v for k, v in arrays.items()}], core_ids=[0])
    return r.results[0]["out_dram"].reshape(NB, T, D)
```
